# Optimizing a Trainium2 kernel written in Bass

```python
import numpy as np
import jax
import jax.numpy as jnp

def _softmax(x, axis=-1):
    return jax.nn.softmax(x, axis=axis)

def _gelu(x):
    return jax.nn.gelu(x, approximate=True)

def _silu(x):
    return jax.nn.silu(x)

def _sigmoid(x):
    return jax.nn.sigmoid(x)

def _layernorm(x, axis=-1, eps=1e-05):
    m = jnp.mean(x, axis=axis, keepdims=True)
    v = jnp.var(x, axis=axis, keepdims=True)
    return (x - m) / jnp.sqrt(v + eps)

def _scatter_add(tgt, idx, src, axis=0):
    return tgt.at[idx].add(src)

def _segment_sum(src, seg, n):
    return jax.ops.segment_sum(src, seg, n)
kernel_name = 'mk_seq_postln_d4_jaxref_r8_6464d3'

def setup_inputs(seed: int=0):
    np.random.seed(seed)
    _w = jnp.asarray

    def _L0_attn_setup():
        import jax, jax.numpy as jnp
        import numpy as np
        import math
        D_MODEL = 256
        NUM_HEAD = 16
        HEAD_DIM = D_MODEL // NUM_HEAD

        def _trunc_normal(key, shape, std):
            return jax.random.truncated_normal(key, -3.0, 3.0, shape, dtype=jnp.float32) * std
        key = jax.random.key(seed)
        kx, kp, ko = jax.random.split(key, 3)
        b, s = (4, 256)
        x = jax.random.normal(kx, (b, s, D_MODEL), dtype=jnp.float32)
        sigma_p = math.sqrt(2.0 / (D_MODEL + 3 * D_MODEL))
        w_project = _trunc_normal(kp, (3 * D_MODEL, D_MODEL), sigma_p)
        sigma_o = math.sqrt(2.0 / (D_MODEL + D_MODEL))
        w_out = _trunc_normal(ko, (D_MODEL, D_MODEL), sigma_o)
        return {'x': x, 'w_project': w_project, 'w_out': w_out}
    _L0_attn_in = _L0_attn_setup()

    def _L0_ffn_setup():
        import jax, jax.numpy as jnp
        import numpy as np
        HIDDEN = 256
        INTER = 1024
        B, S = (4, 128)

        def _qmatmul(x, w_int8, scale):
            y = jnp.einsum('bsh,ho->bso', x, w_int8.astype(x.dtype))
            return y * scale
        key = jax.random.key(seed)
        ks = jax.random.split(key, 7)
        x = jax.random.normal(ks[0], (B, S, HIDDEN), dtype=jnp.float32)
        w_gate = jax.random.randint(ks[1], (HIDDEN, INTER), -128, 128, dtype=jnp.int32).astype(jnp.int8)
        w_up = jax.random.randint(ks[2], (HIDDEN, INTER), -128, 128, dtype=jnp.int32).astype(jnp.int8)
        w_down = jax.random.randint(ks[3], (INTER, HIDDEN), -128, 128, dtype=jnp.int32).astype(jnp.int8)
        s_gate = jax.random.uniform(ks[4], (INTER,), dtype=jnp.float32) * 0.02 + 0.001
        s_up = jax.random.uniform(ks[5], (INTER,), dtype=jnp.float32) * 0.02 + 0.001
        s_down = jax.random.uniform(ks[6], (HIDDEN,), dtype=jnp.float32) * 0.02 + 0.001
        return {'x': x, 'w_gate': w_gate, 'w_up': w_up, 'w_down': w_down, 's_gate': s_gate, 's_up': s_up, 's_down': s_down}
    _L0_ffn_in = _L0_ffn_setup()

    def _L1_attn_setup():
        import jax, jax.numpy as jnp
        import numpy as np
        import math
        D_MODEL = 256
        N_HEADS = 16
        N_KV = 4
        HEAD_DIM = D_MODEL // N_HEADS
        SUB = HEAD_DIM // 2
        WINDOW = 64
        THETA = 10000.0
        B, S = (1, 256)

        def rotate_half(x):
            x1, x2 = (x[..., :x.shape[-1] // 2], x[..., x.shape[-1] // 2:])
            return jnp.concatenate([-x2, x1], axis=-1)
        key = jax.random.key(seed)
        ks = jax.random.split(key, 6)
        std = 0.02
        x = jax.random.normal(ks[0], (B, S, D_MODEL), dtype=jnp.float32)
        Wq = jax.random.normal(ks[1], (D_MODEL, N_HEADS * HEAD_DIM), dtype=jnp.float32) * std
        Wk = jax.random.normal(ks[2], (D_MODEL, N_KV * HEAD_DIM), dtype=jnp.float32) * std
        Wv = jax.random.normal(ks[3], (D_MODEL, N_KV * HEAD_DIM), dtype=jnp.float32) * std
        Wo = jax.random.normal(ks[4], (N_HEADS * HEAD_DIM, D_MODEL), dtype=jnp.float32) * std
        lam = jnp.full((N_HEADS,), 0.1, dtype=jnp.float32)
        return {'x': x, 'Wq': Wq, 'Wk': Wk, 'Wv': Wv, 'Wo': Wo, 'lam': lam}
    _L1_attn_in = _L1_attn_setup()

    def _L1_ffn_setup():
        import jax, jax.numpy as jnp
        import numpy as np
        N_EXPERTS = 8
        TOP_K = 2
        N_GROUP = 4
        TOPK_GROUP = 2
        ROUTED_SCALE = 1.0

        def _group_limited_topk(scores):
            T, N = scores.shape
            E = N // N_GROUP
            group_scores = scores.reshape(T, N_GROUP, E).max(axis=-1)
            _, gidx = jax.lax.top_k(group_scores, TOPK_GROUP)
            gmask = jax.nn.one_hot(gidx, N_GROUP, dtype=scores.dtype).sum(1)
            smask = jnp.repeat(gmask, E, axis=1)
            masked = jnp.where(smask > 0, scores, jnp.zeros((), scores.dtype))
            topk_w, topk_i = jax.lax.top_k(masked, TOP_K)
            return (topk_w, topk_i)
        key = jax.random.key(seed)
        ks = jax.random.split(key, 8)
        B, S, H, F, FS, N = (2, 128, 256, 176, 352, N_EXPERTS)
        std = jnp.float32(0.02)
        return {'hidden_states': jax.random.normal(ks[0], (B, S, H), jnp.float32), 'gate_weight': jax.random.normal(ks[1], (N, H), jnp.float32) * std, 'gate_w': jax.random.normal(ks[2], (N, F, H), jnp.float32) * std, 'up_w': jax.random.normal(ks[3], (N, F, H), jnp.float32) * std, 'down_w': jax.random.normal(ks[4], (N, H, F), jnp.float32) * std, 'sh_gate_w': jax.random.normal(ks[5], (FS, H), jnp.float32) * std, 'sh_up_w': jax.random.normal(ks[6], (FS, H), jnp.float32) * std, 'sh_down_w': jax.random.normal(ks[7], (H, FS), jnp.float32) * std}
    _L1_ffn_in = _L1_ffn_setup()

    def _L2_attn_setup():
        import jax, jax.numpy as jnp
        import numpy as np
        HIDDEN = 256
        HEADS = 16
        HEAD_DIM = HIDDEN // HEADS
        NEG = -10000000000.0
        key = jax.random.key(seed)
        k1, k2, k3 = jax.random.split(key, 3)
        x = jax.random.normal(k1, (2, 256, HIDDEN), dtype=jnp.float32)
        w_qkv = jax.random.normal(k2, (HIDDEN, 3 * HIDDEN), dtype=jnp.float32) / np.sqrt(HIDDEN)
        w_out = jax.random.normal(k3, (HIDDEN, HIDDEN), dtype=jnp.float32) / np.sqrt(HIDDEN)
        return {'x': x, 'w_qkv': w_qkv, 'w_out': w_out}
    _L2_attn_in = _L2_attn_setup()

    def _L2_ffn_setup():
        import jax, jax.numpy as jnp
        import numpy as np

        def binarize_weight(w):
            alpha = jnp.mean(jnp.abs(w), axis=tuple(range(1, w.ndim)), keepdims=True)
            bw = jnp.where(w >= 0, 1.0, -1.0) * alpha
            return jax.lax.stop_gradient(bw - w) + w
        key = jax.random.key(seed)
        k1, k2, k3 = jax.random.split(key, 3)
        in_features, out_features = (256, 256)
        x = jax.random.normal(k1, (8, 256, in_features), dtype=jnp.float32)
        std = np.sqrt(2.0 / out_features).astype(np.float32)
        weight = jax.random.normal(k2, (out_features, in_features), dtype=jnp.float32) * std
        bias = jax.random.normal(k3, (out_features,), dtype=jnp.float32) * 0.01
        return {'x': x, 'weight': weight, 'bias': bias}
    _L2_ffn_in = _L2_ffn_setup()

    def _L3_attn_setup():
        import jax, jax.numpy as jnp
        import numpy as np
        HEADS = 16
        key = jax.random.key(seed)
        ks = jax.random.split(key, 5)
        B, T, D = (2, 256, 256)
        s = 0.02
        return {'x': jax.random.normal(ks[0], (B, T, D), dtype=jnp.float32), 'Wq': jax.random.normal(ks[1], (D, D), dtype=jnp.float32) * s, 'Wk': jax.random.normal(ks[2], (D, D), dtype=jnp.float32) * s, 'Wv': jax.random.normal(ks[3], (D, D), dtype=jnp.float32) * s, 'Wo': jax.random.normal(ks[4], (D, D), dtype=jnp.float32) * s}
    _L3_attn_in = _L3_attn_setup()

    def _L3_ffn_setup():
        import jax, jax.numpy as jnp
        import numpy as np
        D_MODEL = 256
        D_EXPERT = 1024
        EPS = 1e-08

        def ternary_quant(w):
            scale = jnp.mean(jnp.abs(w)) + EPS
            q = jnp.clip(jnp.round(w / scale), -1.0, 1.0) * scale
            return w + jax.lax.stop_gradient(q - w)
        key = jax.random.key(seed)
        k_x, k_up, k_gate, k_down = jax.random.split(key, 4)
        std_in = 1.0 / np.sqrt(D_MODEL)
        std_exp = 1.0 / np.sqrt(D_EXPERT)
        return {'x': jax.random.normal(k_x, (4, 256, D_MODEL), dtype=jnp.float32), 'W_up': jax.random.normal(k_up, (D_EXPERT, D_MODEL), dtype=jnp.float32) * std_in, 'W_gate': jax.random.normal(k_gate, (D_EXPERT, D_MODEL), dtype=jnp.float32) * std_in, 'W_down': jax.random.normal(k_down, (D_MODEL, D_EXPERT), dtype=jnp.float32) * std_exp}
    _L3_ffn_in = _L3_ffn_setup()
    _d = {'L0_attn_x': _L0_attn_in['x'], 'L0_attn_w_project': _L0_attn_in['w_project'], 'L0_attn_w_out': _L0_attn_in['w_out'], 'L0_ffn_w_gate': _L0_ffn_in['w_gate'], 'L0_ffn_w_up': _L0_ffn_in['w_up'], 'L0_ffn_w_down': _L0_ffn_in['w_down'], 'L0_ffn_s_gate': _L0_ffn_in['s_gate'], 'L0_ffn_s_up': _L0_ffn_in['s_up'], 'L0_ffn_s_down': _L0_ffn_in['s_down'], 'L1_attn_Wq': _L1_attn_in['Wq'], 'L1_attn_Wk': _L1_attn_in['Wk'], 'L1_attn_Wv': _L1_attn_in['Wv'], 'L1_attn_Wo': _L1_attn_in['Wo'], 'L1_attn_lam': _L1_attn_in['lam'], 'L1_ffn_gate_weight': _L1_ffn_in['gate_weight'], 'L1_ffn_gate_w': _L1_ffn_in['gate_w'], 'L1_ffn_up_w': _L1_ffn_in['up_w'], 'L1_ffn_down_w': _L1_ffn_in['down_w'], 'L1_ffn_sh_gate_w': _L1_ffn_in['sh_gate_w'], 'L1_ffn_sh_up_w': _L1_ffn_in['sh_up_w'], 'L1_ffn_sh_down_w': _L1_ffn_in['sh_down_w'], 'L2_attn_w_qkv': _L2_attn_in['w_qkv'], 'L2_attn_w_out': _L2_attn_in['w_out'], 'L2_ffn_weight': _L2_ffn_in['weight'], 'L2_ffn_bias': _L2_ffn_in['bias'], 'L3_attn_Wq': _L3_attn_in['Wq'], 'L3_attn_Wk': _L3_attn_in['Wk'], 'L3_attn_Wv': _L3_attn_in['Wv'], 'L3_attn_Wo': _L3_attn_in['Wo'], 'L3_ffn_W_up': _L3_ffn_in['W_up'], 'L3_ffn_W_gate': _L3_ffn_in['W_gate'], 'L3_ffn_W_down': _L3_ffn_in['W_down']}
    _x0 = _d['L0_attn_x']
    _d['L0_attn_x'] = jax.random.normal(jax.random.fold_in(jax.random.key(seed), 1), (1, 1024, 256), dtype=_x0.dtype)
    del _x0
    return _d

def reference(L0_attn_x, L0_attn_w_project, L0_attn_w_out, L0_ffn_w_gate, L0_ffn_w_up, L0_ffn_w_down, L0_ffn_s_gate, L0_ffn_s_up, L0_ffn_s_down, L1_attn_Wq, L1_attn_Wk, L1_attn_Wv, L1_attn_Wo, L1_attn_lam, L1_ffn_gate_weight, L1_ffn_gate_w, L1_ffn_up_w, L1_ffn_down_w, L1_ffn_sh_gate_w, L1_ffn_sh_up_w, L1_ffn_sh_down_w, L2_attn_w_qkv, L2_attn_w_out, L2_ffn_weight, L2_ffn_bias, L3_attn_Wq, L3_attn_Wk, L3_attn_Wv, L3_attn_Wo, L3_ffn_W_up, L3_ffn_W_gate, L3_ffn_W_down):

    def _L0_attn_ref(x, w_project, w_out):
        import jax, jax.numpy as jnp
        import numpy as np
        import math
        D_MODEL = 256
        NUM_HEAD = 16
        HEAD_DIM = D_MODEL // NUM_HEAD

        def _trunc_normal(key, shape, std):
            return jax.random.truncated_normal(key, -3.0, 3.0, shape, dtype=jnp.float32) * std
        b, s, d = x.shape
        qkv = jnp.einsum('bsd,od->bso', x, w_project)
        qkv = qkv.reshape(b, s, 3, NUM_HEAD, HEAD_DIM)
        qkv = jnp.transpose(qkv, (2, 0, 3, 1, 4))
        q, k, v = (qkv[0], qkv[1], qkv[2])
        att = jnp.einsum('bhqd,bhkd->bhqk', q, k) / math.sqrt(HEAD_DIM)
        causal = jnp.triu(jnp.ones((s, s), dtype=bool), k=1)
        att = jnp.where(causal[None, None, :, :], jnp.float32(-1000000000.0), att)
        att = jax.nn.softmax(att, axis=-1)
        out = jnp.einsum('bhqk,bhkd->bhqd', att, v)
        out = jnp.transpose(out, (0, 2, 1, 3)).reshape(b, s, d)
        return jnp.einsum('bsd,od->bso', out, w_out)

    def _L0_ffn_ref(x, w_gate, w_up, w_down, s_gate, s_up, s_down):
        import jax, jax.numpy as jnp
        import numpy as np
        HIDDEN = 256
        INTER = 1024
        B, S = (4, 128)

        def _qmatmul(x, w_int8, scale):
            y = jnp.einsum('bsh,ho->bso', x, w_int8.astype(x.dtype))
            return y * scale
        gate = jax.nn.silu(_qmatmul(x, w_gate, s_gate))
        up = _qmatmul(x, w_up, s_up)
        fuse = gate * up
        return _qmatmul(fuse, w_down, s_down)

    def _L1_attn_ref(x, Wq, Wk, Wv, Wo, lam):
        import jax, jax.numpy as jnp
        import numpy as np
        import math
        D_MODEL = 256
        N_HEADS = 16
        N_KV = 4
        HEAD_DIM = D_MODEL // N_HEADS
        SUB = HEAD_DIM // 2
        WINDOW = 64
        THETA = 10000.0
        B, S = (1, 256)

        def rotate_half(x):
            x1, x2 = (x[..., :x.shape[-1] // 2], x[..., x.shape[-1] // 2:])
            return jnp.concatenate([-x2, x1], axis=-1)
        b, s, _ = x.shape
        q = (x @ Wq).reshape(b, s, N_HEADS, HEAD_DIM).transpose(0, 2, 1, 3)
        k = (x @ Wk).reshape(b, s, N_KV, HEAD_DIM).transpose(0, 2, 1, 3)
        v = (x @ Wv).reshape(b, s, N_KV, HEAD_DIM).transpose(0, 2, 1, 3)
        inv_freq = 1.0 / THETA ** (jnp.arange(0, HEAD_DIM, 2, dtype=jnp.float32) / HEAD_DIM)
        t = jnp.arange(s, dtype=jnp.float32)
        freqs = t[:, None] * inv_freq[None, :]
        emb = jnp.concatenate([freqs, freqs], axis=-1)
        cos, sin = (jnp.cos(emb), jnp.sin(emb))
        q = q * cos + rotate_half(q) * sin
        k = k * cos + rotate_half(k) * sin
        n_rep = N_HEADS // N_KV
        k = jnp.repeat(k, n_rep, axis=1)
        v = jnp.repeat(v, n_rep, axis=1)
        scale = 1.0 / math.sqrt(SUB)
        q1, q2 = (q[..., :SUB], q[..., SUB:])
        k1, k2 = (k[..., :SUB], k[..., SUB:])
        a1 = jnp.einsum('bhqd,bhkd->bhqk', q1, k1) * scale
        a2 = jnp.einsum('bhqd,bhkd->bhqk', q2, k2) * scale
        row = jnp.arange(s)[:, None]
        col = jnp.arange(s)[None, :]
        allowed = (col <= row) & (col >= row - WINDOW + 1)
        neg = jnp.where(allowed, 0.0, -jnp.inf).astype(a1.dtype)
        a1 = a1 + neg
        a2 = a2 + neg
        p1 = jax.nn.softmax(a1.astype(jnp.float32), axis=-1).astype(x.dtype)
        p2 = jax.nn.softmax(a2.astype(jnp.float32), axis=-1).astype(x.dtype)
        diff = jax.nn.relu(p1 - lam[None, :, None, None] * p2)
        diff = diff / (diff.sum(axis=-1, keepdims=True) + 1e-06)
        out = jnp.einsum('bhqk,bhkd->bhqd', diff, v)
        out = out.transpose(0, 2, 1, 3).reshape(b, s, N_HEADS * HEAD_DIM)
        return out @ Wo

    def _L1_ffn_ref(hidden_states, gate_weight, gate_w, up_w, down_w, sh_gate_w, sh_up_w, sh_down_w):
        import jax, jax.numpy as jnp
        import numpy as np
        N_EXPERTS = 8
        TOP_K = 2
        N_GROUP = 4
        TOPK_GROUP = 2
        ROUTED_SCALE = 1.0

        def _group_limited_topk(scores):
            T, N = scores.shape
            E = N // N_GROUP
            group_scores = scores.reshape(T, N_GROUP, E).max(axis=-1)
            _, gidx = jax.lax.top_k(group_scores, TOPK_GROUP)
            gmask = jax.nn.one_hot(gidx, N_GROUP, dtype=scores.dtype).sum(1)
            smask = jnp.repeat(gmask, E, axis=1)
            masked = jnp.where(smask > 0, scores, jnp.zeros((), scores.dtype))
            topk_w, topk_i = jax.lax.top_k(masked, TOP_K)
            return (topk_w, topk_i)
        B, S, H = hidden_states.shape
        h = hidden_states.reshape(-1, H)
        logits = h.astype(jnp.float32) @ gate_weight.astype(jnp.float32).T
        scores = jax.nn.softmax(logits, axis=-1)
        topk_w, topk_i = _group_limited_topk(scores)
        topk_w = (topk_w * ROUTED_SCALE).astype(h.dtype)
        wmat = (jax.nn.one_hot(topk_i, N_EXPERTS, dtype=topk_w.dtype) * topk_w[..., None]).sum(axis=1)
        g = jnp.einsum('th,nfh->ntf', h, gate_w)
        u = jnp.einsum('th,nfh->ntf', h, up_w)
        e = jnp.einsum('ntf,nhf->nth', jax.nn.silu(g) * u, down_w)
        routed = jnp.einsum('nth,tn->th', e, wmat)
        sg = h @ sh_gate_w.T
        su = h @ sh_up_w.T
        shared = jax.nn.silu(sg) * su @ sh_down_w.T
        return (routed + shared).reshape(B, S, H)

    def _L2_attn_ref(x, w_qkv, w_out):
        import jax, jax.numpy as jnp
        import numpy as np
        HIDDEN = 256
        HEADS = 16
        HEAD_DIM = HIDDEN // HEADS
        NEG = -10000000000.0
        b, s, _ = x.shape
        qkv = x @ w_qkv
        qkv = qkv.reshape(b, s, 3, HEADS, HEAD_DIM)
        q, k, v = (qkv[:, :, 0], qkv[:, :, 1], qkv[:, :, 2])
        scale = jnp.sqrt(jnp.float32(HEAD_DIM)).astype(x.dtype)
        q = q / scale
        scores = jnp.einsum('bqhd,bkhd->bhqk', q, k)
        causal_mask = jnp.arange(s)[:, None] >= jnp.arange(s)[None, :]
        scores = jnp.where(causal_mask[None, None], scores, NEG)
        attn = jax.nn.softmax(scores, axis=-1)
        out = jnp.einsum('bhqk,bkhd->bqhd', attn, v).reshape(b, s, HIDDEN)
        return out @ w_out

    def _L2_ffn_ref(x, weight, bias):
        import jax, jax.numpy as jnp
        import numpy as np

        def binarize_weight(w):
            alpha = jnp.mean(jnp.abs(w), axis=tuple(range(1, w.ndim)), keepdims=True)
            bw = jnp.where(w >= 0, 1.0, -1.0) * alpha
            return jax.lax.stop_gradient(bw - w) + w
        bw = binarize_weight(weight)
        return jnp.einsum('bsi,oi->bso', x, bw) + bias

    def _L3_attn_ref(x, Wq, Wk, Wv, Wo):
        import jax, jax.numpy as jnp
        import numpy as np
        HEADS = 16
        B, T, _ = x.shape
        H = HEADS
        Dh = Wq.shape[1] // H
        q = (x @ Wq).reshape(B, T, H, Dh)
        k = (x @ Wk).reshape(B, T, H, Dh)
        v = (x @ Wv).reshape(B, T, H, Dh)
        scores = jnp.einsum('bthd,bshd->bhts', q, k)
        mask = jnp.tril(jnp.ones((T, T), dtype=scores.dtype))
        scores = scores * mask
        attn = jax.nn.softmax(scores / T ** 0.5, axis=-1)
        out = jnp.einsum('bhts,bshd->bthd', attn, v).reshape(B, T, H * Dh)
        return out @ Wo

    def _L3_ffn_ref(x, W_up, W_gate, W_down):
        import jax, jax.numpy as jnp
        import numpy as np
        D_MODEL = 256
        D_EXPERT = 1024
        EPS = 1e-08

        def ternary_quant(w):
            scale = jnp.mean(jnp.abs(w)) + EPS
            q = jnp.clip(jnp.round(w / scale), -1.0, 1.0) * scale
            return w + jax.lax.stop_gradient(q - w)
        wu = ternary_quant(W_up)
        wg = ternary_quant(W_gate)
        wd = ternary_quant(W_down)
        up = jnp.einsum('bsd,ed->bse', x, wu)
        gate = jnp.einsum('bsd,ed->bse', x, wg)
        hidden = jax.nn.silu(up) * gate
        return jnp.einsum('bse,de->bsd', hidden, wd)
    x = L0_attn_x
    x = _layernorm(x + _L0_attn_ref(x, L0_attn_w_project, L0_attn_w_out), axis=-1)
    x = _layernorm(x + _L0_ffn_ref(x, L0_ffn_w_gate, L0_ffn_w_up, L0_ffn_w_down, L0_ffn_s_gate, L0_ffn_s_up, L0_ffn_s_down), axis=-1)
    x = _layernorm(x + _L1_attn_ref(x, L1_attn_Wq, L1_attn_Wk, L1_attn_Wv, L1_attn_Wo, L1_attn_lam), axis=-1)
    x = _layernorm(x + _L1_ffn_ref(x, L1_ffn_gate_weight, L1_ffn_gate_w, L1_ffn_up_w, L1_ffn_down_w, L1_ffn_sh_gate_w, L1_ffn_sh_up_w, L1_ffn_sh_down_w), axis=-1)
    x = _layernorm(x + _L2_attn_ref(x, L2_attn_w_qkv, L2_attn_w_out), axis=-1)
    x = _layernorm(x + _L2_ffn_ref(x, L2_ffn_weight, L2_ffn_bias), axis=-1)
    x = _layernorm(x + _L3_attn_ref(x, L3_attn_Wq, L3_attn_Wk, L3_attn_Wv, L3_attn_Wo), axis=-1)
    x = _layernorm(x + _L3_ffn_ref(x, L3_ffn_W_up, L3_ffn_W_gate, L3_ffn_W_down), axis=-1)
    return x

_drawn_inputs = setup_inputs


def setup_inputs(seed=0):
    import zlib

    import numpy as np

    out = dict(_drawn_inputs(seed))
    spreads = {'L1_attn_lam': (0.10000000149011612, 0.6)}
    factors = {'L1_attn_Wq': 8.0,
     'L1_attn_Wk': 8.0,
     'L1_attn_Wv': 2.941,
     'L1_attn_Wo': 2.945,
     'L1_ffn_gate_weight': 8.0,
     'L1_ffn_gate_w': 8.0,
     'L1_ffn_up_w': 8.0,
     'L1_ffn_down_w': 8.0,
     'L1_ffn_sh_gate_w': 2.797,
     'L1_ffn_sh_up_w': 2.795,
     'L1_ffn_sh_down_w': 2.787,
     'L2_ffn_bias': 8.0,
     'L3_attn_Wq': 8.0,
     'L3_attn_Wk': 8.0,
     'L3_attn_Wv': 6.55,
     'L3_attn_Wo': 6.382}
    for name, (base, spread) in spreads.items():
        noise = np.random.default_rng([zlib.crc32(name.encode()), seed]).standard_normal(out[name].shape)
        drawn = base * np.exp(spread * noise) if base else spread * noise
        out[name] = jnp.asarray(drawn.astype(out[name].dtype))
    for name, factor in factors.items():
        out[name] = (out[name] * factor).astype(out[name].dtype)
    return out
```

```python
from contextlib import ExitStack

import numpy as np
import concourse.bass as bass
from concourse import mybir

F32 = mybir.dt.float32
BF16 = mybir.dt.bfloat16
I32 = mybir.dt.int32
I8 = mybir.dt.int8
ALU = mybir.AluOpType
ACT = mybir.ActivationFunctionType
AX = mybir.AxisListType

P = 128
S = 1024
D = 256
NT = S // P
ND = D // P
HALF = 512
TH = HALF // P
NH, HD = 16, 16
HG = 4
NG = NH // HG
STRIP = 32
GROUPS = 6
Q_PARTS = (0, 0, 1, 0, 2, 1)
K_PARTS = (0, 1, 0, 2, 0, 1)
KROWS = GROUPS * HD
NEG = -1.0e30
LOWEST = -3.0e38
EPS = 1e-5
ONES_PAIR = float(np.array([0x3F803F80], np.uint32).view(np.float32)[0])
KV = 4
WIN = 64
WK = P + WIN
EXPERTS, F_EXP, F_SH = 8, 176, 352
F_MOE = EXPERTS * F_EXP + F_SH
NF_MOE = -(-F_MOE // P)
F = 1024
NF = F // P
NEXP1 = EXPERTS + 1

C_ID, C_MASK, C_MASKT, C_TRI = 0, 128, 256, 384
C_WMASK, C_WMASK0 = 512, 896
C_LOW8, C_LOW4, C_CNT, C_FLOOR, C_LAM = 1280, 1344, 1360, 1368, 1376
C_SG, C_SU, C_GW = 1392, 1400, 1408
C_ALL = 1424


def constants():
    c = np.zeros((P, C_ALL), np.float32)
    p = np.arange(P)[:, None]
    j = np.arange(P)[None, :]
    c[:, C_ID:C_ID + P] = p == j
    c[:, C_MASK:C_MASK + P] = np.where(j > p, NEG, 0)
    c[:, C_MASKT:C_MASKT + P] = np.where(p > j, NEG, 0)
    c[:, C_TRI:C_TRI + P] = p > j
    w = np.arange(WK)[None, :]
    seen = (w >= p + 1) & (w <= p + WIN)
    for at, ok in ((C_WMASK, seen), (C_WMASK0, seen & (w >= WIN))):
        m = np.where(ok, 0, NEG)
        c[:, at:at + WK] = m
        c[:, at + WK:at + 2 * WK] = m
    for at, n in ((C_LOW8, 8), (C_LOW4, 4)):
        c[:, at:at + n * n] = (np.arange(n)[None, :] < np.arange(n)[:, None]).reshape(1, -1)
    tok = np.arange(NT)[None, :] * P + p
    c[:, C_CNT:C_CNT + NT] = S - 1 - tok
    c[:, C_FLOOR:C_FLOOR + NT] = np.where(tok < S - 1, 0.0, LOWEST)
    return c


def expert_selector():
    f = np.arange(NF_MOE * P)
    owner = np.where(f < EXPERTS * F_EXP, f // F_EXP, EXPERTS)
    one = (owner[None, :] == np.arange(NEXP1)[:, None]) & (f < F_MOE)[None, :]
    return np.tile(one, (3, 1)).astype(np.float32)


def rope_tables():
    inv = (1.0 / 10000.0 ** (np.arange(0, HD, 2, dtype=np.float32) / np.float32(HD))).astype(np.float32)
    f = np.arange(S, dtype=np.float32)[None, :] * np.concatenate([inv, inv])[:, None]
    sign = np.where(np.arange(HD) < HD // 2, -1.0, 1.0)[:, None].astype(np.float32)
    t = np.stack([np.cos(f), np.sin(f) * sign], 1).astype(np.float32)
    return np.ascontiguousarray(np.tile(t, (P // HD, 1, 1)))


ATT, WATT, GLU, MOE, BIN, TERN = range(6)
SUBLAYERS = (ATT, GLU, WATT, MOE, ATT, BIN, ATT, TERN)
LAST_ATT = 6
E_EXP = NG * 12 * 2
E_WATT = NT * NH // 2
E_USES = {ATT: E_EXP + 8, WATT: E_WATT + 8, GLU: 2 * NF + 4, MOE: 2 * NF_MOE + 4, BIN: 4, TERN: 2 * NF + 4}


def e_before(s):
    return sum(E_USES[k] for k in SUBLAYERS[:s])


def max_units(g):
    return [("max", g, t, c, j) for t in range(NT) for c in range(1 + (t >= TH)) for j in range(HG)]


def attention_plan():
    plan = max_units(0) + [("mT", 0)]
    before, due = None, []
    for g in range(NG):
        ahead = max_units(g + 1) if g + 1 < NG else []
        for i, (qh, kb) in enumerate((qh, kb) for qh in range(2) for kb in range(TH * (qh + 1))):
            plan += ahead[5 * i:5 * i + 5]
            if i == 10 and ahead:
                plan.append(("mT", g + 1))
            plan.append(("exp", g, qh, kb))
            due = [(n - 1, what) for n, what in due]
            while due and due[0][0] == 0:
                plan.append(due.pop(0)[1])
            if before:
                plan.append(("pv",) + before)
                if before[2] == TH * (before[1] + 1) - 1:
                    plan.append(("acc",) + before[:2])
                    due.append((2, ("accT",) + before[:2]))
            before = (g, qh, kb)
    plan += [what for _, what in due]
    plan += [("pv",) + before, ("acc",) + before[:2], ("accT",) + before[:2]]
    return plan


def windowed_plan():
    plan = []
    for u in range(NT * NH // 2 + 2):
        if u < NT * NH // 2:
            plan.append(("S", u))
        elif u % 2 == 0:
            plan.append(("flush",))
        gi = (u - 3) // 2
        if u % 2 and gi >= 0:
            if gi >= 1:
                plan.append(("pv", gi - 1))
                if gi % 4 == 0:
                    plan.append(("acc", gi // 4 - 1))
            plan.append(("uT", gi))
            if gi >= 6 and gi % 4 == 2:
                plan.append(("accT", (gi - 6) // 4))
    last = NT * NG - 1
    return plan + [("pv", last), ("acc", NT - 1), ("accT", NT - 1)]


PLAN = attention_plan()
W_PLAN = windowed_plan()
STEP = {(g, qh, kb): g * 12 + TH * qh + kb for g in range(NG) for qh in range(2) for kb in range(TH * (qh + 1))}


def span(qh, kb):
    q0 = max(qh * HALF, kb * P)
    return q0, (qh + 1) * HALF - q0


def build(nc, t_in, out, subs=len(SUBLAYERS)):
    with ExitStack() as ctx:
        def sb(name, shape, dt=F32):
            return ctx.enter_context(nc.sbuf_tensor(name, shape, dt))

        def sem(name):
            return ctx.enter_context(nc.semaphore(name))

        X = sb("X", [P, NT, D])
        xT = sb("xT", [P, ND, S])
        QO = sb("QO", [P, NH * S], BF16)
        KO = sb("KO", [P, NH * S], BF16)
        V = sb("V", [P, NT * NH, STRIP])
        PB = sb("PB", [P, 2 * HG * HALF])
        parts = sb("parts", [P, 2, 3, S], BF16)
        rest = sb("rest", [P, 2, HALF])
        A = sb("A", [P, NT, D])
        acc = sb("acc", [P, 2, HALF])
        WF = sb("WF", [P, 2 * ND * F_MOE])
        WA = [sb(f"WA{i}", [P, ND * 4 * D]) for i in range(2)]
        WB = sb("WB", [P, ND, D])
        biasB = sb("biasB", [P, D])
        sdown = sb("sdown", [P, D])
        cst = sb("cst", [P, C_ALL])
        idb = sb("idb", [P, P], BF16)
        maskb = sb("maskb", [P, 2, P], BF16)
        wmaskb = sb("wmaskb", [P, 2, 2 * WK], BF16)
        ones = sb("ones", [P, P])
        pmx = sb("pmx", [P, 2, 3, NT, HG])
        nm = sb("nm", [P, 2, NT, HG])
        nmr = sb("nmr", [P, NT, HG])
        mp = sb("mp", [P, 2, NT, 3, HG], BF16)
        mrow = sb("mrow", [3 * HG, 2, S], BF16)
        em = sb("em", [P, 2, NT, HG])
        rc = sb("rc", [P, 2, HALF // STRIP])
        stats = sb("stats", [P, NT, 6])
        mv = sb("mv", [P, NT, 2])
        lnv = sb("lnv", [P, 4, TH])
        wm = sb("wm", [P, 6, NT, EXPERTS])
        wmx = sb("wmx", [P, NT, NEXP1])
        wp = sb("wp", [P, NT, 3, NEXP1], BF16)
        tern = sb("tern", [P, 24])
        r12 = sb("r12", [P, NT, NH, 2])
        nm2 = sb("nm2", [P, 2, 4])
        cc = sb("cc", [P, 2, 4])

        q_op = QO[:, :].rearrange("p (h n) -> p h n", h=NH)
        k_op = KO[:, :].rearrange("p (h n) -> p h n", h=NH)
        kw_op = KO[:, 0:KV * 2 * (WIN + S)].rearrange("p (h s n) -> p h s n", h=KV, s=2)
        hid = [t[:, :].bitcast(F32)[:, 0:NF_MOE * HALF].rearrange("p (f n) -> p f n", f=NF_MOE) for t in (QO, KO)]
        v_all = V[:, :, :].rearrange("p (t h) c -> p t h c", t=NT)
        pb = PB[:, :].rearrange("p (b h n) -> p b h n", b=2, h=HG)
        sg = PB[:, 0:4 * HALF].rearrange("p (b n) -> p b n", b=4)
        sgu = PB[:, 4 * HALF:6 * HALF].rearrange("p (b n) -> p b n", b=2)
        raw = PB[:, :].bitcast(I8)
        selF = A[0:3 * NEXP1, :, :].rearrange("p t n -> p (t n)")[:, 0:NF_MOE * P]
        selb = acc[0:3 * NEXP1, :, :].rearrange("p b n -> p (b n)").bitcast(BF16)[:, 0:NF_MOE * P]
        tt = cst[:, C_WMASK:C_WMASK + HALF]
        big = rest[:, 0, 0:D]
        carry = rest[:, 1, 0:D]
        rank = PB[:, 6 * HALF:8 * HALF].rearrange("p (b n) -> p b n", b=2)
        pf = parts[:, :, :, :].rearrange("p b k n -> p (b k n)").bitcast(F32)
        wsuf = pf[:, 0:NT * D].rearrange("p (t n) -> p t n", t=NT)
        ew = pf[:, 0:2 * 4 * WK].rearrange("p (b k n) -> p b k n", b=2, k=4)
        uw = pf[:, 1536:1536 + 2 * 4 * WK].rearrange("p (b k n) -> p b k n", b=2, k=4)
        uT = PB[:, :].rearrange("p (b k n) -> p b k n", b=4, k=2)
        rope = A[:, :, :].rearrange("p t n -> p (t n)").rearrange("p (k n) -> p k n", k=2)
        v_own = V[:, 0:NT * KV, :].rearrange("p (t h) c -> p t h c", t=NT)
        v_prev = V[:, NT * KV:2 * NT * KV, :].rearrange("p (t h) c -> p t h c", t=NT)
        gu = WF[:, 0:2 * ND * F].rearrange("p (c k f) -> p c k f", c=ND, k=2)
        wd = WF[:, 2 * ND * F:2 * ND * F + NF * D].rearrange("p (f n) -> p f n", f=NF)
        gu_moe = WF[:, :].rearrange("p (c k f) -> p c k f", c=ND, k=2)
        wd_moe = V[:, :, :].rearrange("p s c -> p (s c)")[:, 0:NF_MOE * D].rearrange("p (f n) -> p f n", f=NF_MOE)
        wT = parts[:, 1, 0, :]
        idf = cst[:, C_ID:C_ID + P]

        def w_att(s, lo, n):
            w = {0: 0, 2: 1, 4: 0, 6: 1}[s]
            width = 4 * D if s != 2 else 960
            v = WA[w][:, 0:ND * width].rearrange("p (c n) -> p c n", c=ND)
            return v[:, :, lo:lo + n]

        bank = [ctx.enter_context(nc.psum_tensor(f"bank{i}", [P, HALF], F32)) for i in range(3)]
        pair = [ctx.enter_context(nc.psum_tensor(f"pair{i}", [P, 2, HALF], F32)) for i in range(2)]
        pvb = ctx.enter_context(nc.psum_tensor("pvb", [P, HALF], F32))

        r_full, r_free = sem("r_full"), sem("r_free")
        e_full, e_free = sem("e_full"), sem("e_free")
        dve_step = sem("dve_step")
        pool_step = sem("pool_step")
        ld_sel = sem("ld_sel")
        ld_x, ld_glu = sem("ld_x"), sem("ld_glu")
        ld_watt, ld_rope, ld_moe, ld_moed = sem("ld_watt"), sem("ld_rope"), sem("ld_moe"), sem("ld_moed")
        ld_att2, ld_bin, ld_att3, ld_tern = sem("ld_att2"), sem("ld_bin"), sem("ld_att3"), sem("ld_tern")
        cast_ready = sem("cast_ready")
        glu_ready = sem("glu_ready")
        v_blank = sem("v_blank")
        k_ones = sem("k_ones")
        parts_ready = sem("parts_ready")
        scr_written = sem("scr_written")
        rep_a, rep_b = sem("rep_a"), sem("rep_b")
        mp_ready = sem("mp_ready")
        mrow_ready = sem("mrow_ready")
        m_in = [sem("m_in0"), sem("m_in1")]
        pv_done = sem("pv_done")
        acc_ready = sem("acc_ready")
        em_ready = sem("em_ready")
        xn_ready = sem("xn_ready")
        wm_ready = sem("wm_ready")
        logit_max = sem("logit_max")
        logit_exp = sem("logit_exp")
        wmax_ready = sem("wmax_ready")
        u_ready = sem("u_ready")
        bin_ready = sem("bin_ready")
        abs_ready = sem("abs_ready")
        tern_scale = sem("tern_scale")
        tern_ready = sem("tern_ready")
        stored = sem("stored")

        scratch = nc.dram_tensor("scratch", [4 * 4, P, 3, S], BF16, kind="Internal").ap()
        x_out = out.rearrange("b (t p) n -> p (b t) n", p=P)

        ATTS = [s for s in range(subs) if SUBLAYERS[s] == ATT]

        def a_of(s):
            return {0: 0, 4: 1, 6: 2}[s]

        REP = {0: (12, 12), 2: (12 + 36, 12), 4: (60, 24), 6: (72, 36)}
        PARTS0 = {0: 0, 2: 4, 4: 7, 6: 11}
        ACC0 = {0: 0, 2: 8, 4: 16, 6: 24}
        PV0 = {0: 0, 2: 48, 4: 56, 6: 104}

        block = ctx.enter_context(nc.Block())

        @block.sync
        def _(sp):
            def load(dst, src, s):
                sp.dma_start(dst, src).then_inc(s, 16)

            load(xT[:, :, :], t_in["xT"], ld_x)
            load(WA[0][:, :], t_in["w_att0"], ld_x)
            load(cst[:, :], t_in["cst"], ld_x)
            load(X[:, :, :], t_in["x"], ld_x)
            load(raw[:, 0:ND * 2 * F].bitcast(I32), t_in["glu_gu"], ld_glu)
            load(raw[:, ND * 2 * F:ND * 2 * F + NF * D].bitcast(I32), t_in["glu_d"], ld_glu)
            load(sdown[:, :], t_in["glu_sd"].partition_broadcast(P), ld_glu)
            load(WA[1][:, 0:ND * 960], t_in["w_watt"], ld_watt)
            load(WB[:, :, :], t_in["bin_w"], ld_bin)
            load(biasB[:, :], t_in["bin_b"].partition_broadcast(P), ld_bin)

            n_scr = 0

            def replicate(s):
                nonlocal n_scr
                for tile in range(4):
                    n = PARTS0[s] + tile
                    sp.wait_ge(parts_ready, n + 1)
                    sp.dma_start(scratch[n], parts[:, n % 2, :, :]).then_inc(scr_written, 16)
                    sp.wait_ge(scr_written, 16 * (n + 1))
                    side, hi = tile % 2, tile // 2
                    dst = (q_op, k_op)[side]
                    for g in range(GROUPS):
                        part = (Q_PARTS, K_PARTS)[side][g]
                        src = scratch[n].rearrange("(h d) k n -> k d h n", d=HD)[part]
                        sp.dma_start(dst[g * HD:(g + 1) * HD, hi * 8:hi * 8 + 8, :], src)\
                            .then_inc((rep_a, rep_b)[hi], 16)

            def replicate_windowed(s):
                HS = HD // 2
                for tile in range(3):
                    n = PARTS0[s] + tile
                    sp.wait_ge(parts_ready, n + 1)
                    rows = P if tile < 2 else KV * HD
                    sp.dma_start(scratch[n][0:rows], parts[0:rows, n % 2, :, :]).then_inc(scr_written, 16)
                    sp.wait_ge(scr_written, 16 * (n + 1))
                    if tile == 2:
                        sp.wait_ge(k_ones, 2)
                    src = scratch[n][0:rows].rearrange("(h u d) k n -> u k d h n", u=2, d=HS)
                    for u in range(2):
                        for g in range(GROUPS):
                            r0 = u * GROUPS * HS + g * HS
                            if tile < 2:
                                dst = q_op[r0:r0 + HS, tile * 8:tile * 8 + 8, :]
                                part = Q_PARTS[g]
                            else:
                                dst = kw_op[r0:r0 + HS, :, u, WIN:WIN + S]
                                part = K_PARTS[g]
                            sp.dma_start(dst, src[u, part]).then_inc(rep_a, 16)

            def maxima(s):
                a = a_of(s)
                for g in range(NG):
                    n = NG * a + g
                    sp.wait_ge(mrow_ready, n + 1)
                    sp.dma_start(q_op[KROWS:KROWS + 3, g * HG:(g + 1) * HG, :], mrow[:, n % 2, :])\
                        .then_inc(m_in[n % 2], 16)

            for s in range(subs):
                if s == 1:
                    sp.wait_ge(xn_ready, NT)
                    load(rope, t_in["rope"], ld_rope)
                if s == 2:
                    sp.wait_ge(xn_ready, 2 * NT)
                    load(WF[:, :], t_in["moe_gu"], ld_moe)
                    load(WA[0][:, :], t_in["w_att2"], ld_att2)
                if s == 3:
                    sp.wait_ge(xn_ready, 3 * NT)
                    load(selF[:, :], t_in["sel"], ld_sel)
                    load(wd_moe, t_in["moe_d"], ld_moed)
                    load(WA[1][:, :], t_in["w_att3"], ld_att3)
                if s == 4:
                    sp.wait_ge(xn_ready, 4 * NT)
                    load(WF[:, 0:2 * ND * F + NF * D], t_in["tern_w"], ld_tern)
                if SUBLAYERS[s] == ATT:
                    replicate(s)
                    maxima(s)
                if SUBLAYERS[s] == WATT:
                    replicate_windowed(s)
            for half in range(2):
                sp.wait_ge(xn_ready, NT * (subs - 1) + TH * (half + 1))
                sl = slice(half * TH, (half + 1) * TH)
                sp.dma_start(x_out[:, sl, :], X[:, sl, :]).then_inc(stored, 16)
            sp.wait_ge(stored, 32)


        ternary_pieces = [(k, gu[:, c, k, lo:lo + HALF]) for k in range(2) for c in range(ND) for lo in (0, HALF)] \
            + [(2, WF[:, 2 * ND * F + lo:2 * ND * F + lo + HALF]) for lo in range(0, NF * D, HALF)]

        @block.gpsimd
        def _(pool):
            steps = 0

            def step(ins):
                nonlocal steps
                steps += 1
                ins.then_inc(pool_step, 1)
                pool.wait_ge(pool_step, steps)

            def k_rows(n):
                pool.memset(KO[KROWS:KROWS + 3, :].bitcast(F32), ONES_PAIR).then_inc(k_ones, 1)
                pool.wait_ge(k_ones, n)

            def blank_v(n):
                step(pool.memset(V[:, :, :], 0.0))
                pool.memset(V[:, :, HD:HD + 1], 1.0).then_inc(v_blank, 1)
                pool.wait_ge(v_blank, n)

            k_rows(1)
            blank_v(1)
            pool.memset(ones[:, :], 1.0).then_inc(v_blank, 1)
            pool.wait_ge(v_blank, 2)
            if subs > 2:
                pool.wait_ge(xn_ready, 2 * NT)
                pool.memset(KO[:, 0:KV * 2 * (WIN + S)].bitcast(F32), 0.0).then_inc(k_ones, 1)
                pool.wait_ge(k_ones, 2)
            for s in range(4, subs):
                if SUBLAYERS[s] == ATT:
                    pool.wait_ge(xn_ready, NT * s)
                    k_rows(3 if s == 4 else 4)
                if s == 4:
                    blank_v(3)
                if s == 6:
                    pool.wait_ge(tern_scale, 1)
                    for k, w in ternary_pieces:
                        step(pool.tensor_scalar(tt[:, :], w, tern[:, 6 + k:7 + k], None, ALU.is_gt))
                        step(pool.tensor_scalar(w, w, tern[:, 9 + k:10 + k], None, ALU.is_lt))
                        step(pool.tensor_tensor(w, w, tt[:, :], ALU.subtract))
                    pool.memset(tt[:, 0:1], 0.0).then_inc(tern_ready, 1)

        @block.scalar
        def _(act):
            e_used = 0

            def e_slot():
                nonlocal e_used
                e_used += 1
                act.wait_ge(e_full, e_used)
                return pair[(e_used - 1) % 2]

            def copy_transposed(half):
                for c in range(ND):
                    ps = e_slot()
                    act.activation(xT[:, c, half * HALF:(half + 1) * HALF], ps[:, 0, :], ACT.Copy).then_inc(e_free, 1)

            def attention(s):
                scale = 1.0 / 32 if s == LAST_ATT else 0.25
                a = a_of(s)
                n_acc = ACC0[s]
                for item in PLAN:
                    if item[0] == "mT" and s == LAST_ATT:
                        g = item[1]
                        act.wait_ge(mp_ready, NG * a + g + 1)
                        act.activation(em[:, g % 2, :, :], nm[:, g % 2, :, :], ACT.Exp, scale=scale)\
                            .then_inc(em_ready, 1)
                    if item[0] == "exp":
                        _, g, qh, kb = item
                        st = STEP[item[1:]]
                        n = span(qh, kb)[1]
                        if st >= 2:
                            act.wait_ge(pv_done, PV0[s] + st - 1)
                        for i in range(2):
                            ps = e_slot()
                            act.activation(pb[:, st % 2, 2 * i:2 * i + 2, 0:n], ps[:, :, 0:n], ACT.Exp, scale=scale)\
                                .then_inc(e_free, 1)
                    if item[0] == "acc":
                        _, g, qh = item
                        act.wait_ge(pv_done, PV0[s] + STEP[g, qh, TH * (qh + 1) - 1] + 1)
                        act.activation(acc[:, n_acc % 2, :], pvb[:, :], ACT.Copy).then_inc(acc_ready, 1)
                        n_acc += 1
                for half in range(2):
                    copy_transposed(half)
                for half in range(2):
                    copy_transposed(half)

            def windowed(s):
                n_acc = ACC0[s]
                for item in W_PLAN:
                    if item[0] == "S":
                        u = item[1]
                        t, p = divmod(u, NH // 2)
                        ps = e_slot()
                        act.wait_ge(wmax_ready, u + 1)
                        if u >= 2:
                            act.wait_ge(u_ready, u - 1)
                        for i in range(2):
                            for z in range(2):
                                k = 2 * i + z
                                last = act.activation(ew[:, u % 2, k, :], ps[:, i, z * WK:(z + 1) * WK], ACT.Exp,
                                                      bias=nm2[:, u % 2, k:k + 1],
                                                      accum_out=r12[:, t, 2 * p + i, z:z + 1])
                        last.then_inc(e_free, 1)
                    if item[0] == "acc":
                        act.wait_ge(pv_done, PV0[s] + item[1] + 1)
                        act.activation(acc[:, n_acc % 2, :], pvb[:, :], ACT.Copy).then_inc(acc_ready, 1)
                        n_acc += 1
                for half in range(4):
                    copy_transposed(half % 2)

            def ffn(nf, gate_scale):
                for i in range(2 * nf):
                    fc = i % nf
                    rows = P if nf == NF or fc < nf - 1 else F_MOE - P * (nf - 1)
                    ps = e_slot()
                    act.activation(sg[0:rows, i % 4, :], ps[0:rows, 0, :], ACT.Silu, scale=gate_scale(fc))\
                        .then_inc(e_free, 1)
                for half in range(2):
                    copy_transposed(half)

            act.wait_ge(ld_x, 16 * 4)
            act.activation(idb[:, :], idf, ACT.Copy).then_inc(cast_ready, 1)
            act.activation(maskb[:, :, :], cst[:, C_MASK:C_MASK + 2 * P].rearrange("p (k n) -> p k n", k=2), ACT.Copy)\
                .then_inc(cast_ready, 1)
            act.activation(wmaskb[:, :, :], cst[:, C_WMASK:C_WMASK + 4 * WK].rearrange("p (k n) -> p k n", k=2), ACT.Copy)\
                .then_inc(cast_ready, 1)
            act.wait_ge(ld_glu, 16 * 3)
            act.activation(WF[:, 0:2 * ND * F], raw[:, 0:2 * ND * F], ACT.Copy).then_inc(glu_ready, 1)
            act.wait_ge(glu_ready, 2)

            for s in range(subs):
                kind = SUBLAYERS[s]
                if kind == ATT:
                    attention(s)
                elif kind == WATT:
                    windowed(s)
                elif kind == GLU:
                    ffn(NF, lambda fc: cst[:, C_SG + fc:C_SG + fc + 1])
                elif kind == MOE:
                    act.wait_ge(ld_sel, 16)
                    act.activation(selb[:, :], selF[:, :], ACT.Copy).then_inc(cast_ready, 1)
                    act.wait_ge(logit_max, 1)
                    act.activation(wm[:, 1, :, :], wm[:, 0, :, :], ACT.Exp).then_inc(logit_exp, 1)
                    ffn(NF_MOE, lambda fc: 1.0)
                elif kind == TERN:
                    ffn(NF, lambda fc: tern[:, 12:13])
                else:
                    for half in range(2):
                        copy_transposed(half)

        @block.vector
        def _(dve):
            r_used = 0
            steps = 0

            def r_slot():
                nonlocal r_used
                r_used += 1
                dve.wait_ge(r_full, r_used)
                return bank[(r_used - 1) % 3]

            def r_done(ins):
                ins.then_inc(r_free, 1)

            def r_wait():
                dve.wait_ge(r_free, r_used)

            def step(ins):
                nonlocal steps
                steps += 1
                ins.then_inc(dve_step, 1)
                dve.wait_ge(dve_step, steps)

            def split(x, hi, mid, lo, tmp):
                step(dve.tensor_copy(hi, x))
                step(dve.tensor_tensor(tmp, x, hi, ALU.subtract))
                step(dve.tensor_copy(mid, tmp))
                return dve.tensor_tensor(lo, tmp, mid, ALU.subtract)

            def post(s, half):
                t0 = half * TH
                for t in range(t0, t0 + TH):
                    if SUBLAYERS[s] == BIN:
                        step(dve.tensor_tensor(X[:, t, :], X[:, t, :], biasB[:, :], ALU.add))
                    ps = r_slot()
                    r_done(dve.tensor_tensor(X[:, t, :], ps[:, 0:D], X[:, t, :], ALU.add))
                    r_wait()
                    step(dve.bn_stats(stats[:, t, :], X[:, t, :]))
                for t in range(t0, t0 + TH):
                    last = dve.bn_aggr(mv[:, t, :], stats[:, t, :])
                step(last)
                v, y, w = lnv[:, 0, :], lnv[:, 1, :], lnv[:, 2, :]
                step(dve.tensor_scalar(v, mv[:, t0:t0 + TH, 1], EPS, None, ALU.add))
                step(dve.tensor_scalar(y.bitcast(I32), v.bitcast(I32), 1, None, ALU.logical_shift_right))
                step(dve.tensor_scalar(y.bitcast(I32), y.bitcast(I32), -1.0, float(0x5F3759DF), ALU.mult, ALU.add))
                for _ in range(3):
                    step(dve.scalar_tensor_tensor(w, y, -0.5, y, ALU.mult, ALU.mult))
                    step(dve.tensor_tensor(w, w, v, ALU.mult))
                    step(dve.scalar_tensor_tensor(y, w, 1.5, y, ALU.add, ALU.mult))
                for t in range(t0, t0 + TH):
                    dve.tensor_scalar(X[:, t, :], X[:, t, :], mv[:, t, 0:1], lnv[:, 1, t - t0:t - t0 + 1],
                                      ALU.subtract, ALU.mult).then_inc(xn_ready, 1)
                dve.wait_ge(xn_ready, NT * s + t0 + TH)

            def finish_parts(s, tile, half, x, rows, tmp):
                n = PARTS0[s] + tile
                if half == 0 and n >= 2:
                    dve.wait_ge(scr_written, 16 * (n - 1))
                hi, mid, lo = (parts[0:rows, n % 2, k, half * HALF:(half + 1) * HALF] for k in range(3))
                last = split(x, hi, mid, lo, tmp)
                if half == 0:
                    step(last)
                else:
                    last.then_inc(parts_ready, 1)
                    dve.wait_ge(parts_ready, n + 1)

            def attention(s):
                a = a_of(s)
                for tile in range(4):
                    for half in range(2):
                        ps = r_slot()
                        r_done(dve.tensor_copy(rest[:, 0, :], ps[:, :]))
                        r_wait()
                        finish_parts(s, tile, half, rest[:, 0, :], P, rest[:, 1, :])
                if s != 6:
                    dve.wait_ge(v_blank, {0: 2, 4: 3}[s])
                for t in range(NT):
                    ps = r_slot()
                    r_done(dve.tensor_copy(v_all[:, t, :, 0:HD], ps[:, 0:D].rearrange("p (h d) -> p h d", d=HD)))
                if s == LAST_ATT:
                    dve.wait_ge(scr_written, 16 * (PARTS0[s] + 4))
                    for t in reversed(range(NT)):
                        ps = r_slot()
                        if t == NT - 1:
                            step(dve.tensor_copy(wsuf[:, t, :], ps[:, 0:D]))
                            r_done(dve.tensor_copy(carry[:, :], ps[:, D:2 * D]))
                        else:
                            step(dve.tensor_tensor(wsuf[:, t, :], ps[:, 0:D], carry[:, :], ALU.add))
                            r_done(dve.tensor_tensor(carry[:, :], ps[:, D:2 * D], carry[:, :], ALU.add))
                        r_wait()
                    for b in range(2):
                        step(dve.tensor_copy(pmx[:, b, 2, :, :],
                                             cst[:, C_FLOOR:C_FLOOR + NT].unsqueeze(2).to_broadcast([P, NT, HG])))
                for item in PLAN:
                    if item[0] == "max":
                        _, g, t, c, j = item
                        n = min((t + 1) * P - c * HALF, HALF)
                        ps = r_slot()
                        r_done(dve.tensor_reduce(pmx[:, g % 2, c, t, j:j + 1], ps[:, 0:n], AX.X, ALU.max))
                    if item[0] == "mT":
                        g = item[1]
                        n = NG * a + g
                        b = g % 2
                        r_wait()
                        step(dve.tensor_reduce(nm[:, b, :, :], pmx[:, b, :, :, :].rearrange("p c t j -> p t j c"),
                                               AX.X, ALU.max, negate=True))
                        split(nm[:, b, :, :], mp[:, b, :, 0, :], mp[:, b, :, 1, :], mp[:, b, :, 2, :], nmr[:, :, :])\
                            .then_inc(mp_ready, 1)
                        ps = r_slot()
                        if n >= 2:
                            dve.wait_ge(m_in[n % 2], 16 * (n // 2))
                        dve.tensor_copy(mrow[:, n % 2, :], ps[0:3 * HG, :].bitcast(BF16)).then_inc(mrow_ready, 1)
                        dve.wait_ge(mrow_ready, n + 1)
                        dve.nop().then_inc(r_free, 1)
                    if item[0] == "accT":
                        _, g, qh = item
                        t0 = qh * TH
                        if s == LAST_ATT:
                            dve.wait_ge(em_ready, g + 1)
                        r_wait()
                        ps = r_slot()[:, :].rearrange("p (t h c) -> p t h c", t=TH, h=HG)
                        o = A[:, t0:t0 + TH, g * HG * HD:(g + 1) * HG * HD].rearrange("p t (h d) -> p t h d", d=HD)
                        den = rc[:, 0, :].rearrange("p (t h) -> p t h", h=HG)
                        inv = rc[:, 1, :].rearrange("p (t h) -> p t h", h=HG)
                        wide = inv.unsqueeze(3).to_broadcast([P, TH, HG, HD])
                        if s != LAST_ATT:
                            step(dve.reciprocal(inv, ps[:, :, :, HD]))
                            r_done(dve.tensor_tensor(o, ps[:, :, :, 0:HD], wide, ALU.mult))
                        else:
                            e = em[:, g % 2, t0:t0 + TH, :]
                            cnt = cst[:, C_CNT + t0:C_CNT + t0 + TH].unsqueeze(2).to_broadcast([P, TH, HG])
                            num = big[:, :].rearrange("p (t h d) -> p t h d", t=TH, h=HG)
                            w = wsuf[:, t0:t0 + TH, g * HG * HD:(g + 1) * HG * HD]\
                                .rearrange("p t (h d) -> p t h d", d=HD)
                            step(dve.tensor_tensor(den, e, cnt, ALU.mult))
                            step(dve.tensor_tensor(den, ps[:, :, :, HD], den, ALU.add))
                            step(dve.reciprocal(inv, den))
                            step(dve.tensor_tensor(num, w, e.unsqueeze(3).to_broadcast([P, TH, HG, HD]), ALU.mult))
                            step(dve.tensor_tensor(num, ps[:, :, :, 0:HD], num, ALU.add))
                            r_done(dve.tensor_tensor(o, num, wide, ALU.mult))
                for half in range(2):
                    post(s, half)

            def windowed(s):
                e0 = e_before(s)
                dve.wait_ge(ld_rope, 16)
                for tile in range(3):
                    rows, sc = (P, (HD / 2) ** -0.5) if tile < 2 else (KV * HD, 1.0)
                    for half in range(2):
                        cols = slice(half * HALF, (half + 1) * HALF)
                        for k in range(2):
                            ps = r_slot()
                            r_done(dve.scalar_tensor_tensor(rest[0:rows, k, :], ps[0:rows, :], sc,
                                                            rope[0:rows, k, cols], ALU.mult, ALU.mult))
                        r_wait()
                        step(dve.tensor_tensor(rest[0:rows, 0, :], rest[0:rows, 0, :], rest[0:rows, 1, :], ALU.add))
                        finish_parts(s, tile, half, rest[0:rows, 0, :], rows, rest[0:rows, 1, :])
                ps = r_slot()
                r_done(dve.tensor_copy(v_own[:, :, :, 0:HD],
                                       ps[:, :].rearrange("p (t h d) -> p t h d", t=NT, h=KV)))
                ps = r_slot()
                r_done(dve.tensor_copy(v_prev[0:WIN, 1:NT, :, 0:HD],
                                       ps[0:WIN, KV * HD:].rearrange("p (t h d) -> p t h d", t=NT - 1, h=KV)))

                def difference(u):
                    t, p = divmod(u, NH // 2)
                    b = u % 2
                    dve.wait_ge(e_free, e0 + u + 1)
                    step(dve.reciprocal(cc[:, b, 0:2], r12[:, t, 2 * p:2 * p + 2, 1]))
                    step(dve.tensor_tensor(cc[:, b, 0:2], cc[:, b, 0:2], r12[:, t, 2 * p:2 * p + 2, 0], ALU.mult))
                    step(dve.tensor_tensor(cc[:, b, 0:2], cc[:, b, 0:2],
                                           cst[:, C_LAM + 2 * p:C_LAM + 2 * p + 2], ALU.mult))
                    for i in range(2):
                        last = dve.scalar_tensor_tensor(uw[:, u // 2 % 2, u % 2 * 2 + i, :], ew[:, b, 2 * i + 1, :],
                                                        cc[:, b, i:i + 1], ew[:, b, 2 * i, :],
                                                        ALU.mult, ALU.subtract)
                    last.then_inc(u_ready, 1)

                for item in W_PLAN:
                    if item[0] == "S":
                        u = item[1]
                        dve.wait_ge(e_full, e0 + u + 1)
                        ps = pair[(e0 + u) % 2]
                        dve.tensor_reduce(nm2[:, u % 2, :].rearrange("p (i z) -> p i z", i=2),
                                          ps[:, :, 0:2 * WK].rearrange("p i (z n) -> p i z n", z=2),
                                          AX.X, ALU.max, negate=True).then_inc(wmax_ready, 1)
                        if u >= 1:
                            difference(u - 1)
                    if item[0] == "flush":
                        difference(NT * NH // 2 - 1)
                    if item[0] == "uT":
                        gi = item[1]
                        for k in range(2):
                            if k == 0 and gi < NG:
                                continue
                            rows = (WIN, P)[k]
                            ps = r_slot()
                            r_done(dve.tensor_scalar(uT[0:rows, gi % 4, k, :], ps[0:rows, :], -1.0, 0.0,
                                                     ALU.mult, ALU.max))
                    if item[0] == "accT":
                        t = item[1]
                        r_wait()
                        ps = r_slot()[:, :].rearrange("p (h g c) -> p h g c", h=HG, g=KV)
                        den = rc[:, 0, :].rearrange("p (h g) -> p h g", g=KV)
                        inv = rc[:, 1, :].rearrange("p (h g) -> p h g", g=KV)
                        r1 = r12[:, t, :, 0].rearrange("p (g h) -> p h g", g=KV)
                        o = A[:, t, :].rearrange("p (g h d) -> p h g d", g=KV, h=HG)
                        step(dve.scalar_tensor_tensor(den, r1, 1e-6, ps[:, :, :, HD], ALU.mult, ALU.add))
                        step(dve.reciprocal(inv, den))
                        r_done(dve.tensor_tensor(o, ps[:, :, :, 0:HD],
                                                 inv.unsqueeze(3).to_broadcast([P, HG, KV, HD]), ALU.mult))
                for half in range(2):
                    post(s, half)

            def ranked(x, n, low, k):
                ge = rank[:, 0, 0:NT * n * n].rearrange("p (t i j) -> p t i j", t=NT, i=n)
                eq = rank[:, 1, 0:NT * n * n].rearrange("p (t i j) -> p t i j", t=NT, i=n)
                rival = x.unsqueeze(2).to_broadcast([P, NT, n, n])
                own = x.unsqueeze(3).to_broadcast([P, NT, n, n])
                lower = cst[:, low:low + n * n].rearrange("p (i j) -> p i j", i=n).unsqueeze(1)\
                    .to_broadcast([P, NT, n, n])
                step(dve.tensor_tensor(ge, rival, own, ALU.is_gt))
                step(dve.tensor_tensor(eq, rival, own, ALU.is_equal))
                step(dve.tensor_tensor(eq, eq, lower, ALU.mult))
                step(dve.tensor_tensor(ge, ge, eq, ALU.add))
                r = wm[:, k, :, 0:n]
                step(dve.tensor_reduce(r, ge, AX.X, ALU.add))
                step(dve.tensor_scalar(r, r, 2.0, None, ALU.is_lt))
                return r

            def route():
                ps = r_slot()[:, 0:NT * EXPERTS].rearrange("p (t e) -> p t e", t=NT)
                top = wm[:, 5, :, 0]
                step(dve.tensor_reduce(top, ps, AX.X, ALU.max))
                r_done(dve.tensor_tensor(wm[:, 0, :, :], ps, top.unsqueeze(2).to_broadcast([P, NT, EXPERTS]),
                                         ALU.subtract))
                r_wait()
                dve.nop().then_inc(logit_max, 1)
                dve.wait_ge(logit_exp, 1)
                step(dve.tensor_reduce(top, wm[:, 1, :, :], AX.X, ALU.add))
                step(dve.reciprocal(wm[:, 5, :, 1], top))
                step(dve.tensor_tensor(wm[:, 2, :, :], wm[:, 1, :, :],
                                       wm[:, 5, :, 1].unsqueeze(2).to_broadcast([P, NT, EXPERTS]), ALU.mult))
                step(dve.tensor_reduce(wm[:, 3, :, 0:4], wm[:, 2, :, :].rearrange("p t (g k) -> p t g k", g=4),
                                       AX.X, ALU.max))
                in_group = ranked(wm[:, 3, :, 0:4], 4, C_LOW4, 4)
                step(dve.tensor_tensor(wm[:, 1, :, :].rearrange("p t (g k) -> p t g k", g=4),
                                       wm[:, 2, :, :].rearrange("p t (g k) -> p t g k", g=4),
                                       in_group.unsqueeze(3).to_broadcast([P, NT, 4, 2]), ALU.mult))
                chosen = ranked(wm[:, 1, :, :], 8, C_LOW8, 4)
                step(dve.memset(wmx[:, :, EXPERTS:NEXP1], 1.0))
                step(dve.tensor_tensor(wmx[:, :, 0:EXPERTS], wm[:, 1, :, :], chosen, ALU.mult))
                tmp = rank[:, 0, 0:NT * NEXP1].rearrange("p (t e) -> p t e", t=NT)
                split(wmx[:, :, :], wp[:, :, 0, :], wp[:, :, 1, :], wp[:, :, 2, :], tmp).then_inc(wm_ready, 1)
                ps = r_slot()
                r_done(dve.tensor_copy(wT[0:3 * NEXP1, :], ps[0:3 * NEXP1, :].bitcast(BF16)))

            def ffn(s, nf, up_scale):
                e0 = e_before(s)
                for half in range(2):
                    for fc in range(nf):
                        i = half * nf + fc
                        rows = P if nf == NF or fc < nf - 1 else F_MOE - P * (nf - 1)
                        h = hid[half][0:rows, fc, :]
                        gate = sg[0:rows, i % 4, :]
                        ps = r_slot()
                        dve.wait_ge(e_free, e0 + i + 1)
                        if SUBLAYERS[s] == MOE:
                            r_done(dve.tensor_tensor(sgu[0:rows, i % 2, :], ps[0:rows, :], gate, ALU.mult))
                            r_wait()
                            ps = r_slot()
                            r_done(dve.tensor_tensor(h, ps[0:rows, :], sgu[0:rows, i % 2, :], ALU.mult))
                        else:
                            r_done(dve.scalar_tensor_tensor(h, ps[:, :], up_scale(fc), gate, ALU.mult, ALU.mult))
                    post(s, half)

            dve.wait_ge(ld_glu, 16 * 3)
            dve.tensor_tensor(wd[:, :, :], raw[:, 2 * ND * F:2 * ND * F + NF * D].rearrange("p (f n) -> p f n", f=NF),
                              sdown[:, :].unsqueeze(1).to_broadcast([P, NF, D]), ALU.mult).then_inc(glu_ready, 1)
            step(dve.memset(pmx[:, :, :, :, :], LOWEST))
            for s in range(subs):
                kind = SUBLAYERS[s]
                if kind == ATT:
                    attention(s)
                elif kind == WATT:
                    windowed(s)
                elif kind == GLU:
                    ffn(s, NF, lambda fc: cst[:, C_SU + fc:C_SU + fc + 1])
                elif kind == MOE:
                    route()
                    ffn(s, NF_MOE, None)
                elif kind == TERN:
                    ffn(s, NF, lambda fc: tern[:, 13:14])
                else:
                    dve.wait_ge(ld_bin, 32)
                    dve.scalar_tensor_tensor(rest[:, :, 0:D], WB[:, :, :], -1.0, WB[:, :, :], ALU.mult, ALU.max)\
                        .then_inc(abs_ready, 1)
                    dve.wait_ge(abs_ready, 1)
                    step(dve.tensor_scalar(WB[:, :, :], WB[:, :, :], 0.0, 2.0, ALU.is_ge, ALU.mult))
                    step(dve.tensor_scalar(WB[:, :, :], WB[:, :, :], 1.0, None, ALU.subtract))
                    ps = r_slot()
                    r_done(dve.tensor_scalar(carry[:, :], ps[:, 0:D], 1.0 / D, None, ALU.mult))
                    r_wait()
                    dve.tensor_tensor(WB[:, :, :], WB[:, :, :], carry[:, :].unsqueeze(1).to_broadcast([P, ND, D]),
                                      ALU.mult).then_inc(bin_ready, 1)
                    if subs > 6:
                        dve.wait_ge(ld_tern, 16)
                        for k in range(2):
                            step(dve.tensor_reduce(tern[:, k:k + 1], gu[:, :, k, :], AX.XY, ALU.add,
                                                   apply_absolute_value=True))
                        dve.tensor_reduce(tern[:, 2:3], wd[:, :, :], AX.XY, ALU.add,
                                          apply_absolute_value=True).then_inc(abs_ready, 1)
                        ps = r_slot()
                        r_done(dve.tensor_scalar(tern[:, 3:6], ps[:, 0:3], 1.0 / (D * F), 1e-8, ALU.mult, ALU.add))
                        r_wait()
                        step(dve.tensor_scalar(tern[:, 6:9], tern[:, 3:6], 0.5, None, ALU.mult))
                        step(dve.tensor_scalar(tern[:, 9:12], tern[:, 3:6], -0.5, None, ALU.mult))
                        step(dve.tensor_scalar(tern[:, 12:13], tern[:, 3:4], -1.0, None, ALU.mult))
                        dve.tensor_tensor(tern[:, 13:14], tern[:, 4:5], tern[:, 5:6], ALU.mult).then_inc(tern_scale, 1)
                    for half in range(2):
                        post(s, half)

        @block.tensor
        def _(pe):
            r_used = 0
            e_used = 0
            x_at = [0, 0]

            def r_slot():
                nonlocal r_used
                r_used += 1
                if r_used > 3:
                    pe.wait_ge(r_free, r_used - 3)
                return bank[(r_used - 1) % 3]

            def e_slot():
                nonlocal e_used
                e_used += 1
                if e_used > 2:
                    pe.wait_ge(e_free, e_used - 2)
                return pair[(e_used - 1) % 2]

            def x_ready(half):
                if x_at[half]:
                    pe.wait_ge(e_free, x_at[half])

            def over_width(ps, w, x):
                for c in range(ND):
                    last = pe.matmul(ps, w(c), x(c), start=(c == 0), stop=(c == ND - 1))
                return last

            def transpose_half(src, half):
                for c in range(ND):
                    ps = e_slot()
                    for tt_ in range(TH):
                        last = pe.transpose(ps[:, 0, tt_ * P:(tt_ + 1) * P],
                                            src[:, half * TH + tt_, c * P:(c + 1) * P], idf)
                    last.then_inc(e_full, 1)

            def new_x(s, half):
                pe.wait_ge(xn_ready, NT * s + TH * (half + 1))
                transpose_half(X, half)
                x_at[half] = e_used

            def project_out(s, half, w):
                for t in range(half * TH, (half + 1) * TH):
                    ps = r_slot()
                    over_width(ps[:, 0:D], lambda c: xT[:, c, t * P:(t + 1) * P], lambda c: w[:, c, :])\
                        .then_inc(r_full, 1)

            def attention_out(s, w):
                for half in range(2):
                    transpose_half(A, half)
                    pe.wait_ge(e_free, e_used)
                    project_out(s, half, w)
                for half in range(2):
                    new_x(s, half)

            def attention(s):
                a = a_of(s)
                e_at = {}
                pe.wait_ge(*{0: (ld_x, 16 * 4), 4: (ld_att2, 16), 6: (ld_att3, 16)}[s])
                for tile in range(4):
                    side, hi = tile % 2, tile // 2
                    w = w_att(s, side * D + hi * P, P)
                    for half in range(2):
                        x_ready(half)
                        ps = r_slot()
                        over_width(ps[:, :], lambda c: w[:, c, :],
                                   lambda c: xT[:, c, half * HALF:(half + 1) * HALF]).then_inc(r_full, 1)
                w = w_att(s, 2 * D, D)
                for t in range(NT):
                    ps = r_slot()
                    over_width(ps[:, 0:D], lambda c: xT[:, c, t * P:(t + 1) * P], lambda c: w[:, c, :])\
                        .then_inc(r_full, 1)
                v_at = r_used
                if s == LAST_ATT:
                    pe.wait_ge(r_free, v_at)
                    pe.wait_ge(v_blank, 2)
                    for t in reversed(range(NT)):
                        ps = r_slot()
                        v = v_all[:, t, :, 0:HD]
                        pe.matmul(ps[:, 0:D], cst[:, C_TRI:C_TRI + P], v, start=True, stop=True)
                        pe.matmul(ps[:, D:2 * D], ones[:, :], v, start=True, stop=True).then_inc(r_full, 1)
                pe.wait_ge(cast_ready, 2)
                pe.wait_ge(k_ones, {0: 1, 4: 3, 6: 4}[s])
                for item in PLAN:
                    if item[0] == "max":
                        _, g, t, c, j = item
                        h = g * HG + j
                        if item == ("max", 0, 0, 0, 0):
                            pe.wait_ge(rep_a, 16 * REP[s][0])
                        if item == ("max", 2, 0, 0, 0):
                            pe.wait_ge(rep_b, 16 * REP[s][1])
                        n = min((t + 1) * P - c * HALF, HALF)
                        diag = (t + 1) * P - c * HALF <= HALF
                        ps = r_slot()
                        last = pe.matmul(ps[:, 0:n], q_op[0:KROWS, h, t * P:(t + 1) * P],
                                         k_op[0:KROWS, h, c * HALF:c * HALF + n], start=True, stop=not diag)
                        if diag:
                            last = pe.matmul(ps[:, n - P:n], idb[:, :], maskb[:, 0, :], start=False, stop=True)
                        last.then_inc(r_full, 1)
                    if item[0] == "mT":
                        g = item[1]
                        pe.wait_ge(mp_ready, NG * a + g + 1)
                        ps = r_slot()[0:3 * HG, :].bitcast(BF16)
                        for t in range(NT):
                            last = pe.transpose(ps[:, t * P:(t + 1) * P],
                                                mp[:, g % 2, t, :, :].rearrange("p k j -> p (k j)"), idb[:, :])
                        last.then_inc(r_full, 1)
                    if item[0] == "exp":
                        _, g, qh, kb = item
                        if (qh, kb) == (0, 0):
                            n = NG * a + g
                            pe.wait_ge(m_in[n % 2], 16 * (n // 2 + 1))
                        q0, n = span(qh, kb)
                        diag = kb * P >= qh * HALF
                        for i in range(2):
                            ps = e_slot()
                            for j in range(2):
                                h = g * HG + 2 * i + j
                                last = pe.matmul(ps[:, j, 0:n], k_op[0:KROWS + 3, h, kb * P:(kb + 1) * P],
                                                 q_op[0:KROWS + 3, h, q0:q0 + n], start=True, stop=not diag)
                                if diag:
                                    last = pe.matmul(ps[:, j, 0:P], idb[:, :], maskb[:, 1, :], start=False, stop=True)
                            last.then_inc(e_full, 1)
                        e_at[g, qh, kb] = e_used
                    if item[0] == "pv":
                        _, g, qh, kb = item
                        st = STEP[g, qh, kb]
                        q0, n = span(qh, kb)
                        if st == 0:
                            pe.wait_ge(r_free, v_at)
                        if kb == 0 and ACC0[s] + 2 * g + qh:
                            pe.wait_ge(acc_ready, ACC0[s] + 2 * g + qh)
                        pe.wait_ge(e_free, e_at[g, qh, kb])
                        for j in range(HG):
                            last = pe.matmul(pvb[j * STRIP:(j + 1) * STRIP, q0 - qh * HALF:HALF],
                                             v_all[:, kb, g * HG + j, :], pb[:, st % 2, j, 0:n],
                                             start=(kb == 0), stop=(kb == TH * (qh + 1) - 1))
                        last.then_inc(pv_done, 1)
                    if item[0] == "accT":
                        _, g, qh = item
                        n = ACC0[s] + 2 * g + qh
                        pe.wait_ge(acc_ready, n + 1)
                        ps = r_slot()
                        for tt_ in range(TH):
                            last = pe.transpose(ps[:, tt_ * P:(tt_ + 1) * P], acc[:, n % 2, tt_ * P:(tt_ + 1) * P], idf)
                        last.then_inc(r_full, 1)
                pe.wait_ge(r_free, r_used)
                attention_out(s, w_att(s, 3 * D, D))

            def windowed(s):
                assert e_used == e_before(s)
                pe.wait_ge(ld_watt, 16)
                for tile in range(3):
                    rows, at = ((P, (tile * P, D + tile * P)) if tile < 2 else (KV * HD, (2 * D, 2 * D + KV * HD)))
                    for half in range(2):
                        x_ready(half)
                        for k in range(2):
                            w = w_att(s, at[k], rows)
                            ps = r_slot()
                            over_width(ps[0:rows, :], lambda c: w[:, c, :],
                                       lambda c: xT[:, c, half * HALF:(half + 1) * HALF]).then_inc(r_full, 1)
                w = w_att(s, 2 * D + 2 * KV * HD, KV * HD)
                ps = r_slot()
                for t in range(NT):
                    last = over_width(ps[:, t * KV * HD:(t + 1) * KV * HD], lambda c: xT[:, c, t * P:(t + 1) * P],
                                      lambda c: w[:, c, :])
                last.then_inc(r_full, 1)
                ps = r_slot()
                for t in range(1, NT):
                    last = over_width(ps[0:WIN, t * KV * HD:(t + 1) * KV * HD],
                                      lambda c: xT[:, c, t * P - WIN:t * P], lambda c: w[:, c, :])
                last.then_inc(r_full, 1)
                v_at = r_used
                uT_at = {}
                pe.wait_ge(cast_ready, 3)
                pe.wait_ge(rep_a, 16 * REP[s][0])
                for item in W_PLAN:
                    if item[0] == "S":
                        u = item[1]
                        t, p = divmod(u, NH // 2)
                        ps = e_slot()
                        for i in range(2):
                            o = ps[:, i, 0:2 * WK]
                            pe.matmul(o, q_op[0:KROWS, 2 * p + i, t * P:(t + 1) * P],
                                      kw_op[0:KROWS, p // 2, :, t * P:t * P + WK], start=True, stop=False)
                            last = pe.matmul(o, idb[:, :], wmaskb[:, int(t == 0), :], start=False, stop=True)
                        last.then_inc(e_full, 1)
                    if item[0] == "uT":
                        gi = item[1]
                        pe.wait_ge(u_ready, 2 * gi + 2)
                        for k in range(2):
                            if k == 0 and gi < NG:
                                continue
                            rows, lo = ((WIN, 0), (P, WIN))[k]
                            ps = r_slot()
                            for hh in range(HG):
                                last = pe.transpose(ps[0:rows, hh * P:(hh + 1) * P],
                                                    uw[:, gi % 2, hh, lo:lo + rows], idf)
                            last.then_inc(r_full, 1)
                        uT_at[gi] = r_used
                    if item[0] == "pv":
                        gi = item[1]
                        t, g = divmod(gi, NG)
                        if gi == 0:
                            pe.wait_ge(r_free, v_at)
                        if g == 0:
                            pe.wait_ge(acc_ready, ACC0[s] + t)
                        pe.wait_ge(r_free, uT_at[gi])
                        o = pvb[g * STRIP:(g + 1) * STRIP, :]
                        if t:
                            pe.matmul(o, v_prev[0:WIN, t, g, :], uT[0:WIN, gi % 4, 0, :], start=True, stop=False)
                        last = pe.matmul(o, v_own[:, t, g, :], uT[:, gi % 4, 1, :], start=(t == 0), stop=True)
                        if g == NG - 1:
                            last.then_inc(pv_done, 1)
                    if item[0] == "accT":
                        t = item[1]
                        n = ACC0[s] + t
                        pe.wait_ge(acc_ready, n + 1)
                        ps = r_slot()
                        for hh in range(HG):
                            last = pe.transpose(ps[:, hh * P:(hh + 1) * P], acc[:, n % 2, hh * P:(hh + 1) * P], idf)
                        last.then_inc(r_full, 1)
                pe.wait_ge(r_free, r_used)
                attention_out(s, w_att(s, 704, D))

            def ffn(s, nf, w_gu, w_d):
                assert e_used == e_before(s)
                moe = SUBLAYERS[s] == MOE
                if moe:
                    pe.wait_ge(ld_moe, 16)
                    ps = r_slot()
                    for t in range(NT):
                        x_ready(t // TH)
                        last = over_width(ps[:, t * EXPERTS:(t + 1) * EXPERTS], lambda c: xT[:, c, t * P:(t + 1) * P],
                                          lambda c: cst[:, C_GW + c * EXPERTS:C_GW + (c + 1) * EXPERTS])
                    last.then_inc(r_full, 1)
                    pe.wait_ge(wm_ready, 1)
                    ps = r_slot()[0:3 * NEXP1, :].bitcast(BF16)
                    for t in range(NT):
                        last = pe.transpose(ps[:, t * P:(t + 1) * P], wp[:, t, :, :].rearrange("p k e -> p (k e)"),
                                            idb[:, :])
                    last.then_inc(r_full, 1)
                    wT_at = r_used
                if s == 1:
                    pe.wait_ge(glu_ready, 2)
                if SUBLAYERS[s] == TERN:
                    pe.wait_ge(tern_ready, 1)
                rows = [P] * nf
                if moe:
                    rows[-1] = F_MOE - P * (nf - 1)

                def gate_up(half):
                    x_ready(half)
                    xs = [xT[:, c, half * HALF:(half + 1) * HALF] for c in range(ND)]
                    for fc in range(nf):
                        n = rows[fc]
                        ps = e_slot()
                        over_width(ps[0:n, 0, :], lambda c: w_gu[:, c, 0, fc * P:fc * P + n], lambda c: xs[c])\
                            .then_inc(e_full, 1)
                        ps = r_slot()
                        over_width(ps[0:n, :], lambda c: w_gu[:, c, 1, fc * P:fc * P + n], lambda c: xs[c])\
                            .then_inc(r_full, 1)
                        if moe:
                            ps = r_slot()
                            if half == 0 and fc == 0:
                                pe.wait_ge(r_free, wT_at)
                                pe.wait_ge(cast_ready, 4)
                            pe.matmul(ps[0:n, :], selb[:, fc * P:fc * P + n],
                                      wT[0:3 * NEXP1, half * HALF:(half + 1) * HALF], start=True, stop=True)\
                                .then_inc(r_full, 1)
                    return r_used

                def down(half, h_at):
                    pe.wait_ge(r_free, h_at)
                    if moe and half == 0:
                        pe.wait_ge(ld_moed, 16)
                    for t in range(half * TH, (half + 1) * TH):
                        ps = r_slot()
                        at = (t - half * TH) * P
                        for fc in range(nf):
                            n = rows[fc]
                            last = pe.matmul(ps[:, 0:D], hid[half][0:n, fc, at:at + P], w_d[0:n, fc, :],
                                             start=(fc == 0), stop=(fc == nf - 1))
                        last.then_inc(r_full, 1)

                h_at = gate_up(0)
                down(0, h_at)
                h_at = gate_up(1)
                new_x(s, 0)
                down(1, h_at)
                new_x(s, 1)

            for s in range(subs):
                kind = SUBLAYERS[s]
                if kind == ATT:
                    attention(s)
                elif kind == WATT:
                    windowed(s)
                elif kind == GLU:
                    ffn(s, NF, gu, wd)
                elif kind == MOE:
                    ffn(s, NF_MOE, gu_moe, wd_moe)
                elif kind == TERN:
                    ffn(s, NF, gu, wd)
                else:
                    pe.wait_ge(v_blank, 2)
                    pe.wait_ge(abs_ready, 1)
                    ps = r_slot()
                    over_width(ps[:, 0:D], lambda c: ones[:, :], lambda c: rest[:, c, 0:D]).then_inc(r_full, 1)
                    if subs > 6:
                        pe.wait_ge(abs_ready, 2)
                        ps = r_slot()
                        pe.matmul(ps[:, 0:3], ones[:, :], tern[:, 0:3], start=True, stop=True).then_inc(r_full, 1)
                    pe.wait_ge(bin_ready, 1)
                    for half in range(2):
                        x_ready(half)
                        project_out(s, half, WB)
                    for half in range(2):
                        new_x(s, half)


def arrange(i):
    g = {k: np.asarray(v) for k, v in i.items()}

    def chunks(a):
        return np.ascontiguousarray(a.reshape(-1, P, a.shape[1]).transpose(1, 0, 2))

    x = g["L0_attn_x"].reshape(S, D)
    swap = (np.arange(HD) + HD // 2) % HD
    wq, wk = g["L1_attn_Wq"], g["L1_attn_Wk"]
    wqs = wq.reshape(D, NH, HD)[:, :, swap].reshape(D, NH * HD)
    wks = wk.reshape(D, KV, HD)[:, :, swap].reshape(D, KV * HD)
    cst = constants()
    cst[:, C_LAM:C_LAM + NH] = g["L1_attn_lam"][None, :]
    cst[:, C_SG:C_SG + NF] = g["L0_ffn_s_gate"].reshape(NF, P).T
    cst[:, C_SU:C_SU + NF] = g["L0_ffn_s_up"].reshape(NF, P).T
    cst[:, C_GW:C_GW + ND * EXPERTS] = chunks(g["L1_ffn_gate_weight"].T).reshape(P, -1)
    gate = np.concatenate([g["L1_ffn_gate_w"].reshape(-1, D), g["L1_ffn_sh_gate_w"]], 0).T
    up = np.concatenate([g["L1_ffn_up_w"].reshape(-1, D), g["L1_ffn_sh_up_w"]], 0).T
    down = np.concatenate([g["L1_ffn_down_w"].transpose(0, 2, 1).reshape(-1, D), g["L1_ffn_sh_down_w"].T,
                           np.zeros((NF_MOE * P - F_MOE, D), np.float32)], 0)
    flat = lambda a: np.ascontiguousarray(a).reshape(P, -1)
    return {
        "x": chunks(x),
        "xT": chunks(x.T),
        "cst": cst,
        "sel": expert_selector(),
        "rope": rope_tables(),
        "w_att0": flat(chunks(np.concatenate([g["L0_attn_w_project"].T, g["L0_attn_w_out"].T], 1))),
        "w_watt": flat(chunks(np.concatenate([wq, wqs, wk, wks, g["L1_attn_Wv"], g["L1_attn_Wo"]], 1))),
        "w_att2": flat(chunks(np.concatenate([g["L2_attn_w_qkv"], g["L2_attn_w_out"]], 1))),
        "w_att3": flat(chunks(np.concatenate([g[f"L3_attn_{k}"] for k in ("Wq", "Wk", "Wv", "Wo")], 1))),
        "glu_gu": flat(chunks(np.concatenate([g["L0_ffn_w_gate"], g["L0_ffn_w_up"]], 1))).view(np.int32),
        "glu_d": flat(chunks(g["L0_ffn_w_down"])).view(np.int32),
        "glu_sd": np.ascontiguousarray(g["L0_ffn_s_down"]),
        "moe_gu": flat(chunks(np.concatenate([gate, up], 1))),
        "moe_d": chunks(down),
        "bin_w": chunks(g["L2_ffn_weight"].T),
        "bin_b": np.ascontiguousarray(g["L2_ffn_bias"]),
        "tern_w": np.concatenate([flat(chunks(np.concatenate([g["L3_ffn_W_up"].T, g["L3_ffn_W_gate"].T], 1))),
                                  flat(chunks(g["L3_ffn_W_down"].T))], 1),
    }


def kernel(**inputs):
    import concourse.bacc as bacc
    from concourse.bass_utils import run_bass_kernel_spmd

    nc = bacc.Bacc("TRN2", target_bir_lowering=False, num_devices=1)
    arrays = arrange(inputs)
    t_in = {k: nc.dram_tensor("in_" + k, a.shape, mybir.dt.from_np(a.dtype), kind="ExternalInput").ap()
            for k, a in arrays.items()}
    out = nc.dram_tensor("out", (1, S, D), F32, kind="ExternalOutput").ap()
    build(nc, t_in, out)
    return run_bass_kernel_spmd(nc, [{"in_" + k: a for k, a in arrays.items()}], core_ids=[0]).results[0]["out"]
```

```python
from contextlib import ExitStack

import numpy as np
import concourse.bass as bass
from concourse import mybir

F32 = mybir.dt.float32
BF16 = mybir.dt.bfloat16
F32R = mybir.dt.float32r
I32 = mybir.dt.int32
I8 = mybir.dt.int8
ALU = mybir.AluOpType
ACT = mybir.ActivationFunctionType
AX = mybir.AxisListType

TOP_BITS = 12
TOP = -(1 << (24 - TOP_BITS))
P = 128
S = 1024
D = 256
NT = S // P
ND = D // P
HALF = 512
TH = HALF // P
NH, HD = 16, 16
HG = 4
NG = NH // HG
STRIP = 32
GROUPS = 6
Q_PARTS = (0, 0, 1, 0, 2, 1)
K_PARTS = (0, 1, 0, 2, 0, 1)
KROWS = GROUPS * HD
NEG = -1.0e30
LOWEST = -3.0e38
EPS = 1e-5
ONES_PAIR = float(np.array([0x3F803F80], np.uint32).view(np.float32)[0])
KV = 4
WIN = 64
EW = 6
WK = P + WIN
EXPERTS, F_EXP, F_SH = 8, 176, 352
F_MOE = EXPERTS * F_EXP + F_SH
NF_MOE = -(-F_MOE // P)
F = 1024
NF = F // P
NEXP1 = EXPERTS + 1

C_ID, C_MASK, C_MASKT, C_TRI = 0, 128, 256, 384
C_WMASK, C_WMASK0 = 512, 896
C_LOW8, C_LOW4, C_CNT, C_FLOOR, C_LAM = 1280, 1344, 1360, 1368, 1376
C_SG, C_SU, C_GW = 1392, 1400, 1408
C_ALL = 1424


def constants():
    c = np.zeros((P, C_ALL), np.float32)
    p = np.arange(P)[:, None]
    j = np.arange(P)[None, :]
    c[:, C_ID:C_ID + P] = p == j
    c[:, C_MASK:C_MASK + P] = np.where(j > p, NEG, 0)
    c[:, C_MASKT:C_MASKT + P] = np.where(p > j, NEG, 0)
    c[:, C_TRI:C_TRI + P] = p > j
    w = np.arange(WK)[None, :]
    seen = (w >= p + 1) & (w <= p + WIN)
    for at, ok in ((C_WMASK, seen), (C_WMASK0, seen & (w >= WIN))):
        m = np.where(ok, 0, NEG)
        c[:, at:at + WK] = m
        c[:, at + WK:at + 2 * WK] = m
    for at, n in ((C_LOW8, 8), (C_LOW4, 4)):
        c[:, at:at + n * n] = (np.arange(n)[None, :] < np.arange(n)[:, None]).reshape(1, -1)
    tok = np.arange(NT)[None, :] * P + p
    c[:, C_CNT:C_CNT + NT] = S - 1 - tok
    c[:, C_FLOOR:C_FLOOR + NT] = np.where(tok < S - 1, 0.0, LOWEST)
    return c


def expert_selector():
    f = np.arange(NF_MOE * P)
    owner = np.where(f < EXPERTS * F_EXP, f // F_EXP, EXPERTS)
    one = (owner[None, :] == np.arange(NEXP1)[:, None]) & (f < F_MOE)[None, :]
    return np.tile(one, (3, 1)).astype(np.float32)


def rope_tables():
    inv = (1.0 / 10000.0 ** (np.arange(0, HD, 2, dtype=np.float32) / np.float32(HD))).astype(np.float32)
    f = np.arange(S, dtype=np.float32)[None, :] * np.concatenate([inv, inv])[:, None]
    sign = np.where(np.arange(HD) < HD // 2, -1.0, 1.0)[:, None].astype(np.float32)
    t = np.stack([np.cos(f), np.sin(f) * sign], 1).astype(np.float32)
    return np.ascontiguousarray(np.tile(t, (P // HD, 1, 1)))


ATT, WATT, GLU, MOE, BIN, TERN = range(6)
SUBLAYERS = (ATT, GLU, WATT, MOE, ATT, BIN, ATT, TERN)
LAST_ATT = 6
E_EXP = NG * 12 * 2
E_USES = {ATT: E_EXP + 8, WATT: 6, GLU: 2 * NF + 4, MOE: 2 * NF_MOE + 4, BIN: 4, TERN: 2 * NF + 4}


def e_before(s):
    return sum(E_USES[k] for k in SUBLAYERS[:s])


def max_units(g):
    return [("max", g, t, c, j) for t in range(NT) for c in range(1 + (t >= TH)) for j in range(HG)]


OUT_STEPS = {3: [("outT",)], 4: [("proj", 0), ("proj", 1)], 5: [("proj", 2), ("proj", 3), ("norm",)], 7: [("new",)]}


def attention_plan():
    plan = max_units(0) + [("mT", 0)]
    before, due = None, []
    for g in range(NG):
        ahead = max_units(g + 1) if g + 1 < NG else []
        for i, (qh, kb) in enumerate((qh, kb) for qh in range(2) for kb in range(TH * (qh + 1))):
            plan += ahead[5 * i:5 * i + 5]
            if i == 10 and ahead:
                plan.append(("mT", g + 1))
            plan.append(("exp", g, qh, kb))
            due = [(n - 1, what) for n, what in due]
            while due and due[0][0] == 0:
                plan.append(due.pop(0)[1])
            if before:
                plan.append(("pv",) + before)
                if before[2] == TH * (before[1] + 1) - 1:
                    plan.append(("acc",) + before[:2])
                    due.append((2, ("accT",) + before[:2]))
            if g == NG - 1 and qh == 1 and kb in OUT_STEPS:
                plan += OUT_STEPS[kb]
            before = (g, qh, kb)
    plan += [what for _, what in due]
    plan += [("pv",) + before, ("acc",) + before[:2], ("accT",) + before[:2]]
    return plan


W_OUT_STEPS = {TH * (NG + 1) + i: what for i, what in
               enumerate([("outT",), ("proj", 0), ("proj", 1), ("proj", 2), ("proj", 3), ("norm",)])}


def windowed_plan():
    units, plan = NT * NH // 2, []
    for u in range(units):
        plan.append(("S", u))
        gi = (u - 5) // 2
        if u % 2 == 1 and gi >= 0:
            if gi and gi % NG == 0:
                plan += [("pv", gi // NG - 1), ("acc", gi // NG - 1)]
            plan.append(("uT", gi))
            if gi in W_OUT_STEPS:
                plan.append(W_OUT_STEPS[gi])
            if gi > NG and gi % NG == 1:
                plan.append(("accT", gi // NG - 1))
    last = NT - 1
    return plan + [("flush",), ("uT", NT * NG - 2), ("uT", NT * NG - 1), ("pv", last), ("acc", last), ("accT", last)]


PLAN = attention_plan()
W_PLAN = windowed_plan()
R_ATT = 4 * 2 + NT + NG * (len(max_units(0)) + 1) + NG * 2 + NT
R_GLU = 2 * NF + NT


def uses_of_r(gi):
    n = R_ATT + R_GLU + 3 * 2 * 2 + 2
    for item in W_PLAN:
        if item[0] in ("outT", "proj"):
            n += {"outT": ND, "proj": 1}[item[0]]
        if item[0] in ("uT", "accT"):
            n += 1 + (item[0] == "uT" and item[1] >= NG)
        if item == ("uT", gi):
            return n

STEP = {(g, qh, kb): g * 12 + TH * qh + kb for g in range(NG) for qh in range(2) for kb in range(TH * (qh + 1))}


def span(qh, kb):
    q0 = max(qh * HALF, kb * P)
    return q0, (qh + 1) * HALF - q0


def build(nc, t_in, out, subs=len(SUBLAYERS)):
    with ExitStack() as ctx:
        def sb(name, shape, dt=F32):
            return ctx.enter_context(nc.sbuf_tensor(name, shape, dt))

        def sem(name):
            return ctx.enter_context(nc.semaphore(name))

        with nc.sbuf_tensor("QO", [P, NH * S], BF16) as QO, \
                nc.sbuf_tensor("KO", [P, NH * S], BF16) as KO, \
                nc.sbuf_tensor("PB", [P, 2 * HG * HALF], F32) as PB, \
                nc.sbuf_tensor("parts", [P, 2, 3, S], BF16) as parts, \
                nc.sbuf_tensor("WF", [P, 2 * ND * F_MOE], F32) as WF:
            pass
        QO_r, KO_r = sb("QO_r", [P, NH * S // 2], F32R), sb("KO_r", [P, NH * S // 2], F32R)
        PB_r = sb("PB_r", [P, 2 * HG * HALF], F32R)
        parts_r = sb("parts_r", [P, 3 * S], F32R)
        WF_r = sb("WF_r", [P, 2 * ND * F_MOE], F32R)
        X = sb("X", [P, NT, D])
        xT = sb("xT", [P, ND, S])
        V = sb("V", [P, NT * NH, STRIP])
        rest = sb("rest", [P, 2, HALF])
        A = sb("A", [P, NT, D])
        acc = sb("acc", [P, 2, HALF])
        WA = [sb(f"WA{i}", [P, ND * 4 * D]) for i in range(2)]
        WB = sb("WB", [P, ND, D])
        biasB = sb("biasB", [P, D])
        sdown = sb("sdown", [P, D])
        cst = sb("cst", [P, C_ALL])
        idb = sb("idb", [P, P], BF16)
        maskb = sb("maskb", [P, 2, P], BF16)
        wmaskb = sb("wmaskb", [P, 2, 2 * WK], BF16)
        ones = sb("ones", [P, P])
        pmx = sb("pmx", [P, 2, 3, NT, HG])
        nm = sb("nm", [P, 2, NT, HG])
        nmr = sb("nmr", [P, NT, HG])
        mp = sb("mp", [P, 2, NT, 3, HG], BF16)
        mrow = sb("mrow", [3 * HG, 2, S], BF16)
        em = sb("em", [P, 2, NT, HG])
        rc = sb("rc", [P, 2, HALF // STRIP])
        stats = sb("stats", [P, NT, 6])
        mv = sb("mv", [P, NT, 2])
        lnv = sb("lnv", [P, 4, TH])
        wm = sb("wm", [P, 6, NT, EXPERTS])
        wmx = sb("wmx", [P, NT, NEXP1])
        wp = sb("wp", [P, NT, 3, NEXP1], BF16)
        tern = sb("tern", [P, 24])
        r12 = sb("r12", [P, NT, NH, 2])
        nm2 = sb("nm2", [P, 2, 4])
        cc = sb("cc", [P, 2, 3, HG])

        q_op = QO[:, :].rearrange("p (h n) -> p h n", h=NH)
        k_op = KO[:, :].rearrange("p (h n) -> p h n", h=NH)
        kw_op = KO[:, 0:KV * 2 * (WIN + S)].rearrange("p (h s n) -> p h s n", h=KV, s=2)
        hid = [t[:, :].bitcast(F32)[:, 0:NF_MOE * HALF].rearrange("p (f n) -> p f n", f=NF_MOE) for t in (QO, KO)]
        v_all = V[:, :, :].rearrange("p (t h) c -> p t h c", t=NT)
        pb = PB[:, :].rearrange("p (b h n) -> p b h n", b=2, h=HG)
        sg = PB[:, 0:4 * HALF].rearrange("p (b n) -> p b n", b=4)
        sgu = PB[:, 4 * HALF:6 * HALF].rearrange("p (b n) -> p b n", b=2)
        raw = PB[:, :].bitcast(I8)
        selF = A[0:3 * NEXP1, :, :].rearrange("p t n -> p (t n)")[:, 0:NF_MOE * P]
        selb = acc[0:3 * NEXP1, :, :].rearrange("p b n -> p (b n)").bitcast(BF16)[:, 0:NF_MOE * P]
        tt = cst[:, C_WMASK:C_WMASK + HALF]
        big = rest[:, 0, 0:D]
        carry = rest[:, 1, 0:D]
        rank = PB[:, 6 * HALF:8 * HALF].rearrange("p (b n) -> p b n", b=2)
        pf = parts[:, :, :, :].rearrange("p b k n -> p (b k n)").bitcast(F32)
        wsuf = pf[:, 0:NT * D].rearrange("p (t n) -> p t n", t=NT)
        spare = KO[:, KV * 2 * (WIN + S):].bitcast(F32)
        ew = [(spare[:, i * 4 * WK:(i + 1) * 4 * WK] if i < EW - 1 else pf[:, 0:4 * WK])
              .rearrange("p (k n) -> p k n", k=4) for i in range(EW)]
        uw = pf[:, 1536:1536 + 2 * 4 * WK].rearrange("p (b n) -> p b n", b=2)
        u_own, u_prev = uw[:, :, 0:HG * P], uw[:, :, HG * P:HG * WK]

        def e_head(gi, hh):
            return ew[(2 * gi + hh // 2) % EW][:, 2 * (hh % 2):2 * (hh % 2) + 2, :]

        def u_of(gi, hh):
            return ((u_prev[:, gi % 2, hh * WIN:(hh + 1) * WIN], slice(0, WIN)),
                    (u_own[:, gi % 2, hh * P:(hh + 1) * P], slice(WIN, WK)))

        uT = PB[:, :].rearrange("p (b k n) -> p b k n", b=4, k=2)
        rope = A[:, :, :].rearrange("p t n -> p (t n)").rearrange("p (k n) -> p k n", k=2)
        v_own = V[:, 0:NT * KV, :].rearrange("p (t h) c -> p t h c", t=NT)
        v_prev = [V[:, k * NT * KV:(k + 1) * NT * KV, :].rearrange("p (t h) c -> p t h c", t=NT) for k in (1, 2)]
        gu = WF[:, 0:2 * ND * F].rearrange("p (c k f) -> p c k f", c=ND, k=2)
        wd = WF[:, 2 * ND * F:2 * ND * F + NF * D].rearrange("p (f n) -> p f n", f=NF)
        gu_r = WF_r[:, 0:2 * ND * F].rearrange("p (c k f) -> p c k f", c=ND, k=2)
        wd_r = WF_r[:, 2 * ND * F:2 * ND * F + NF * D].rearrange("p (f n) -> p f n", f=NF)
        hid_k = [t[:, :].rearrange("p (k f n) -> p k f n", k=2, f=NF) for t in (QO_r, KO_r)]
        x_k = [[t.rearrange("p (k c n) -> p k c n", k=2, c=ND) for t in (a, b)]
               for a, b in ((pf[:, 0:2 * S], parts_r[:, 0:2 * S]), (PB[:, 2 * S:4 * S], PB_r[:, 2 * S:4 * S]))]
        gu_moe = WF[:, :].rearrange("p (c k f) -> p c k f", c=ND, k=2)
        wd_moe = V[:, :, :].rearrange("p s c -> p (s c)")[:, 0:NF_MOE * D].rearrange("p (f n) -> p f n", f=NF_MOE)
        wT = parts[:, 1, 0, :]
        idf = cst[:, C_ID:C_ID + P]

        def w_att(s, lo, n):
            w = {0: 0, 2: 1, 4: 0, 6: 1}[s]
            width = 4 * D if s != 2 else 960
            v = WA[w][:, 0:ND * width].rearrange("p (c n) -> p c n", c=ND)
            return v[:, :, lo:lo + n]

        bank = [ctx.enter_context(nc.psum_tensor(f"bank{i}", [P, HALF], F32)) for i in range(3)]
        pair = [ctx.enter_context(nc.psum_tensor(f"pair{i}", [P, 2, HALF], F32)) for i in range(2)]
        pvb = ctx.enter_context(nc.psum_tensor("pvb", [P, HALF], F32))

        r_full, r_free = sem("r_full"), sem("r_free")
        e_full, e_free = sem("e_full"), sem("e_free")
        dve_step = sem("dve_step")
        pool_step = sem("pool_step")
        ld_sel = sem("ld_sel")
        ld_x, ld_glu = sem("ld_x"), sem("ld_glu")
        ld_watt, ld_rope, ld_moe, ld_moed = sem("ld_watt"), sem("ld_rope"), sem("ld_moe"), sem("ld_moed")
        ld_att2, ld_bin, ld_att3, ld_tern = sem("ld_att2"), sem("ld_bin"), sem("ld_att3"), sem("ld_tern")
        cast_ready = sem("cast_ready")
        glu_ready = sem("glu_ready")
        v_blank = sem("v_blank")
        k_ones = sem("k_ones")
        parts_ready = sem("parts_ready")
        scr_written = sem("scr_written")
        rep_a, rep_b = sem("rep_a"), sem("rep_b")
        mp_ready = sem("mp_ready")
        mrow_ready = sem("mrow_ready")
        m_in = [sem("m_in0"), sem("m_in1")]
        pv_done = sem("pv_done")
        acc_ready = sem("acc_ready")
        em_ready = sem("em_ready")
        xn_ready = sem("xn_ready")
        wm_ready = sem("wm_ready")
        logit_max = sem("logit_max")
        logit_exp = sem("logit_exp")
        wmax_ready = sem("wmax_ready")
        u_ready = sem("u_ready")
        u0_ready = sem("u0_ready")
        w_full, w_free = sem("w_full"), sem("w_free")
        ratio_ready = sem("ratio_ready")
        bin_ready = sem("bin_ready")
        abs_ready = sem("abs_ready")
        tern_scale = sem("tern_scale")
        tern_ready = sem("tern_ready")
        x_first, x_rest = sem("x_first"), sem("x_rest")
        h_first, h_last = sem("h_first"), sem("h_last")
        h_typed = sem("h_typed")
        stored = sem("stored")

        scratch = nc.dram_tensor("scratch", [4 * 4, P, 3, S], BF16, kind="Internal").ap()
        x_out = out.rearrange("b (t p) n -> p (b t) n", p=P)

        ATTS = [s for s in range(subs) if SUBLAYERS[s] == ATT]

        def a_of(s):
            return {0: 0, 4: 1, 6: 2}[s]

        REP = {0: (12, 12), 2: (12 + 36, 12), 4: (60, 24), 6: (72, 36)}
        PARTS0 = {0: 0, 2: 4, 4: 7, 6: 11}
        ACC0 = {0: 0, 2: 8, 4: 16, 6: 24}
        PV0 = {0: 0, 2: 48, 4: 56, 6: 104}

        block = ctx.enter_context(nc.Block())

        @block.sync
        def _(sp):
            def load(dst, src, s):
                sp.dma_start(dst, src).then_inc(s, 16)

            load(xT[:, :, :], t_in["xT"], ld_x)
            load(WA[0][:, :], t_in["w_att0"], ld_x)
            load(cst[:, :], t_in["cst"], ld_x)
            load(X[:, :, :], t_in["x"], ld_x)
            load(raw[:, 0:ND * 2 * F].bitcast(I32), t_in["glu_gu"], ld_glu)
            load(raw[:, ND * 2 * F:ND * 2 * F + NF * D].bitcast(I32), t_in["glu_d"], ld_glu)
            load(sdown[:, :], t_in["glu_sd"].partition_broadcast(P), ld_glu)
            load(WA[1][:, 0:ND * 960], t_in["w_watt"], ld_watt)
            load(WB[:, :, :], t_in["bin_w"], ld_bin)
            load(biasB[:, :], t_in["bin_b"].partition_broadcast(P), ld_bin)

            n_scr = 0

            def replicate(s):
                nonlocal n_scr
                for tile in range(4):
                    n = PARTS0[s] + tile
                    sp.wait_ge(parts_ready, n + 1)
                    sp.dma_start(scratch[n], parts[:, n % 2, :, :]).then_inc(scr_written, 16)
                    sp.wait_ge(scr_written, 16 * (n + 1))
                    side, hi = tile % 2, tile // 2
                    dst = (q_op, k_op)[side]
                    for g in range(GROUPS):
                        part = (Q_PARTS, K_PARTS)[side][g]
                        src = scratch[n].rearrange("(h d) k n -> k d h n", d=HD)[part]
                        sp.dma_start(dst[g * HD:(g + 1) * HD, hi * 8:hi * 8 + 8, :], src)\
                            .then_inc((rep_a, rep_b)[hi], 16)

            def replicate_windowed(s):
                HS = HD // 2
                for tile in range(3):
                    n = PARTS0[s] + tile
                    sp.wait_ge(parts_ready, n + 1)
                    rows = P if tile < 2 else KV * HD
                    sp.dma_start(scratch[n][0:rows], parts[0:rows, n % 2, :, :]).then_inc(scr_written, 16)
                    sp.wait_ge(scr_written, 16 * (n + 1))
                    if tile == 2:
                        sp.wait_ge(k_ones, 2)
                    src = scratch[n][0:rows].rearrange("(h u d) k n -> u k d h n", u=2, d=HS)
                    for u in range(2):
                        for g in range(GROUPS):
                            r0 = u * GROUPS * HS + g * HS
                            if tile < 2:
                                dst = q_op[r0:r0 + HS, tile * 8:tile * 8 + 8, :]
                                part = Q_PARTS[g]
                            else:
                                dst = kw_op[r0:r0 + HS, :, u, WIN:WIN + S]
                                part = K_PARTS[g]
                            sp.dma_start(dst, src[u, part]).then_inc(rep_a, 16)

            def maxima(s):
                a = a_of(s)
                for g in range(NG):
                    n = NG * a + g
                    sp.wait_ge(mrow_ready, n + 1)
                    sp.dma_start(q_op[KROWS:KROWS + 3, g * HG:(g + 1) * HG, :], mrow[:, n % 2, :])\
                        .then_inc(m_in[n % 2], 16)

            for s in range(subs):
                if s == 1:
                    sp.wait_ge(xn_ready, NT)
                    load(rope, t_in["rope"], ld_rope)
                if s == 2:
                    sp.wait_ge(xn_ready, 2 * NT)
                    load(WF[:, :], t_in["moe_gu"], ld_moe)
                    load(WA[0][:, :], t_in["w_att2"], ld_att2)
                if s == 3:
                    sp.wait_ge(xn_ready, 3 * NT)
                    load(selF[:, :], t_in["sel"], ld_sel)
                    load(wd_moe, t_in["moe_d"], ld_moed)
                    load(WA[1][:, :], t_in["w_att3"], ld_att3)
                if s == 4:
                    sp.wait_ge(xn_ready, 4 * NT)
                    load(WF[:, 0:2 * ND * F + NF * D], t_in["tern_w"], ld_tern)
                if SUBLAYERS[s] == ATT:
                    replicate(s)
                    maxima(s)
                if SUBLAYERS[s] == WATT:
                    replicate_windowed(s)
            for half in range(2):
                sp.wait_ge(xn_ready, NT * (subs - 1) + TH * (half + 1))
                sl = slice(half * TH, (half + 1) * TH)
                sp.dma_start(x_out[:, sl, :], X[:, sl, :]).then_inc(stored, 16)
            sp.wait_ge(stored, 32)


        ternary_pieces = [(k, gu[:, c, k, lo:lo + HALF], gu_r[:, c, k, lo:lo + HALF])
                          for k in range(2) for c in range(ND) for lo in (0, HALF)] \
            + [(2, WF[:, lo:lo + HALF], WF_r[:, lo:lo + HALF])
               for lo in range(2 * ND * F, 2 * ND * F + NF * D, HALF)]

        @block.gpsimd
        def _(pool):
            steps = 0

            def step(ins):
                nonlocal steps
                steps += 1
                ins.then_inc(pool_step, 1)
                pool.wait_ge(pool_step, steps)

            def k_rows(n):
                pool.memset(KO[KROWS:KROWS + 3, :].bitcast(F32), ONES_PAIR).then_inc(k_ones, 1)
                pool.wait_ge(k_ones, n)

            def blank_v(n):
                step(pool.memset(V[:, :, :], 0.0))
                pool.memset(V[:, :, HD:HD + 1], 1.0).then_inc(v_blank, 1)
                pool.wait_ge(v_blank, n)

            k_rows(1)
            blank_v(1)
            pool.memset(ones[:, :], 1.0).then_inc(v_blank, 1)
            pool.wait_ge(v_blank, 2)
            if subs > 2:
                pool.wait_ge(xn_ready, 2 * NT)
                pool.memset(KO[:, 0:KV * 2 * (WIN + S)].bitcast(F32), 0.0).then_inc(k_ones, 1)
                pool.wait_ge(k_ones, 2)
                for gi in range(NT * NG):
                    pool.wait_ge(ratio_ready, gi + 1)
                    for hh in range(1, HG):
                        e2 = e_head(gi, hh)[:, 1, :]
                        last = pool.tensor_scalar(e2, e2, cc[:, gi % 2, 2, hh:hh + 1], 1.0,
                                                  ALU.mult, ALU.mult)
                    step(last)
                    if gi >= 2:
                        pool.wait_ge(r_full, uses_of_r(gi - 2))
                    for hh in range(1, HG):
                        for dst, cut in u_of(gi, hh):
                            last = pool.tensor_tensor(dst, e_head(gi, hh)[:, 1, cut], e_head(gi, hh)[:, 0, cut], ALU.subtract)
                    last.then_inc(u_ready, 1)
                    pool.wait_ge(u_ready, gi + 1)
            for s in range(4, subs):
                if SUBLAYERS[s] == ATT:
                    pool.wait_ge(xn_ready, NT * s)
                    k_rows(3 if s == 4 else 4)
                if s == 4:
                    blank_v(3)
                if s == 6:
                    pool.wait_ge(tern_scale, 1)
                    for k, w, w_r in ternary_pieces:
                        step(pool.tensor_scalar(tt[:, :], w, tern[:, 6 + k:7 + k], 1.0, ALU.is_gt, ALU.mult))
                        step(pool.tensor_scalar(w, w, tern[:, 9 + k:10 + k], 1.0, ALU.is_lt, ALU.mult))
                        step(pool.tensor_tensor(w_r, w, tt[:, :], ALU.subtract))
                    pool.memset(tt[:, 0:1], 0.0).then_inc(tern_ready, 1)

        @block.scalar
        def _(act):
            e_used = 0

            def e_slot():
                nonlocal e_used
                e_used += 1
                act.wait_ge(e_full, e_used)
                return pair[(e_used - 1) % 2]

            def copy_transposed(half):
                for c in range(ND):
                    ps = e_slot()
                    act.activation(xT[:, c, half * HALF:(half + 1) * HALF], ps[:, 0, :], ACT.Copy).then_inc(e_free, 1)

            def attention(s):
                scale = 1.0 / 32 if s == LAST_ATT else 0.25
                a = a_of(s)
                n_acc = ACC0[s]
                for item in PLAN:
                    if item[0] == "mT" and s == LAST_ATT:
                        g = item[1]
                        act.wait_ge(mp_ready, NG * a + g + 1)
                        act.activation(em[:, g % 2, :, :], nm[:, g % 2, :, :], ACT.Exp, scale=scale)\
                            .then_inc(em_ready, 1)
                    if item[0] == "exp":
                        _, g, qh, kb = item
                        st = STEP[item[1:]]
                        n = span(qh, kb)[1]
                        if st >= 2:
                            act.wait_ge(pv_done, PV0[s] + st - 1)
                        for i in range(2):
                            ps = e_slot()
                            act.activation(pb[:, st % 2, 2 * i:2 * i + 2, 0:n], ps[:, :, 0:n], ACT.Exp, scale=scale)\
                                .then_inc(e_free, 1)
                    if item[0] == "acc":
                        _, g, qh = item
                        act.wait_ge(pv_done, PV0[s] + STEP[g, qh, TH * (qh + 1) - 1] + 1)
                        act.activation(acc[:, n_acc % 2, :], pvb[:, :], ACT.Copy).then_inc(acc_ready, 1)
                        n_acc += 1
                    if item[0] in ("outT", "new"):
                        copy_transposed(0)
                for _ in ("outT", "new"):
                    copy_transposed(1)

            def windowed(s):
                n_acc = ACC0[s]
                for item in W_PLAN:
                    if item[0] == "S":
                        u = item[1]
                        t, p = divmod(u, NH // 2)
                        if u >= EW:
                            act.wait_ge(u_ready, (u - EW) // 2 + 1)
                            act.wait_ge(u0_ready, (u - EW) // 2 + 1)
                        for i in range(2):
                            act.wait_ge(wmax_ready, 2 * u + i + 1)
                            for z in range(2):
                                k = 2 * i + z
                                last = act.activation(ew[u % EW][:, k, :], pair[u % 2][:, i, z * WK:(z + 1) * WK],
                                                      ACT.Exp, bias=nm2[:, u % 2, k:k + 1],
                                                      accum_out=r12[:, t, 2 * p + i, z:z + 1])
                            last.then_inc(w_free, 1)
                    if item[0] == "acc":
                        act.wait_ge(pv_done, PV0[s] + item[1] + 1)
                        act.activation(acc[:, n_acc % 2, :], pvb[:, :], ACT.Copy).then_inc(acc_ready, 1)
                        n_acc += 1
                for half in (1, 0, 1):
                    copy_transposed(half)

            def ffn(nf, gate_scale, n_hid=None):
                def typed(i):
                    act.wait_ge(h_first, n_hid + i + 1)
                    act.activation(hid_k[i // nf][:, 0, i % nf, :], acc[:, i % 2, :], ACT.Copy).then_inc(h_typed, 1)

                for i in range(2 * nf):
                    fc = i % nf
                    rows = P if nf == NF or fc < nf - 1 else F_MOE - P * (nf - 1)
                    ps = e_slot()
                    act.activation(sg[0:rows, i % 4, :], ps[0:rows, 0, :], ACT.Silu, scale=gate_scale(fc))\
                        .then_inc(e_free, 1)
                    if n_hid is not None and fc:
                        typed(i - 1)
                        if fc == nf - 1:
                            typed(i)
                for half in range(2):
                    copy_transposed(half)

            act.wait_ge(ld_x, 16 * 4)
            act.activation(idb[:, :], idf, ACT.Copy).then_inc(cast_ready, 1)
            act.activation(maskb[:, :, :], cst[:, C_MASK:C_MASK + 2 * P].rearrange("p (k n) -> p k n", k=2), ACT.Copy)\
                .then_inc(cast_ready, 1)
            act.activation(wmaskb[:, :, :], cst[:, C_WMASK:C_WMASK + 4 * WK].rearrange("p (k n) -> p k n", k=2), ACT.Copy)\
                .then_inc(cast_ready, 1)
            act.wait_ge(ld_glu, 16 * 3)
            act.activation(WF_r[:, 0:2 * ND * F], raw[:, 0:2 * ND * F], ACT.Copy).then_inc(glu_ready, 1)
            act.wait_ge(glu_ready, 2)

            for s in range(subs):
                kind = SUBLAYERS[s]
                if kind == ATT:
                    attention(s)
                elif kind == WATT:
                    windowed(s)
                elif kind == GLU:
                    ffn(NF, lambda fc: cst[:, C_SG + fc:C_SG + fc + 1], 0)
                elif kind == MOE:
                    act.wait_ge(ld_sel, 16)
                    act.activation(selb[:, :], selF[:, :], ACT.Copy).then_inc(cast_ready, 1)
                    act.wait_ge(logit_max, 1)
                    act.activation(wm[:, 1, :, :], wm[:, 0, :, :], ACT.Exp).then_inc(logit_exp, 1)
                    ffn(NF_MOE, lambda fc: 1.0)
                elif kind == TERN:
                    ffn(NF, lambda fc: tern[:, 12:13], 2 * NF)
                else:
                    for half in range(2):
                        copy_transposed(half)

        @block.vector
        def _(dve):
            r_used = 0
            steps = 0

            def r_slot():
                nonlocal r_used
                r_used += 1
                dve.wait_ge(r_full, r_used)
                return bank[(r_used - 1) % 3]

            def r_done(ins):
                ins.then_inc(r_free, 1)

            def r_wait():
                dve.wait_ge(r_free, r_used)

            def step(ins):
                nonlocal steps
                steps += 1
                ins.then_inc(dve_step, 1)
                dve.wait_ge(dve_step, steps)

            def split(x, hi, mid, lo, tmp):
                step(dve.tensor_copy(hi, x))
                step(dve.tensor_tensor(tmp, x, hi, ALU.subtract))
                step(dve.tensor_copy(mid, tmp))
                return dve.tensor_tensor(lo, tmp, mid, ALU.subtract)

            def residual(s, t):
                if SUBLAYERS[s] == BIN:
                    step(dve.tensor_tensor(X[:, t, :], X[:, t, :], biasB[:, :], ALU.add))
                ps = r_slot()
                if SUBLAYERS[s] == GLU:
                    y = WF[:, 2 * ND * F + NF * D:][:, 0:D]
                    r_done(dve.tensor_tensor(y, ps[:, 0:D], sdown[:, :], ALU.mult))
                    r_wait()
                    step(dve.tensor_tensor(X[:, t, :], y, X[:, t, :], ALU.add))
                else:
                    r_done(dve.tensor_tensor(X[:, t, :], ps[:, 0:D], X[:, t, :], ALU.add))
                    r_wait()
                step(dve.bn_stats(stats[:, t, :], X[:, t, :]))

            def post(s, half):
                for t in range(half * TH, (half + 1) * TH):
                    residual(s, t)
                normalise(s, half)

            def normalise(s, half):
                t0 = half * TH
                for t in range(t0, t0 + TH):
                    last = dve.bn_aggr(mv[:, t, :], stats[:, t, :])
                step(last)
                v, y, w = lnv[:, 0, :], lnv[:, 1, :], lnv[:, 2, :]
                step(dve.tensor_scalar(v, mv[:, t0:t0 + TH, 1], EPS, None, ALU.add))
                step(dve.tensor_scalar(y.bitcast(I32), v.bitcast(I32), 1, None, ALU.logical_shift_right))
                step(dve.tensor_scalar(y.bitcast(I32), y.bitcast(I32), -1.0, float(0x5F3759DF), ALU.mult, ALU.add))
                for _ in range(3):
                    step(dve.scalar_tensor_tensor(w, y, -0.5, y, ALU.mult, ALU.mult))
                    step(dve.tensor_tensor(w, w, v, ALU.mult))
                    step(dve.scalar_tensor_tensor(y, w, 1.5, y, ALU.add, ALU.mult))
                for t in range(t0, t0 + TH):
                    dve.tensor_scalar(X[:, t, :], X[:, t, :], mv[:, t, 0:1], lnv[:, 1, t - t0:t - t0 + 1],
                                      ALU.subtract, ALU.mult).then_inc(xn_ready, 1)
                dve.wait_ge(xn_ready, NT * s + t0 + TH)

            def finish_parts(s, tile, half, x, rows, tmp):
                n = PARTS0[s] + tile
                if half == 0 and n >= 2:
                    dve.wait_ge(scr_written, 16 * (n - 1))
                hi, mid, lo = (parts[0:rows, n % 2, k, half * HALF:(half + 1) * HALF] for k in range(3))
                last = split(x, hi, mid, lo, tmp)
                if half == 0:
                    step(last)
                else:
                    last.then_inc(parts_ready, 1)
                    dve.wait_ge(parts_ready, n + 1)

            def attention(s):
                a = a_of(s)
                for tile in range(4):
                    for half in range(2):
                        ps = r_slot()
                        r_done(dve.tensor_copy(rest[:, 0, :], ps[:, :]))
                        r_wait()
                        finish_parts(s, tile, half, rest[:, 0, :], P, rest[:, 1, :])
                if s != 6:
                    dve.wait_ge(v_blank, {0: 2, 4: 3}[s])
                for t in range(NT):
                    ps = r_slot()
                    r_done(dve.tensor_copy(v_all[:, t, :, 0:HD], ps[:, 0:D].rearrange("p (h d) -> p h d", d=HD)))
                if s == LAST_ATT:
                    dve.wait_ge(scr_written, 16 * (PARTS0[s] + 4))
                    for t in reversed(range(NT)):
                        ps = r_slot()
                        if t == NT - 1:
                            step(dve.tensor_copy(wsuf[:, t, :], ps[:, 0:D]))
                            r_done(dve.tensor_copy(carry[:, :], ps[:, D:2 * D]))
                        else:
                            step(dve.tensor_tensor(wsuf[:, t, :], ps[:, 0:D], carry[:, :], ALU.add))
                            r_done(dve.tensor_tensor(carry[:, :], ps[:, D:2 * D], carry[:, :], ALU.add))
                        r_wait()
                    for b in range(2):
                        step(dve.tensor_copy(pmx[:, b, 2, :, :],
                                             cst[:, C_FLOOR:C_FLOOR + NT].unsqueeze(2).to_broadcast([P, NT, HG])))
                for item in PLAN:
                    if item[0] == "max":
                        _, g, t, c, j = item
                        n = min((t + 1) * P - c * HALF, HALF)
                        ps = r_slot()
                        r_done(dve.tensor_reduce(pmx[:, g % 2, c, t, j:j + 1], ps[:, 0:n], AX.X, ALU.max))
                    if item[0] == "mT":
                        g = item[1]
                        n = NG * a + g
                        b = g % 2
                        r_wait()
                        step(dve.tensor_reduce(nm[:, b, :, :], pmx[:, b, :, :, :].rearrange("p c t j -> p t j c"),
                                               AX.X, ALU.max, negate=True))
                        split(nm[:, b, :, :], mp[:, b, :, 0, :], mp[:, b, :, 1, :], mp[:, b, :, 2, :], nmr[:, :, :])\
                            .then_inc(mp_ready, 1)
                        ps = r_slot()
                        if n >= 2:
                            dve.wait_ge(m_in[n % 2], 16 * (n // 2))
                        dve.tensor_copy(mrow[:, n % 2, :], ps[0:3 * HG, :].bitcast(BF16)).then_inc(mrow_ready, 1)
                        dve.wait_ge(mrow_ready, n + 1)
                        dve.nop().then_inc(r_free, 1)
                    if item[0] == "accT":
                        _, g, qh = item
                        t0 = qh * TH
                        if s == LAST_ATT:
                            dve.wait_ge(em_ready, g + 1)
                        r_wait()
                        ps = r_slot()[:, :].rearrange("p (t h c) -> p t h c", t=TH, h=HG)
                        o = A[:, t0:t0 + TH, g * HG * HD:(g + 1) * HG * HD].rearrange("p t (h d) -> p t h d", d=HD)
                        den = rc[:, 0, :].rearrange("p (t h) -> p t h", h=HG)
                        inv = rc[:, 1, :].rearrange("p (t h) -> p t h", h=HG)
                        wide = inv.unsqueeze(3).to_broadcast([P, TH, HG, HD])
                        if s != LAST_ATT:
                            step(dve.reciprocal(inv, ps[:, :, :, HD]))
                            r_done(dve.tensor_tensor(o, ps[:, :, :, 0:HD], wide, ALU.mult))
                        else:
                            e = em[:, g % 2, t0:t0 + TH, :]
                            cnt = cst[:, C_CNT + t0:C_CNT + t0 + TH].unsqueeze(2).to_broadcast([P, TH, HG])
                            num = big[:, :].rearrange("p (t h d) -> p t h d", t=TH, h=HG)
                            w = wsuf[:, t0:t0 + TH, g * HG * HD:(g + 1) * HG * HD]\
                                .rearrange("p t (h d) -> p t h d", d=HD)
                            step(dve.tensor_tensor(den, e, cnt, ALU.mult))
                            step(dve.tensor_tensor(den, ps[:, :, :, HD], den, ALU.add))
                            step(dve.reciprocal(inv, den))
                            step(dve.tensor_tensor(num, w, e.unsqueeze(3).to_broadcast([P, TH, HG, HD]), ALU.mult))
                            step(dve.tensor_tensor(num, ps[:, :, :, 0:HD], num, ALU.add))
                            r_done(dve.tensor_tensor(o, num, wide, ALU.mult))
                    if item[0] == "proj":
                        residual(s, item[1])
                    if item[0] == "norm":
                        normalise(s, 0)
                post(s, 1)

            def windowed(s):
                dve.wait_ge(ld_rope, 16)
                for tile in range(3):
                    rows, sc = (P, (HD / 2) ** -0.5) if tile < 2 else (KV * HD, 1.0)
                    for half in range(2):
                        cols = slice(half * HALF, (half + 1) * HALF)
                        for k in range(2):
                            ps = r_slot()
                            r_done(dve.scalar_tensor_tensor(rest[0:rows, k, :], ps[0:rows, :], sc,
                                                            rope[0:rows, k, cols], ALU.mult, ALU.mult))
                        r_wait()
                        step(dve.tensor_tensor(rest[0:rows, 0, :], rest[0:rows, 0, :], rest[0:rows, 1, :], ALU.add))
                        finish_parts(s, tile, half, rest[0:rows, 0, :], rows, rest[0:rows, 1, :])
                step(dve.memset(V[WIN:P, NT * KV:2 * NT * KV, :], 0.0))
                step(dve.memset(V[0:WIN, 2 * NT * KV:3 * NT * KV, :], 0.0))
                ps = r_slot()
                vs = ps[:, :].rearrange("p (t h d) -> p t h d", t=NT, h=KV)
                step(dve.tensor_copy(v_prev[1][WIN:P, 1:NT, :, 0:HD], vs[WIN:P, 0:NT - 1]))
                r_done(dve.tensor_copy(v_own[:, :, :, 0:HD], vs))
                ps = r_slot()
                r_done(dve.tensor_copy(v_prev[0][0:WIN, 1:NT, :, 0:HD],
                                       ps[0:WIN, KV * HD:].rearrange("p (t h d) -> p t h d", t=NT - 1, h=KV)))

                def difference(gi):
                    t, g = divmod(gi, NG)
                    b = gi % 2
                    heads = slice(g * HG, (g + 1) * HG)
                    dve.wait_ge(w_free, HG * (gi + 1))
                    if gi >= 2:
                        dve.wait_ge(u_ready, gi - 1)
                        dve.wait_ge(r_full, uses_of_r(gi - 2))
                    step(dve.reciprocal(cc[:, b, 0, :], r12[:, t, heads, 1]))
                    step(dve.tensor_tensor(cc[:, b, 1, :], cc[:, b, 0, :], r12[:, t, heads, 0], ALU.mult))
                    dve.tensor_tensor(cc[:, b, 2, :], cc[:, b, 1, :], cst[:, C_LAM + g * HG:C_LAM + (g + 1) * HG], ALU.mult)\
                        .then_inc(ratio_ready, 1)
                    dve.wait_ge(ratio_ready, gi + 1)
                    for dst, cut in u_of(gi, 0):
                        last = dve.scalar_tensor_tensor(dst, e_head(gi, 0)[:, 1, cut], cc[:, b, 2, 0:1],
                                                        e_head(gi, 0)[:, 0, cut], ALU.mult, ALU.subtract)
                    last.then_inc(u0_ready, 1)

                for item in W_PLAN:
                    if item[0] == "S":
                        u = item[1]
                        for i in range(2):
                            dve.wait_ge(w_full, 2 * u + i + 1)
                            dve.tensor_reduce(nm2[:, u % 2, 2 * i:2 * i + 2],
                                              pair[u % 2][:, i, 0:2 * WK].rearrange("p (z n) -> p z n", z=2),
                                              AX.X, ALU.max, negate=True).then_inc(wmax_ready, 1)
                        if u % 2 == 0 and u >= 2:
                            difference(u // 2 - 1)
                    if item[0] == "flush":
                        difference(NT * NG - 1)
                    if item[0] == "uT":
                        gi = item[1]
                        for k in range(1 + (gi >= NG)):
                            n = (HALF, HALF // 2)[k]
                            ps = r_slot()
                            r_done(dve.tensor_scalar(uT[:, gi % NG, k, 0:n], ps[:, 0:n], -1.0, 0.0,
                                                     ALU.mult, ALU.max))
                    if item[0] == "accT":
                        t = item[1]
                        r_wait()
                        ps = r_slot()[:, :].rearrange("p (h g c) -> p h g c", h=HG, g=KV)
                        den = rc[:, 0, :].rearrange("p (h g) -> p h g", g=KV)
                        inv = rc[:, 1, :].rearrange("p (h g) -> p h g", g=KV)
                        r1 = r12[:, t, :, 0].rearrange("p (g h) -> p h g", g=KV)
                        o = A[:, t, :].rearrange("p (g h d) -> p h g d", g=KV, h=HG)
                        step(dve.scalar_tensor_tensor(den, r1, 1e-6, ps[:, :, :, HD], ALU.mult, ALU.add))
                        step(dve.reciprocal(inv, den))
                        r_done(dve.tensor_tensor(o, ps[:, :, :, 0:HD],
                                                 inv.unsqueeze(3).to_broadcast([P, HG, KV, HD]), ALU.mult))
                    if item[0] == "outT":
                        for c in range(ND):
                            r_done(dve.tensor_copy(xT[:, c, 0:HALF], r_slot()[:, :]))
                    if item[0] == "proj":
                        residual(s, item[1])
                    if item[0] == "norm":
                        normalise(s, 0)
                post(s, 1)

            def ranked(x, n, low, k):
                ge = rank[:, 0, 0:NT * n * n].rearrange("p (t i j) -> p t i j", t=NT, i=n)
                eq = rank[:, 1, 0:NT * n * n].rearrange("p (t i j) -> p t i j", t=NT, i=n)
                rival = x.unsqueeze(2).to_broadcast([P, NT, n, n])
                own = x.unsqueeze(3).to_broadcast([P, NT, n, n])
                lower = cst[:, low:low + n * n].rearrange("p (i j) -> p i j", i=n).unsqueeze(1)\
                    .to_broadcast([P, NT, n, n])
                step(dve.tensor_tensor(ge, rival, own, ALU.is_gt))
                step(dve.tensor_tensor(eq, rival, own, ALU.is_equal))
                step(dve.tensor_tensor(eq, eq, lower, ALU.mult))
                step(dve.tensor_tensor(ge, ge, eq, ALU.add))
                r = wm[:, k, :, 0:n]
                step(dve.tensor_reduce(r, ge, AX.X, ALU.add))
                step(dve.tensor_scalar(r, r, 2.0, None, ALU.is_lt))
                return r

            def route():
                ps = r_slot()[:, 0:NT * EXPERTS].rearrange("p (t e) -> p t e", t=NT)
                top = wm[:, 5, :, 0]
                step(dve.tensor_reduce(top, ps, AX.X, ALU.max))
                r_done(dve.tensor_tensor(wm[:, 0, :, :], ps, top.unsqueeze(2).to_broadcast([P, NT, EXPERTS]),
                                         ALU.subtract))
                r_wait()
                dve.nop().then_inc(logit_max, 1)
                dve.wait_ge(logit_exp, 1)
                step(dve.tensor_reduce(top, wm[:, 1, :, :], AX.X, ALU.add))
                step(dve.reciprocal(wm[:, 5, :, 1], top))
                step(dve.tensor_tensor(wm[:, 2, :, :], wm[:, 1, :, :],
                                       wm[:, 5, :, 1].unsqueeze(2).to_broadcast([P, NT, EXPERTS]), ALU.mult))
                step(dve.tensor_reduce(wm[:, 3, :, 0:4], wm[:, 2, :, :].rearrange("p t (g k) -> p t g k", g=4),
                                       AX.X, ALU.max))
                in_group = ranked(wm[:, 3, :, 0:4], 4, C_LOW4, 4)
                step(dve.tensor_tensor(wm[:, 1, :, :].rearrange("p t (g k) -> p t g k", g=4),
                                       wm[:, 2, :, :].rearrange("p t (g k) -> p t g k", g=4),
                                       in_group.unsqueeze(3).to_broadcast([P, NT, 4, 2]), ALU.mult))
                chosen = ranked(wm[:, 1, :, :], 8, C_LOW8, 4)
                step(dve.memset(wmx[:, :, EXPERTS:NEXP1], 1.0))
                step(dve.tensor_tensor(wmx[:, :, 0:EXPERTS], wm[:, 1, :, :], chosen, ALU.mult))
                tmp = rank[:, 0, 0:NT * NEXP1].rearrange("p (t e) -> p t e", t=NT)
                split(wmx[:, :, :], wp[:, :, 0, :], wp[:, :, 1, :], wp[:, :, 2, :], tmp).then_inc(wm_ready, 1)
                ps = r_slot()
                r_done(dve.tensor_copy(wT[0:3 * NEXP1, :], ps[0:3 * NEXP1, :].bitcast(BF16)))

            def short_ffn(s, up_scale):
                e0 = e_before(s)
                which = 0 if s == 1 else 1

                def split_x(half):
                    dve.wait_ge(e_free, e0 - ND * (1 - half))
                    n = 2 * which + half
                    f, fr = x_k[half]
                    x = xT[:, :, half * HALF:(half + 1) * HALF]
                    step(dve.tensor_scalar(f[:, 0].bitcast(I32), x.bitcast(I32), TOP, None, ALU.bitwise_and))
                    dve.tensor_tensor(fr[:, 1], x, f[:, 0], ALU.subtract).then_inc(x_rest, 1)
                    dve.wait_ge(x_rest, n + 1)
                    dve.tensor_copy(fr[:, 0], f[:, 0]).then_inc(x_first, 1)
                    dve.wait_ge(x_first, n + 1)

                def last_bits(i):
                    n = 2 * NF * which + i
                    dve.wait_ge(h_first, n + 1)
                    dve.tensor_tensor(hid_k[i // NF][:, 1, i % NF, :], rest[:, i % 2, :], acc[:, i % 2, :], ALU.subtract)\
                        .then_inc(h_last, 1)

                split_x(0)
                for half in range(2):
                    for fc in range(NF):
                        i = half * NF + fc
                        n = 2 * NF * which + i
                        ps = r_slot()
                        dve.wait_ge(e_free, e0 + i + 1)
                        if i >= 2:
                            dve.wait_ge(h_last, n - 1)
                        r_done(dve.scalar_tensor_tensor(rest[:, i % 2, :], ps[:, :], up_scale(fc), sg[:, i % 4, :],
                                                        ALU.mult, ALU.mult))
                        if fc:
                            last_bits(i - 1)
                        r_wait()
                        if i >= 2:
                            dve.wait_ge(h_typed, n - 1)
                        dve.tensor_scalar(acc[:, i % 2, :].bitcast(I32), rest[:, i % 2, :].bitcast(I32),
                                          TOP, None, ALU.bitwise_and).then_inc(h_first, 1)
                        if i == 2:
                            split_x(1)
                    last_bits(half * NF + NF - 1)
                    post(s, half)

            def ffn(s, nf):
                e0 = e_before(s)
                for half in range(2):
                    for fc in range(nf):
                        i = half * nf + fc
                        rows = P if fc < nf - 1 else F_MOE - P * (nf - 1)
                        ps = r_slot()
                        dve.wait_ge(e_free, e0 + i + 1)
                        r_done(dve.tensor_tensor(sgu[0:rows, i % 2, :], ps[0:rows, :], sg[0:rows, i % 4, :], ALU.mult))
                        r_wait()
                        ps = r_slot()
                        r_done(dve.tensor_tensor(hid[half][0:rows, fc, :], ps[0:rows, :], sgu[0:rows, i % 2, :],
                                                 ALU.mult))
                    post(s, half)

            dve.wait_ge(ld_glu, 16 * 3)
            dve.tensor_copy(WF_r[:, 2 * ND * F:2 * ND * F + NF * D], raw[:, 2 * ND * F:2 * ND * F + NF * D])\
                .then_inc(glu_ready, 1)
            step(dve.memset(pmx[:, :, :, :, :], LOWEST))
            for s in range(subs):
                kind = SUBLAYERS[s]
                if kind == ATT:
                    attention(s)
                elif kind == WATT:
                    windowed(s)
                elif kind == GLU:
                    short_ffn(s, lambda fc: cst[:, C_SU + fc:C_SU + fc + 1])
                elif kind == MOE:
                    route()
                    ffn(s, NF_MOE)
                elif kind == TERN:
                    short_ffn(s, lambda fc: tern[:, 13:14])
                else:
                    dve.wait_ge(ld_bin, 32)
                    dve.scalar_tensor_tensor(rest[:, :, 0:D], WB[:, :, :], -1.0, WB[:, :, :], ALU.mult, ALU.max)\
                        .then_inc(abs_ready, 1)
                    dve.wait_ge(abs_ready, 1)
                    step(dve.tensor_scalar(WB[:, :, :], WB[:, :, :], 0.0, 2.0, ALU.is_ge, ALU.mult))
                    step(dve.tensor_scalar(WB[:, :, :], WB[:, :, :], 1.0, None, ALU.subtract))
                    ps = r_slot()
                    r_done(dve.tensor_scalar(carry[:, :], ps[:, 0:D], 1.0 / D, None, ALU.mult))
                    r_wait()
                    dve.tensor_tensor(WB[:, :, :], WB[:, :, :], carry[:, :].unsqueeze(1).to_broadcast([P, ND, D]),
                                      ALU.mult).then_inc(bin_ready, 1)
                    if subs > 6:
                        dve.wait_ge(ld_tern, 16)
                        for k in range(2):
                            step(dve.tensor_reduce(tern[:, k:k + 1], gu[:, :, k, :], AX.XY, ALU.add,
                                                   apply_absolute_value=True))
                        dve.tensor_reduce(tern[:, 2:3], wd[:, :, :], AX.XY, ALU.add,
                                          apply_absolute_value=True).then_inc(abs_ready, 1)
                        ps = r_slot()
                        r_done(dve.tensor_scalar(tern[:, 3:6], ps[:, 0:3], 1.0 / (D * F), 1e-8, ALU.mult, ALU.add))
                        r_wait()
                        step(dve.tensor_scalar(tern[:, 6:9], tern[:, 3:6], 0.5, None, ALU.mult))
                        step(dve.tensor_scalar(tern[:, 9:12], tern[:, 3:6], -0.5, None, ALU.mult))
                        step(dve.tensor_scalar(tern[:, 12:13], tern[:, 3:4], -1.0, None, ALU.mult))
                        dve.tensor_tensor(tern[:, 13:14], tern[:, 4:5], tern[:, 5:6], ALU.mult).then_inc(tern_scale, 1)
                    for half in range(2):
                        post(s, half)

        @block.tensor
        def _(pe):
            r_used = 0
            e_used = 0
            x_at = [0, 0]

            def r_slot():
                nonlocal r_used
                r_used += 1
                if r_used > 3:
                    pe.wait_ge(r_free, r_used - 3)
                return bank[(r_used - 1) % 3]

            def e_slot():
                nonlocal e_used
                e_used += 1
                if e_used > 2:
                    pe.wait_ge(e_free, e_used - 2)
                return pair[(e_used - 1) % 2]

            def x_ready(half):
                if x_at[half]:
                    pe.wait_ge(e_free, x_at[half])

            def over_width(ps, w, x):
                for c in range(ND):
                    last = pe.matmul(ps, w(c), x(c), start=(c == 0), stop=(c == ND - 1))
                return last

            def transpose_tiles(ps, src, half, c):
                for tt_ in range(TH):
                    last = pe.transpose(ps[:, tt_ * P:(tt_ + 1) * P], src[:, half * TH + tt_, c * P:(c + 1) * P], idf)
                return last

            def transpose_half(src, half):
                for c in range(ND):
                    transpose_tiles(e_slot()[:, 0, :], src, half, c).then_inc(e_full, 1)

            def new_x(s, half):
                pe.wait_ge(xn_ready, NT * s + TH * (half + 1))
                transpose_half(X, half)
                x_at[half] = e_used

            def project_tile(t, w):
                ps = r_slot()
                over_width(ps[:, 0:D], lambda c: xT[:, c, t * P:(t + 1) * P], lambda c: w[:, c, :]).then_inc(r_full, 1)

            def project_out(s, half, w):
                for t in range(half * TH, (half + 1) * TH):
                    project_tile(t, w)

            def last_half_out(s, w, new_first):
                pe.wait_ge(r_free, r_used)
                transpose_half(A, 1)
                if new_first:
                    new_x(s, 0)
                pe.wait_ge(e_free, e_used)
                project_out(s, 1, w)
                new_x(s, 1)

            def attention(s):
                a = a_of(s)
                e_at = {}
                pe.wait_ge(*{0: (ld_x, 16 * 4), 4: (ld_att2, 16), 6: (ld_att3, 16)}[s])
                for tile in range(4):
                    side, hi = tile % 2, tile // 2
                    w = w_att(s, side * D + hi * P, P)
                    for half in range(2):
                        x_ready(half)
                        ps = r_slot()
                        over_width(ps[:, :], lambda c: w[:, c, :],
                                   lambda c: xT[:, c, half * HALF:(half + 1) * HALF]).then_inc(r_full, 1)
                w = w_att(s, 2 * D, D)
                for t in range(NT):
                    ps = r_slot()
                    over_width(ps[:, 0:D], lambda c: xT[:, c, t * P:(t + 1) * P], lambda c: w[:, c, :])\
                        .then_inc(r_full, 1)
                v_at = r_used
                if s == LAST_ATT:
                    pe.wait_ge(r_free, v_at)
                    pe.wait_ge(v_blank, 2)
                    for t in reversed(range(NT)):
                        ps = r_slot()
                        v = v_all[:, t, :, 0:HD]
                        pe.matmul(ps[:, 0:D], cst[:, C_TRI:C_TRI + P], v, start=True, stop=True)
                        pe.matmul(ps[:, D:2 * D], ones[:, :], v, start=True, stop=True).then_inc(r_full, 1)
                pe.wait_ge(cast_ready, 2)
                pe.wait_ge(k_ones, {0: 1, 4: 3, 6: 4}[s])
                for item in PLAN:
                    if item[0] == "max":
                        _, g, t, c, j = item
                        h = g * HG + j
                        if item == ("max", 0, 0, 0, 0):
                            pe.wait_ge(rep_a, 16 * REP[s][0])
                        if item == ("max", 2, 0, 0, 0):
                            pe.wait_ge(rep_b, 16 * REP[s][1])
                        n = min((t + 1) * P - c * HALF, HALF)
                        diag = (t + 1) * P - c * HALF <= HALF
                        ps = r_slot()
                        last = pe.matmul(ps[:, 0:n], q_op[0:KROWS, h, t * P:(t + 1) * P],
                                         k_op[0:KROWS, h, c * HALF:c * HALF + n], start=True, stop=not diag)
                        if diag:
                            last = pe.matmul(ps[:, n - P:n], idb[:, :], maskb[:, 0, :], start=False, stop=True)
                        last.then_inc(r_full, 1)
                    if item[0] == "mT":
                        g = item[1]
                        pe.wait_ge(mp_ready, NG * a + g + 1)
                        ps = r_slot()[0:3 * HG, :].bitcast(BF16)
                        for t in range(NT):
                            last = pe.transpose(ps[:, t * P:(t + 1) * P],
                                                mp[:, g % 2, t, :, :].rearrange("p k j -> p (k j)"), idb[:, :])
                        last.then_inc(r_full, 1)
                    if item[0] == "exp":
                        _, g, qh, kb = item
                        if (qh, kb) == (0, 0):
                            n = NG * a + g
                            pe.wait_ge(m_in[n % 2], 16 * (n // 2 + 1))
                        q0, n = span(qh, kb)
                        diag = kb * P >= qh * HALF
                        for i in range(2):
                            ps = e_slot()
                            for j in range(2):
                                h = g * HG + 2 * i + j
                                last = pe.matmul(ps[:, j, 0:n], k_op[0:KROWS + 3, h, kb * P:(kb + 1) * P],
                                                 q_op[0:KROWS + 3, h, q0:q0 + n], start=True, stop=not diag)
                                if diag:
                                    last = pe.matmul(ps[:, j, 0:P], idb[:, :], maskb[:, 1, :], start=False, stop=True)
                            last.then_inc(e_full, 1)
                        e_at[g, qh, kb] = e_used
                    if item[0] == "pv":
                        _, g, qh, kb = item
                        st = STEP[g, qh, kb]
                        q0, n = span(qh, kb)
                        if st == 0:
                            pe.wait_ge(r_free, v_at)
                        if kb == 0 and ACC0[s] + 2 * g + qh:
                            pe.wait_ge(acc_ready, ACC0[s] + 2 * g + qh)
                        pe.wait_ge(e_free, e_at[g, qh, kb])
                        for j in range(HG):
                            last = pe.matmul(pvb[j * STRIP:(j + 1) * STRIP, q0 - qh * HALF:HALF],
                                             v_all[:, kb, g * HG + j, :], pb[:, st % 2, j, 0:n],
                                             start=(kb == 0), stop=(kb == TH * (qh + 1) - 1))
                        last.then_inc(pv_done, 1)
                    if item[0] == "accT":
                        _, g, qh = item
                        n = ACC0[s] + 2 * g + qh
                        pe.wait_ge(acc_ready, n + 1)
                        ps = r_slot()
                        for tt_ in range(TH):
                            last = pe.transpose(ps[:, tt_ * P:(tt_ + 1) * P], acc[:, n % 2, tt_ * P:(tt_ + 1) * P], idf)
                        last.then_inc(r_full, 1)
                    if item[0] == "outT":
                        pe.wait_ge(r_free, r_used)
                        transpose_half(A, 0)
                    if item[0] == "proj":
                        pe.wait_ge(e_free, e_used)
                        project_tile(item[1], w_att(s, 3 * D, D))
                    if item[0] == "new":
                        new_x(s, 0)
                last_half_out(s, w_att(s, 3 * D, D), False)

            def windowed(s):
                assert e_used == e_before(s)
                pe.wait_ge(ld_watt, 16)
                for tile in range(3):
                    rows, at = ((P, (tile * P, D + tile * P)) if tile < 2 else (KV * HD, (2 * D, 2 * D + KV * HD)))
                    for half in range(2):
                        x_ready(half)
                        for k in range(2):
                            w = w_att(s, at[k], rows)
                            ps = r_slot()
                            over_width(ps[0:rows, :], lambda c: w[:, c, :],
                                       lambda c: xT[:, c, half * HALF:(half + 1) * HALF]).then_inc(r_full, 1)
                w = w_att(s, 2 * D + 2 * KV * HD, KV * HD)
                ps = r_slot()
                for t in range(NT):
                    last = over_width(ps[:, t * KV * HD:(t + 1) * KV * HD], lambda c: xT[:, c, t * P:(t + 1) * P],
                                      lambda c: w[:, c, :])
                last.then_inc(r_full, 1)
                ps = r_slot()
                for t in range(1, NT):
                    last = over_width(ps[0:WIN, t * KV * HD:(t + 1) * KV * HD],
                                      lambda c: xT[:, c, t * P - WIN:t * P], lambda c: w[:, c, :])
                last.then_inc(r_full, 1)
                v_at = r_used
                uT_at = {}
                pe.wait_ge(cast_ready, 3)
                pe.wait_ge(e_free, e_used)
                pe.wait_ge(rep_a, 16 * REP[s][0])
                for item in W_PLAN:
                    if item[0] == "S":
                        u = item[1]
                        t, p = divmod(u, NH // 2)
                        for i in range(2):
                            h = 2 * u + i
                            if h >= 4:
                                pe.wait_ge(w_free, h - 3)
                            for z in range(2):
                                o = pair[u % 2][:, i, z * WK:(z + 1) * WK]
                                pe.matmul(o, q_op[0:KROWS, 2 * p + i, t * P:(t + 1) * P],
                                          kw_op[0:KROWS, p // 2, z, t * P:t * P + WK], start=True, stop=False)
                                last = pe.matmul(o, idb[:, :], wmaskb[:, int(t == 0), 0:WK], start=False, stop=True)
                            last.then_inc(w_full, 1)
                    if item[0] == "uT":
                        gi = item[1]
                        pe.wait_ge(u_ready, gi + 1)
                        pe.wait_ge(u0_ready, gi + 1)
                        ps = r_slot()
                        for hh in range(HG):
                            last = pe.transpose(ps[:, hh * P:(hh + 1) * P], u_own[:, gi % 2, hh * P:(hh + 1) * P], idf)
                        last.then_inc(r_full, 1)
                        if gi >= NG:
                            ps = r_slot()
                            for k in range(2):
                                last = pe.transpose(ps[:, k * P:(k + 1) * P], u_prev[:, gi % 2, k * P:(k + 1) * P], idf)
                            last.then_inc(r_full, 1)
                        assert r_used == uses_of_r(gi)
                        uT_at[gi] = r_used
                    if item[0] == "pv":
                        t = item[1]
                        if t == 0:
                            pe.wait_ge(r_free, v_at)
                        pe.wait_ge(acc_ready, ACC0[s] + t)
                        pe.wait_ge(r_free, uT_at[NG * t + NG - 1])
                        for g in range(NG):
                            last = pe.matmul(pvb[g * STRIP:(g + 1) * STRIP, :], v_own[:, t, g, :], uT[:, g, 0, :],
                                             start=True, stop=(t == 0))
                        for k in range(2 if t else 0):
                            for g in range(NG):
                                o = pvb[g * STRIP:(g + 1) * STRIP, :].rearrange("p (j k q) -> p k j q", j=2, k=2)
                                last = pe.matmul(o[:, k], v_prev[k][:, t, g, :], uT[:, g, 1, 0:HALF // 2],
                                                 start=False, stop=(k == 1))
                        last.then_inc(pv_done, 1)
                    if item[0] == "accT":
                        t = item[1]
                        n = ACC0[s] + t
                        pe.wait_ge(acc_ready, n + 1)
                        ps = r_slot()
                        for hh in range(HG):
                            last = pe.transpose(ps[:, hh * P:(hh + 1) * P], acc[:, n % 2, hh * P:(hh + 1) * P], idf)
                        last.then_inc(r_full, 1)
                    if item[0] == "outT":
                        pe.wait_ge(r_free, r_used)
                        for c in range(ND):
                            transpose_tiles(r_slot(), A, 0, c).then_inc(r_full, 1)
                        outT_at = r_used
                    if item[0] == "proj":
                        pe.wait_ge(r_free, outT_at)
                        project_tile(item[1], w_att(s, 704, D))
                pe.wait_ge(w_free, NT * NH)
                last_half_out(s, w_att(s, 704, D), True)

            def short_ffn(s):
                which = 0 if s == 1 else 1
                assert e_used == e_before(s)
                pe.wait_ge(*((glu_ready, 2) if s == 1 else (tern_ready, 1)))

                def gate_up(half):
                    pe.wait_ge(x_rest, 2 * which + half + 1)
                    pe.wait_ge(x_first, 2 * which + half + 1)
                    for fc in range(NF):
                        for side in range(2):
                            ps = e_slot()[:, 0, :] if side == 0 else r_slot()[:, :]
                            for c in range(ND):
                                for k in range(2):
                                    last = pe.matmul(ps, gu_r[:, c, side, fc * P:(fc + 1) * P], x_k[half][1][:, k, c, :],
                                                     start=(c + k == 0), stop=(c + k == 2))
                            last.then_inc((e_full, r_full)[side], 1)

                def down(half):
                    n = NF * (2 * which + half + 1)
                    pe.wait_ge(h_last, n)
                    pe.wait_ge(h_typed, n)
                    for t in range(half * TH, (half + 1) * TH):
                        ps = r_slot()
                        at = (t - half * TH) * P
                        for fc in range(NF):
                            for k in range(2):
                                last = pe.matmul(ps[:, 0:D], hid_k[half][:, k, fc, at:at + P], wd_r[:, fc, :],
                                                 start=(fc + k == 0), stop=(fc + k == NF))
                        last.then_inc(r_full, 1)

                gate_up(0)
                down(0)
                gate_up(1)
                new_x(s, 0)
                down(1)
                new_x(s, 1)

            def ffn(s, nf, w_gu, w_d):
                assert e_used == e_before(s)
                moe = SUBLAYERS[s] == MOE
                if moe:
                    pe.wait_ge(ld_moe, 16)
                    ps = r_slot()
                    for t in range(NT):
                        x_ready(t // TH)
                        last = over_width(ps[:, t * EXPERTS:(t + 1) * EXPERTS], lambda c: xT[:, c, t * P:(t + 1) * P],
                                          lambda c: cst[:, C_GW + c * EXPERTS:C_GW + (c + 1) * EXPERTS])
                    last.then_inc(r_full, 1)
                    pe.wait_ge(wm_ready, 1)
                    ps = r_slot()[0:3 * NEXP1, :].bitcast(BF16)
                    for t in range(NT):
                        last = pe.transpose(ps[:, t * P:(t + 1) * P], wp[:, t, :, :].rearrange("p k e -> p (k e)"),
                                            idb[:, :])
                    last.then_inc(r_full, 1)
                    wT_at = r_used
                rows = [P] * nf
                if moe:
                    rows[-1] = F_MOE - P * (nf - 1)

                def gate_up(half):
                    x_ready(half)
                    xs = [xT[:, c, half * HALF:(half + 1) * HALF] for c in range(ND)]
                    for fc in range(nf):
                        n = rows[fc]
                        ps = e_slot()
                        over_width(ps[0:n, 0, :], lambda c: w_gu[:, c, 0, fc * P:fc * P + n], lambda c: xs[c])\
                            .then_inc(e_full, 1)
                        ps = r_slot()
                        over_width(ps[0:n, :], lambda c: w_gu[:, c, 1, fc * P:fc * P + n], lambda c: xs[c])\
                            .then_inc(r_full, 1)
                        if moe:
                            ps = r_slot()
                            if half == 0 and fc == 0:
                                pe.wait_ge(r_free, wT_at)
                                pe.wait_ge(cast_ready, 4)
                            pe.matmul(ps[0:n, :], selb[:, fc * P:fc * P + n],
                                      wT[0:3 * NEXP1, half * HALF:(half + 1) * HALF], start=True, stop=True)\
                                .then_inc(r_full, 1)
                    return r_used

                def down(half, h_at):
                    pe.wait_ge(r_free, h_at)
                    if moe and half == 0:
                        pe.wait_ge(ld_moed, 16)
                    for t in range(half * TH, (half + 1) * TH):
                        ps = r_slot()
                        at = (t - half * TH) * P
                        for fc in range(nf):
                            n = rows[fc]
                            last = pe.matmul(ps[:, 0:D], hid[half][0:n, fc, at:at + P], w_d[0:n, fc, :],
                                             start=(fc == 0), stop=(fc == nf - 1))
                        last.then_inc(r_full, 1)

                h_at = gate_up(0)
                down(0, h_at)
                h_at = gate_up(1)
                new_x(s, 0)
                down(1, h_at)
                new_x(s, 1)

            for s in range(subs):
                kind = SUBLAYERS[s]
                if kind == ATT:
                    attention(s)
                elif kind == WATT:
                    windowed(s)
                elif kind == GLU:
                    short_ffn(s)
                elif kind == MOE:
                    ffn(s, NF_MOE, gu_moe, wd_moe)
                elif kind == TERN:
                    short_ffn(s)
                else:
                    pe.wait_ge(v_blank, 2)
                    pe.wait_ge(abs_ready, 1)
                    ps = r_slot()
                    over_width(ps[:, 0:D], lambda c: ones[:, :], lambda c: rest[:, c, 0:D]).then_inc(r_full, 1)
                    if subs > 6:
                        pe.wait_ge(abs_ready, 2)
                        ps = r_slot()
                        pe.matmul(ps[:, 0:3], ones[:, :], tern[:, 0:3], start=True, stop=True).then_inc(r_full, 1)
                    pe.wait_ge(bin_ready, 1)
                    for half in range(2):
                        x_ready(half)
                        project_out(s, half, WB)
                    for half in range(2):
                        new_x(s, half)


def arrange(i):
    g = {k: np.asarray(v) for k, v in i.items()}

    def chunks(a):
        return np.ascontiguousarray(a.reshape(-1, P, a.shape[1]).transpose(1, 0, 2))

    x = g["L0_attn_x"].reshape(S, D)
    swap = (np.arange(HD) + HD // 2) % HD
    wq, wk = g["L1_attn_Wq"], g["L1_attn_Wk"]
    wqs = wq.reshape(D, NH, HD)[:, :, swap].reshape(D, NH * HD)
    wks = wk.reshape(D, KV, HD)[:, :, swap].reshape(D, KV * HD)
    cst = constants()
    cst[:, C_LAM:C_LAM + NH] = g["L1_attn_lam"][None, :]
    cst[:, C_SG:C_SG + NF] = g["L0_ffn_s_gate"].reshape(NF, P).T
    cst[:, C_SU:C_SU + NF] = g["L0_ffn_s_up"].reshape(NF, P).T
    cst[:, C_GW:C_GW + ND * EXPERTS] = chunks(g["L1_ffn_gate_weight"].T).reshape(P, -1)
    gate = np.concatenate([g["L1_ffn_gate_w"].reshape(-1, D), g["L1_ffn_sh_gate_w"]], 0).T
    up = np.concatenate([g["L1_ffn_up_w"].reshape(-1, D), g["L1_ffn_sh_up_w"]], 0).T
    down = np.concatenate([g["L1_ffn_down_w"].transpose(0, 2, 1).reshape(-1, D), g["L1_ffn_sh_down_w"].T,
                           np.zeros((NF_MOE * P - F_MOE, D), np.float32)], 0)
    flat = lambda a: np.ascontiguousarray(a).reshape(P, -1)
    return {
        "x": chunks(x),
        "xT": chunks(x.T),
        "cst": cst,
        "sel": expert_selector(),
        "rope": rope_tables(),
        "w_att0": flat(chunks(np.concatenate([g["L0_attn_w_project"].T, g["L0_attn_w_out"].T], 1))),
        "w_watt": flat(chunks(np.concatenate([wq, wqs, wk, wks, g["L1_attn_Wv"], g["L1_attn_Wo"]], 1))),
        "w_att2": flat(chunks(np.concatenate([g["L2_attn_w_qkv"], g["L2_attn_w_out"]], 1))),
        "w_att3": flat(chunks(np.concatenate([g[f"L3_attn_{k}"] for k in ("Wq", "Wk", "Wv", "Wo")], 1))),
        "glu_gu": flat(chunks(np.concatenate([g["L0_ffn_w_gate"], g["L0_ffn_w_up"]], 1))).view(np.int32),
        "glu_d": flat(chunks(g["L0_ffn_w_down"])).view(np.int32),
        "glu_sd": np.ascontiguousarray(g["L0_ffn_s_down"]),
        "moe_gu": flat(chunks(np.concatenate([gate, up], 1))),
        "moe_d": chunks(down),
        "bin_w": chunks(g["L2_ffn_weight"].T),
        "bin_b": np.ascontiguousarray(g["L2_ffn_bias"]),
        "tern_w": np.concatenate([flat(chunks(np.concatenate([g["L3_ffn_W_up"].T, g["L3_ffn_W_gate"].T], 1))),
                                  flat(chunks(g["L3_ffn_W_down"].T))], 1),
    }


def kernel(**inputs):
    import concourse.bacc as bacc
    from concourse.bass_utils import run_bass_kernel_spmd

    nc = bacc.Bacc("TRN2", target_bir_lowering=False, num_devices=1)
    arrays = arrange(inputs)
    t_in = {k: nc.dram_tensor("in_" + k, a.shape, mybir.dt.from_np(a.dtype), kind="ExternalInput").ap()
            for k, a in arrays.items()}
    out = nc.dram_tensor("out", (1, S, D), F32, kind="ExternalOutput").ap()
    build(nc, t_in, out)
    return run_bass_kernel_spmd(nc, [{"in_" + k: a for k, a in arrays.items()}], core_ids=[0]).results[0]["out"]
```

```python
from contextlib import ExitStack

import numpy as np
import concourse.bass as bass
from concourse import mybir

F32 = mybir.dt.float32
BF16 = mybir.dt.bfloat16
F32R = mybir.dt.float32r
I32 = mybir.dt.int32
I8 = mybir.dt.int8
ALU = mybir.AluOpType
ACT = mybir.ActivationFunctionType
AX = mybir.AxisListType

TOP_BITS = 12
TOP = -(1 << (24 - TOP_BITS))
P = 128
S = 1024
D = 256
NT = S // P
ND = D // P
HALF = 512
TH = HALF // P
NH, HD = 16, 16
HG = 4
NG = NH // HG
STRIP = 32
GROUPS = 6
Q_PARTS = (0, 0, 1, 0, 2, 1)
K_PARTS = (0, 1, 0, 2, 0, 1)
KROWS = GROUPS * HD
NEG = -1.0e30
LOWEST = -3.0e38
EPS = 1e-5
ONES_PAIR = float(np.array([0x3F803F80], np.uint32).view(np.float32)[0])
KV = 4
WIN = 64
EW = 6
WK = P + WIN
EXPERTS, F_EXP, F_SH = 8, 176, 352
F_MOE = EXPERTS * F_EXP + F_SH
NF_MOE = -(-F_MOE // P)
F = 1024
NF = F // P
NEXP1 = EXPERTS + 1

TILE_HALVES = [(0, 0), (1, 0), (0, 1), (1, 1), (2, 0), (2, 1), (3, 0), (3, 1)]

C_ID, C_MASK, C_MASKT, C_TRI = 0, 128, 256, 384
C_WMASK, C_WMASK0 = 512, 896
C_LOW8, C_LOW4, C_CNT, C_FLOOR, C_LAM = 1280, 1344, 1360, 1368, 1376
C_SG, C_SU, C_GW = 1392, 1400, 1408
C_ALL = 1424


def constants():
    c = np.zeros((P, C_ALL), np.float32)
    p = np.arange(P)[:, None]
    j = np.arange(P)[None, :]
    c[:, C_ID:C_ID + P] = p == j
    c[:, C_MASK:C_MASK + P] = np.where(j > p, NEG, 0)
    c[:, C_MASKT:C_MASKT + P] = np.where(p > j, NEG, 0)
    c[:, C_TRI:C_TRI + P] = p > j
    w = np.arange(WK)[None, :]
    seen = (w >= p + 1) & (w <= p + WIN)
    for at, ok in ((C_WMASK, seen), (C_WMASK0, seen & (w >= WIN))):
        m = np.where(ok, 0, NEG)
        c[:, at:at + WK] = m
        c[:, at + WK:at + 2 * WK] = m
    for at, n in ((C_LOW8, 8), (C_LOW4, 4)):
        c[:, at:at + n * n] = (np.arange(n)[None, :] < np.arange(n)[:, None]).reshape(1, -1)
    tok = np.arange(NT)[None, :] * P + p
    c[:, C_CNT:C_CNT + NT] = S - 1 - tok
    c[:, C_FLOOR:C_FLOOR + NT] = np.where(tok < S - 1, 0.0, LOWEST)
    return c


def expert_selector():
    f = np.arange(NF_MOE * P)
    owner = np.where(f < EXPERTS * F_EXP, f // F_EXP, EXPERTS)
    one = (owner[None, :] == np.arange(NEXP1)[:, None]) & (f < F_MOE)[None, :]
    return np.tile(one, (3, 1)).astype(np.float32)


def rope_tables():
    inv = (1.0 / 10000.0 ** (np.arange(0, HD, 2, dtype=np.float32) / np.float32(HD))).astype(np.float32)
    f = np.arange(S, dtype=np.float32)[None, :] * np.concatenate([inv, inv])[:, None]
    sign = np.where(np.arange(HD) < HD // 2, -1.0, 1.0)[:, None].astype(np.float32)
    t = np.stack([np.cos(f), np.sin(f) * sign], 1).astype(np.float32)
    return np.ascontiguousarray(np.tile(t, (P // HD, 1, 1)))


ATT, WATT, GLU, MOE, BIN, TERN = range(6)
SUBLAYERS = (ATT, GLU, WATT, MOE, ATT, BIN, ATT, TERN)
LAST_ATT = 6
LEAD = 2
E_EXP = NG * 12 * 2
E_USES = {ATT: 8 + E_EXP + 8, WATT: 6, GLU: 2 * NF + 4, MOE: 2 * NF_MOE + 4, BIN: 4, TERN: 2 * NF + 4}


def e_before(s):
    return sum(E_USES[k] for k in SUBLAYERS[:s]) - (ND if s else 0)


def e_chunk(s, i):
    return e_before(s) + i + 1 + (ND if s and i >= LEAD else 0)


OUT_STEPS = {3: [("outT",)], 4: [("proj", 0), ("proj", 1)], 5: [("proj", 2), ("proj", 3), ("norm",)], 7: [("new",)]}

STAGES = [(g, qh) for g in range(NG) for qh in range(2)]
DELAY, DELAY_FIRST = 2, 3
HEAD_START = 18
AHEAD = 2


def max_units(g, qh):
    units = [(("max", g, t, c, j), 60 + min((t + 1) * P - c * HALF, HALF))
             for t in range(qh * TH, (qh + 1) * TH) for c in range(1 + qh) for j in range(HG)]
    return units + [(("m", g, qh), 600)]


WEIGHT_STEPS = {0: (0, 1), 1: (2,), 2: (3,), 3: (4,), 5: (5,)}


def attention_plan():
    ahead = [(item, cost, n) for n, stage in enumerate(STAGES) for item, cost in max_units(*stage)]
    steps = [(g, qh, kb) for g, qh in STAGES for kb in range(TH * (qh + 1))]
    first = [steps.index(stage + (0,)) for stage in STAGES]
    plan, before, due, lead, found = [], None, [], 0.0, []

    def take():
        item, cost, _ = ahead.pop(0)
        plan.append(item)
        if item[0] == "m":
            found.append([DELAY, ("mT",) + item[1:]])
        return cost

    def transposes():
        for f in found:
            f[0] -= 1
        while found and found[0][0] <= 0:
            plan.append(found.pop(0)[1])

    while ahead[0][2] == 0:
        take()
    for n in range(HEAD_START):
        take()
        if n == DELAY_FIRST:
            plan.append(found.pop(0)[1])
    for k, (g, qh, kb) in enumerate(steps):
        rate = max([sum(c for _, c, n in ahead if n <= m) / max(1, first[m] - AHEAD - k)
                    for m in range(len(STAGES)) if ahead and m >= ahead[0][2]], default=0)
        for i in range(2):
            lead += rate / 2
            while ahead and lead > 0:
                lead -= take()
            if i == 0 and g == 0:
                plan += [("suffix", t) for t in (NT - 1 - 2 * k, NT - 2 - 2 * k) if t >= 0]
            plan.append(("exp", g, qh, kb, i))
            if (g, qh, i) == (NG - 1, 1, 1):
                plan += [("weights", n) for n in WEIGHT_STEPS.get(kb, ())]
            transposes()
        due = [(n - 1, what) for n, what in due]
        while due and due[0][0] == 0:
            plan.append(due.pop(0)[1])
        if before:
            plan.append(("pv",) + before)
            if before[2] == TH * (before[1] + 1) - 1:
                plan.append(("acc",) + before[:2])
                due.append((2, ("accT",) + before[:2]))
        if g == NG - 1 and qh == 1 and kb in OUT_STEPS:
            plan += OUT_STEPS[kb]
        before = (g, qh, kb)
    plan += [what for _, what in due]
    plan += [("pv",) + before, ("acc",) + before[:2], ("accT",) + before[:2]]
    return plan


W_TILES = (2, 0, 1)
W_HALVES = [(tile, half) for tile in W_TILES for half in range(2)]

W_OUT_STEPS = {TH * (NG + 1) + i: what for i, what in
               enumerate([("outT",), ("proj", 0), ("proj", 1), ("proj", 2), ("proj", 3), ("norm",)])}


def windowed_plan():
    units, plan = NT * NH // 2, []
    for u in range(units):
        plan.append(("S", u))
        gi = (u - 5) // 2
        if u % 2 == 1 and gi >= 0:
            if gi and gi % NG == 0:
                plan += [("pv", gi // NG - 1), ("acc", gi // NG - 1)]
            plan.append(("uT", gi))
            if gi in W_OUT_STEPS:
                plan.append(W_OUT_STEPS[gi])
            if gi > NG and gi % NG == 1:
                plan.append(("accT", gi // NG - 1))
    last = NT - 1
    return plan + [("flush",), ("uT", NT * NG - 2), ("uT", NT * NG - 1), ("pv", last), ("acc", last), ("accT", last)]


PLAN = attention_plan()
W_PLAN = windowed_plan()
R_ATT = NT + sum(item[0] in ("max", "mT", "accT", "proj") for item in PLAN) + TH
R_GLU = 2 * NF + NT


def uses_of_r(gi):
    n = R_ATT + R_GLU + 3 * 2 * 2 + 2
    for item in W_PLAN:
        if item[0] in ("outT", "proj"):
            n += {"outT": ND, "proj": 1}[item[0]]
        if item[0] in ("uT", "accT"):
            n += 1 + (item[0] == "uT" and item[1] >= NG)
        if item == ("uT", gi):
            return n

STEP = {(g, qh, kb): g * 12 + TH * qh + kb for g in range(NG) for qh in range(2) for kb in range(TH * (qh + 1))}


def span(qh, kb):
    q0 = max(qh * HALF, kb * P)
    return q0, (qh + 1) * HALF - q0


def build(nc, t_in, out):
    with ExitStack() as ctx:
        def sb(name, shape, dt=F32):
            return ctx.enter_context(nc.sbuf_tensor(name, shape, dt))

        def sem(name):
            return ctx.enter_context(nc.semaphore(name))

        with nc.sbuf_tensor("QO", [P, NH * S], BF16) as QO, \
                nc.sbuf_tensor("KO", [P, NH * S], BF16) as KO, \
                nc.sbuf_tensor("PB", [P, 2 * HG * HALF], F32) as PB, \
                nc.sbuf_tensor("parts", [P, 2, 3, S], BF16) as parts, \
                nc.sbuf_tensor("WF", [P, 2 * ND * F_MOE], F32) as WF:
            pass
        QO_r, KO_r = sb("QO_r", [P, NH * S // 2], F32R), sb("KO_r", [P, NH * S // 2], F32R)
        PB_r = sb("PB_r", [P, 2 * HG * HALF], F32R)
        parts_r = sb("parts_r", [P, 3 * S], F32R)
        WF_r = sb("WF_r", [P, 2 * ND * F_MOE], F32R)
        X = sb("X", [P, NT, D])
        xT = sb("xT", [P, ND, S])
        V = sb("V", [P, NT * NH, STRIP])
        rest = sb("rest", [P, 2, HALF])
        A = sb("A", [P, NT, D])
        acc = sb("acc", [P, 2, HALF])
        WA = [sb(f"WA{i}", [P, ND * 4 * D]) for i in range(2)]
        WB = sb("WB", [P, ND, D])
        biasB = sb("biasB", [P, D])
        sdown = sb("sdown", [P, D])
        cst = sb("cst", [P, C_ALL])
        idb = sb("idb", [P, P], BF16)
        maskb = sb("maskb", [P, 2, P], BF16)
        wmaskb = sb("wmaskb", [P, 2, 2 * WK], BF16)
        ones = sb("ones", [P, P])
        pmx = sb("pmx", [P, 2, 3, NT, HG])
        nm = sb("nm", [P, 2, NT, HG])
        nmr = sb("nmr", [P, NT, HG])
        mp = sb("mp", [P, 2, NT, 3, HG], BF16)
        mrow = sb("mrow", [3 * HG, 4, HALF], BF16)
        em = sb("em", [P, 2, NT, HG])
        rc = sb("rc", [P, 2, HALF // STRIP])
        stats = sb("stats", [P, NT, 6])
        mv = sb("mv", [P, NT, 2])
        lnv = sb("lnv", [P, 4, TH])
        wm = sb("wm", [P, 6, NT, EXPERTS])
        wmx = sb("wmx", [P, NT, NEXP1])
        wp = sb("wp", [P, NT, 3, NEXP1], BF16)
        tern = sb("tern", [P, 24])
        r12 = sb("r12", [P, NT, NH, 2])
        nm2 = sb("nm2", [P, 2, 4])
        cc = sb("cc", [P, 2, 3, HG])

        q_op = QO[:, :].rearrange("p (h n) -> p h n", h=NH)
        k_op = KO[:, :].rearrange("p (h n) -> p h n", h=NH)
        kw_op = KO[:, 0:KV * 2 * (WIN + S)].rearrange("p (h s n) -> p h s n", h=KV, s=2)
        hid = [t[:, :].bitcast(F32)[:, 0:NF_MOE * HALF].rearrange("p (f n) -> p f n", f=NF_MOE) for t in (QO, KO)]
        v_all = V[:, :, :].rearrange("p (t h) c -> p t h c", t=NT)
        pb = PB[:, :].rearrange("p (b h n) -> p b h n", b=2, h=HG)
        sg = PB[:, 0:4 * HALF].rearrange("p (b n) -> p b n", b=4)
        sgu = PB[:, 4 * HALF:7 * HALF].rearrange("p (b n) -> p b n", b=3)
        raw = PB[:, :].bitcast(I8)
        selF = A[0:3 * NEXP1, :, :].rearrange("p t n -> p (t n)")[:, 0:NF_MOE * P]
        selb = acc[0:3 * NEXP1, :, :].rearrange("p b n -> p (b n)").bitcast(BF16)[:, 0:NF_MOE * P]
        tt = cst[:, C_WMASK:C_WMASK + HALF]
        big = rest[:, 0, 0:D]
        carry = rest[:, 1, 0:D]
        rank = PB[:, 6 * HALF:8 * HALF].rearrange("p (b n) -> p b n", b=2)
        pf = parts[:, :, :, :].rearrange("p b k n -> p (b k n)").bitcast(F32)
        wsuf = pf[:, 0:NT * D].rearrange("p (t n) -> p t n", t=NT)
        spare = KO[:, KV * 2 * (WIN + S):].bitcast(F32)
        ew = [(spare[:, i * 4 * WK:(i + 1) * 4 * WK] if i < EW - 1 else pf[:, 0:4 * WK])
              .rearrange("p (k n) -> p k n", k=4) for i in range(EW)]
        uw = pf[:, 1536:1536 + 2 * 4 * WK].rearrange("p (b n) -> p b n", b=2)
        u_own, u_prev = uw[:, :, 0:HG * P], uw[:, :, HG * P:HG * WK]

        def e_head(gi, hh):
            return ew[(2 * gi + hh // 2) % EW][:, 2 * (hh % 2):2 * (hh % 2) + 2, :]

        def u_of(gi, hh):
            return ((u_prev[:, gi % 2, hh * WIN:(hh + 1) * WIN], slice(0, WIN)),
                    (u_own[:, gi % 2, hh * P:(hh + 1) * P], slice(WIN, WK)))

        uT = PB[:, :].rearrange("p (b k n) -> p b k n", b=4, k=2)
        rope = A[:, :, :].rearrange("p t n -> p (t n)").rearrange("p (k n) -> p k n", k=2)
        w_buf = (rest, acc, pb[:, 0, 0:2, :])
        v_own = V[:, 0:NT * KV, :].rearrange("p (t h) c -> p t h c", t=NT)
        v_prev = [V[:, k * NT * KV:(k + 1) * NT * KV, :].rearrange("p (t h) c -> p t h c", t=NT) for k in (1, 2)]
        gu = WF[:, 0:2 * ND * F].rearrange("p (c k f) -> p c k f", c=ND, k=2)
        wd = WF[:, 2 * ND * F:2 * ND * F + NF * D].rearrange("p (f n) -> p f n", f=NF)
        gu_r = WF_r[:, 0:2 * ND * F].rearrange("p (c k f) -> p c k f", c=ND, k=2)
        wd_r = WF_r[:, 2 * ND * F:2 * ND * F + NF * D].rearrange("p (f n) -> p f n", f=NF)
        hid_k = [t[:, :].rearrange("p (k f n) -> p k f n", k=2, f=NF) for t in (QO_r, KO_r)]
        x_k = [[t.rearrange("p (k c n) -> p k c n", k=2, c=ND) for t in (a, b)]
               for a, b in ((pf[:, 0:2 * S], parts_r[:, 0:2 * S]), (PB[:, 2 * S:4 * S], PB_r[:, 2 * S:4 * S]))]
        gu_moe = WF[:, :].rearrange("p (c k f) -> p c k f", c=ND, k=2)
        wd_moe = V[:, :, :].rearrange("p s c -> p (s c)")[:, 0:NF_MOE * D].rearrange("p (f n) -> p f n", f=NF_MOE)
        wT = parts[:, 1, 0, :]
        idf = cst[:, C_ID:C_ID + P]

        def w_att(s, lo, n):
            w = {0: 0, 2: 1, 4: 0, 6: 1}[s]
            width = 4 * D if s != 2 else 960
            v = WA[w][:, 0:ND * width].rearrange("p (c n) -> p c n", c=ND)
            return v[:, :, lo:lo + n]

        bank = [ctx.enter_context(nc.psum_tensor(f"bank{i}", [P, HALF], F32)) for i in range(3)]
        pair = [ctx.enter_context(nc.psum_tensor(f"pair{i}", [P, 2, HALF], F32)) for i in range(2)]
        pvb = ctx.enter_context(nc.psum_tensor("pvb", [P, HALF], F32))

        r_full, r_free = sem("r_full"), sem("r_free")
        e_full, e_free = sem("e_full"), sem("e_free")
        dve_step = sem("dve_step")
        pool_step = sem("pool_step")
        ld_sel = sem("ld_sel")
        ld_x1 = sem("ld_x1")
        ld_x, ld_cst, ld_res, ld_glu = sem("ld_x"), sem("ld_cst"), sem("ld_res"), sem("ld_glu")
        ld_watt, ld_rope, ld_moe, ld_moed = sem("ld_watt"), sem("ld_rope"), sem("ld_moe"), sem("ld_moed")
        ld_att2, ld_bin, ld_att3, ld_tern = sem("ld_att2"), sem("ld_bin"), sem("ld_att3"), sem("ld_tern")
        cast_ready = sem("cast_ready")
        glu_ready = sem("glu_ready")
        v_blank = sem("v_blank")
        k_ones = sem("k_ones")
        parts_ready = sem("parts_ready")
        rows_copied = sem("rows_copied")
        rows_split = sem("rows_split")
        scr_written = sem("scr_written")
        rep_a, rep_b = sem("rep_a"), sem("rep_b")
        mp_ready = sem("mp_ready")
        mrow_ready = sem("mrow_ready")
        m_in = [sem("m_in0"), sem("m_in1")]
        pv_done = sem("pv_done")
        acc_ready = sem("acc_ready")
        em_ready = sem("em_ready")
        xn_ready = sem("xn_ready")
        wm_ready = sem("wm_ready")
        logit_max = sem("logit_max")
        logit_exp = sem("logit_exp")
        wmax_ready = sem("wmax_ready")
        u_ready = sem("u_ready")
        u0_ready = sem("u0_ready")
        w_full, w_free = sem("w_full"), sem("w_free")
        w_rows = sem("w_rows")
        w_hi, w_mid, w_lo = sem("w_hi"), sem("w_mid"), sem("w_lo")
        w_blank = sem("w_blank")
        ratio_ready = sem("ratio_ready")
        bin_ready = sem("bin_ready")
        abs_ready = sem("abs_ready")
        tern_scale = sem("tern_scale")
        tern_ready = sem("tern_ready")
        x_first, x_rest = sem("x_first"), sem("x_rest")
        h_first, h_last = sem("h_first"), sem("h_last")
        h_typed = sem("h_typed")
        stored = sem("stored")

        scratch = nc.dram_tensor("scratch", [4 * 4, P, 3, S], BF16, kind="Internal").ap()
        x_out = out.rearrange("b (t p) n -> p (b t) n", p=P)

        def a_of(s):
            return {0: 0, 4: 1, 6: 2}[s]

        REP = {0: (12, 12), 2: (12 + 24, 12 + 12), 4: (48, 36), 6: (60, 48)}
        PARTS0 = {0: 0, 2: 4, 4: 7, 6: 11}
        ACC0 = {0: 0, 2: 8, 4: 16, 6: 24}
        PV0 = {0: 0, 2: 48, 4: 56, 6: 104}

        block = ctx.enter_context(nc.Block())

        @block.sync
        def _(sp):
            def load(dst, src, s):
                sp.dma_start(dst, src).then_inc(s, 16)

            load(xT[:, :, 0:HALF], t_in["xT"][:, :, 0:HALF], ld_x)
            load(WA[0][:, :], t_in["w_att0"], ld_x)
            load(xT[:, :, HALF:S], t_in["xT"][:, :, HALF:S], ld_x1)
            load(cst[:, :], t_in["cst"], ld_cst)
            load(X[:, :, :], t_in["x"], ld_res)
            load(raw[:, 0:ND * 2 * F].bitcast(I32), t_in["glu_gu"], ld_glu)
            load(raw[:, ND * 2 * F:ND * 2 * F + NF * D].bitcast(I32), t_in["glu_d"], ld_glu)
            load(sdown[:, :], t_in["glu_sd"].partition_broadcast(P), ld_glu)
            load(WA[1][:, 0:ND * 960], t_in["w_watt"], ld_watt)
            load(WB[:, :, :], t_in["bin_w"], ld_bin)
            load(biasB[:, :], t_in["bin_b"].partition_broadcast(P), ld_bin)

            n_scr = 0

            def replicate(s):
                nonlocal n_scr
                for hi in range(2):
                    for side in range(2):
                        n = PARTS0[s] + 2 * hi + side
                        sp.wait_ge(parts_ready, 4 * a_of(s) + 2 * hi + side + 1)
                        sp.dma_start(scratch[n], parts[:, n % 2, :, :]).then_inc(scr_written, 16)
                    for side in range(2):
                        n = PARTS0[s] + 2 * hi + side
                        sp.wait_ge(scr_written, 16 * (PARTS0[s] + 2 * hi + 2))
                        dst = (q_op, k_op)[side]
                        for g in range(GROUPS):
                            part = (Q_PARTS, K_PARTS)[side][g]
                            src = scratch[n].rearrange("(h d) k n -> k d h n", d=HD)[part]
                            sp.dma_start(dst[g * HD:(g + 1) * HD, hi * 8:hi * 8 + 8, :], src)\
                                .then_inc((rep_a, rep_b)[hi], 16)

            def replicate_windowed(s):
                HS = HD // 2
                for i, tile in enumerate(W_TILES):
                    n = PARTS0[s] + i
                    sp.wait_ge(w_lo, 2 * (i + 1))
                    rows = P if tile < 2 else KV * HD
                    sp.dma_start(scratch[n][0:rows], parts[0:rows, n % 2, :, :]).then_inc(scr_written, 16)
                    sp.wait_ge(scr_written, 16 * (n + 1))
                    if tile == 2:
                        sp.wait_ge(k_ones, 2)
                    src = scratch[n][0:rows].rearrange("(h u d) k n -> u k d h n", u=2, d=HS)
                    for u in range(2):
                        for g in range(GROUPS):
                            r0 = u * GROUPS * HS + g * HS
                            if tile < 2:
                                dst = q_op[r0:r0 + HS, tile * 8:tile * 8 + 8, :]
                                part = Q_PARTS[g]
                            else:
                                dst = kw_op[r0:r0 + HS, :, u, WIN:WIN + S]
                                part = K_PARTS[g]
                            sp.dma_start(dst, src[u, part]).then_inc(rep_b if tile == 1 else rep_a, 16)

            def maxima(s):
                a = a_of(s)
                for m, (g, qh) in enumerate(STAGES):
                    n = len(STAGES) * a + m
                    sp.wait_ge(mrow_ready, n + 1)
                    sp.dma_start(q_op[KROWS:KROWS + 3, g * HG:(g + 1) * HG, qh * HALF:(qh + 1) * HALF], mrow[:, n % 4, :])\
                        .then_inc(m_in[n % 2], 16)
                    if (s, m) == (4, 1):
                        load(WF[:, 0:2 * ND * F + NF * D], t_in["tern_w"], ld_tern)

            for s in range(len(SUBLAYERS)):
                if s == 1:
                    sp.wait_ge(xn_ready, NT)
                    load(rope, t_in["rope"], ld_rope)
                if s == 3:
                    sp.wait_ge(xn_ready, 3 * NT)
                    load(selF[:, :], t_in["sel"], ld_sel)
                    load(wd_moe, t_in["moe_d"], ld_moed)
                    load(WA[1][:, :], t_in["w_att3"], ld_att3)
                if SUBLAYERS[s] == ATT:
                    replicate(s)
                    maxima(s)
                if SUBLAYERS[s] == WATT:
                    replicate_windowed(s)
                    load(WF[:, :], t_in["moe_gu"], ld_moe)
                    load(WA[0][:, :], t_in["w_att2"], ld_att2)
            for half in range(2):
                sp.wait_ge(xn_ready, NT * (len(SUBLAYERS) - 1) + TH * (half + 1))
                sl = slice(half * TH, (half + 1) * TH)
                sp.dma_start(x_out[:, sl, :], X[:, sl, :]).then_inc(stored, 16)
            sp.wait_ge(stored, 32)


        ternary_pieces = [(k, gu[:, c, k, lo:lo + HALF], gu_r[:, c, k, lo:lo + HALF])
                          for k in range(2) for c in range(ND) for lo in (0, HALF)] \
            + [(2, WF[:, lo:lo + HALF], WF_r[:, lo:lo + HALF])
               for lo in range(2 * ND * F, 2 * ND * F + NF * D, HALF)]

        @block.gpsimd
        def _(pool):
            steps = 0

            def step(ins):
                nonlocal steps
                steps += 1
                ins.then_inc(pool_step, 1)
                pool.wait_ge(pool_step, steps)

            def k_rows(n):
                pool.memset(KO[KROWS:KROWS + 3, :].bitcast(F32), ONES_PAIR).then_inc(k_ones, 1)
                pool.wait_ge(k_ones, n)

            def blank_v(n):
                step(pool.memset(V[:, :, :], 0.0))
                pool.memset(V[:, :, HD:HD + 1], 1.0).then_inc(v_blank, 1)
                pool.wait_ge(v_blank, n)

            def last_bits(s):
                for i in range(2 * NF):
                    n = 2 * NF * int(s > 1) + i
                    pool.wait_ge(h_first, n + 1)
                    pool.tensor_tensor(hid_k[i // NF][:, 1, i % NF, :], rest[:, i % 2, :], acc[:, i % 2, :], ALU.subtract)\
                        .then_inc(h_last, 1)

            k_rows(1)
            blank_v(1)
            pool.memset(ones[:, :], 1.0).then_inc(v_blank, 1)
            pool.wait_ge(v_blank, 2)
            pool.wait_ge(ld_glu, 16 * 3)
            pool.tensor_copy(WF_r[:, 0:2 * ND * F], raw[:, 0:2 * ND * F]).then_inc(glu_ready, 1)
            last_bits(1)
            pool.wait_ge(xn_ready, 2 * NT)
            pool.memset(KO[:, 0:KV * 2 * (WIN + S)].bitcast(F32), 0.0).then_inc(k_ones, 1)
            pool.wait_ge(k_ones, 2)
            step(pool.memset(V[WIN:P, NT * KV:2 * NT * KV, :], 0.0))
            pool.memset(V[0:WIN, 2 * NT * KV:3 * NT * KV, :], 0.0).then_inc(w_blank, 1)
            for i, (tile, half) in enumerate(W_HALVES):
                n = PARTS0[2] + i // 2
                rows = P if tile < 2 else KV * HD
                cols = slice(half * HALF, (half + 1) * HALF)
                pool.wait_ge(w_mid, i + 1)
                pool.tensor_tensor(parts[0:rows, n % 2, 2, cols], w_buf[i % 3][0:rows, 1, :],
                                   parts[0:rows, n % 2, 1, cols], ALU.subtract).then_inc(w_lo, 1)
            for gi in range(NT * NG):
                pool.wait_ge(ratio_ready, gi + 1)
                for hh in range(1, HG):
                    e2 = e_head(gi, hh)[:, 1, :]
                    last = pool.tensor_scalar(e2, e2, cc[:, gi % 2, 2, hh:hh + 1], 1.0,
                                              ALU.mult, ALU.mult)
                step(last)
                if gi >= 2:
                    pool.wait_ge(r_full, uses_of_r(gi - 2))
                for hh in range(1, HG):
                    for dst, cut in u_of(gi, hh):
                        last = pool.tensor_tensor(dst, e_head(gi, hh)[:, 1, cut], e_head(gi, hh)[:, 0, cut], ALU.subtract)
                last.then_inc(u_ready, 1)
                pool.wait_ge(u_ready, gi + 1)
            for s in range(4, len(SUBLAYERS)):
                if s == 4:
                    pool.wait_ge(xn_ready, NT * s)
                    blank_v(3)
                    k_rows(3)
                if s == 6:
                    pool.wait_ge(tern_scale, 1)
                    for k, w, w_r in ternary_pieces:
                        step(pool.tensor_scalar(tt[:, :], w, tern[:, 6 + k:7 + k], 1.0, ALU.is_gt, ALU.mult))
                        step(pool.tensor_scalar(w, w, tern[:, 9 + k:10 + k], 1.0, ALU.is_lt, ALU.mult))
                        step(pool.tensor_tensor(w_r, w, tt[:, :], ALU.subtract))
                    pool.memset(tt[:, 0:1], 0.0).then_inc(tern_ready, 1)
                    last_bits(7)

        @block.scalar
        def _(act):
            e_used = 0

            def e_slot():
                nonlocal e_used
                e_used += 1
                act.wait_ge(e_full, e_used)
                return pair[(e_used - 1) % 2]

            def copy_transposed(half):
                for c in range(ND):
                    ps = e_slot()
                    act.activation(xT[:, c, half * HALF:(half + 1) * HALF], ps[:, 0, :], ACT.Copy).then_inc(e_free, 1)

            def cast_constants():
                act.wait_ge(ld_cst, 16)
                act.activation(idb[:, :], idf, ACT.Copy).then_inc(cast_ready, 1)
                act.activation(maskb[:, :, :], cst[:, C_MASK:C_MASK + 2 * P].rearrange("p (k n) -> p k n", k=2), ACT.Copy)\
                    .then_inc(cast_ready, 1)
                act.activation(wmaskb[:, :, :], cst[:, C_WMASK:C_WMASK + 4 * WK].rearrange("p (k n) -> p k n", k=2), ACT.Copy)\
                    .then_inc(cast_ready, 1)

            def attention(s):
                scale = 1.0 / 32 if s == LAST_ATT else 0.25
                a = a_of(s)
                n_acc = ACC0[s]
                for i, (tile, half) in enumerate(TILE_HALVES):
                    n = PARTS0[s] + tile
                    if s and i == LEAD:
                        copy_transposed(1)
                    ps = e_slot()
                    if i >= 2:
                        act.wait_ge(rows_split, 8 * a + i - 1)
                    act.activation(rest[:, i % 2, :], ps[:, 0, :], ACT.Copy).then_inc(rows_copied, 1)
                    if half == 0 and n >= 2:
                        act.wait_ge(scr_written, 16 * (PARTS0[s] + 2 * (tile // 2)))
                    act.activation(parts[:, n % 2, 0, half * HALF:(half + 1) * HALF], ps[:, 0, :], ACT.Copy)\
                        .then_inc(e_free, 1)
                if s == 0:
                    cast_constants()
                    act.wait_ge(glu_ready, 2)
                for item in PLAN:
                    if item[0] == "mT" and s == LAST_ATT:
                        _, g, qh = item
                        ts = slice(qh * TH, (qh + 1) * TH)
                        act.wait_ge(mp_ready, 2 * (NG * a + g) + qh + 1)
                        act.activation(em[:, g % 2, ts, :], nm[:, g % 2, ts, :], ACT.Exp, scale=scale)\
                            .then_inc(em_ready, 1)
                    if item[0] == "exp":
                        _, g, qh, kb, i = item
                        st = STEP[g, qh, kb]
                        n = span(qh, kb)[1]
                        if st >= 2 and i == 0:
                            act.wait_ge(pv_done, PV0[s] + st - 1)
                        ps = e_slot()
                        act.activation(pb[:, st % 2, 2 * i:2 * i + 2, 0:n], ps[:, :, 0:n], ACT.Exp, scale=scale)\
                            .then_inc(e_free, 1)
                    if item[0] == "acc":
                        _, g, qh = item
                        act.wait_ge(pv_done, PV0[s] + STEP[g, qh, TH * (qh + 1) - 1] + 1)
                        act.activation(acc[:, n_acc % 2, :], pvb[:, :], ACT.Copy).then_inc(acc_ready, 1)
                        n_acc += 1
                    if item[0] in ("outT", "new"):
                        copy_transposed(0)
                copy_transposed(1)

            def windowed(s):
                n_acc = ACC0[s]
                copy_transposed(1)
                for i, (tile, half) in enumerate(W_HALVES):
                    n = PARTS0[s] + i // 2
                    rows = P if tile < 2 else KV * HD
                    act.wait_ge(w_rows, i + 1)
                    if i == 4:
                        act.wait_ge(scr_written, 16 * (n - 1))
                    act.activation(parts[0:rows, n % 2, 0, half * HALF:(half + 1) * HALF], w_buf[i % 3][0:rows, 0, :],
                                   ACT.Copy).then_inc(w_hi, 1)
                for item in W_PLAN:
                    if item[0] == "S":
                        u = item[1]
                        t, p = divmod(u, NH // 2)
                        if u >= EW:
                            act.wait_ge(u_ready, (u - EW) // 2 + 1)
                            act.wait_ge(u0_ready, (u - EW) // 2 + 1)
                        for i in range(2):
                            act.wait_ge(wmax_ready, 2 * u + i + 1)
                            for z in range(2):
                                k = 2 * i + z
                                last = act.activation(ew[u % EW][:, k, :], pair[u % 2][:, i, z * WK:(z + 1) * WK],
                                                      ACT.Exp, bias=nm2[:, u % 2, k:k + 1],
                                                      accum_out=r12[:, t, 2 * p + i, z:z + 1])
                            last.then_inc(w_free, 1)
                    if item[0] == "acc":
                        act.wait_ge(pv_done, PV0[s] + item[1] + 1)
                        act.activation(acc[:, n_acc % 2, :], pvb[:, :], ACT.Copy).then_inc(acc_ready, 1)
                        n_acc += 1
                for half in (1, 0):
                    copy_transposed(half)

            def ffn(s, nf, gate_scale, n_hid=None):
                def typed(i):
                    act.wait_ge(h_first, n_hid + i + 1)
                    act.activation(hid_k[i // nf][:, 0, i % nf, :], acc[:, i % 2, :], ACT.Copy).then_inc(h_typed, 1)

                for i in range(2 * nf):
                    fc = i % nf
                    rows = P if nf == NF or fc < nf - 1 else F_MOE - P * (nf - 1)
                    ps = e_slot()
                    act.activation(sg[0:rows, i % 4, :], ps[0:rows, 0, :], ACT.Silu, scale=gate_scale(fc))\
                        .then_inc(e_free, 1)
                    if i == LEAD - 1:
                        copy_transposed(1)
                        if SUBLAYERS[s] == MOE:
                            act.wait_ge(logit_max, 1)
                            act.activation(wm[:, 1, :, :], wm[:, 0, :, :], ACT.Exp).then_inc(logit_exp, 1)
                            act.wait_ge(ld_sel, 16)
                            act.activation(selb[:, :], selF[:, :], ACT.Copy).then_inc(cast_ready, 1)
                    if n_hid is not None and fc:
                        typed(i - 1)
                        if fc == nf - 1:
                            typed(i)
                if s < len(SUBLAYERS) - 1:
                    copy_transposed(0)

            for s in range(len(SUBLAYERS)):
                kind = SUBLAYERS[s]
                if kind == ATT:
                    attention(s)
                elif kind == WATT:
                    windowed(s)
                elif kind == GLU:
                    ffn(s, NF, lambda fc: cst[:, C_SG + fc:C_SG + fc + 1], 0)
                elif kind == MOE:
                    ffn(s, NF_MOE, lambda fc: 1.0)
                elif kind == TERN:
                    ffn(s, NF, lambda fc: tern[:, 12:13], 2 * NF)
                else:
                    for half in (1, 0):
                        copy_transposed(half)

        @block.vector
        def _(dve):
            r_used = 0
            steps = 0

            def r_slot():
                nonlocal r_used
                r_used += 1
                dve.wait_ge(r_full, r_used)
                return bank[(r_used - 1) % 3]

            def r_done(ins):
                ins.then_inc(r_free, 1)

            def r_wait():
                dve.wait_ge(r_free, r_used)

            def step(ins):
                nonlocal steps
                steps += 1
                ins.then_inc(dve_step, 1)
                dve.wait_ge(dve_step, steps)

            def split(x, hi, mid, lo, tmp):
                step(dve.tensor_copy(hi, x))
                step(dve.tensor_tensor(tmp, x, hi, ALU.subtract))
                step(dve.tensor_copy(mid, tmp))
                return dve.tensor_tensor(lo, tmp, mid, ALU.subtract)

            def residual(s, t):
                if s == t == 0:
                    dve.wait_ge(ld_res, 16)
                ps = r_slot()
                if SUBLAYERS[s] == GLU:
                    y = WF[:, 2 * ND * F + NF * D:][:, 0:D]
                    r_done(dve.tensor_tensor(y, ps[:, 0:D], sdown[:, :], ALU.mult))
                    r_wait()
                    step(dve.tensor_tensor(X[:, t, :], y, X[:, t, :], ALU.add))
                else:
                    r_done(dve.tensor_tensor(X[:, t, :], ps[:, 0:D], X[:, t, :], ALU.add))
                    r_wait()
                if SUBLAYERS[s] == BIN:
                    step(dve.tensor_tensor(X[:, t, :], X[:, t, :], biasB[:, :], ALU.add))
                step(dve.bn_stats(stats[:, t, :], X[:, t, :]))

            def post(s, half):
                for t in range(half * TH, (half + 1) * TH):
                    residual(s, t)
                normalise(s, half)

            def normalise(s, half):
                t0 = half * TH
                for t in range(t0, t0 + TH):
                    last = dve.bn_aggr(mv[:, t, :], stats[:, t, :])
                step(last)
                v, y, w = lnv[:, 0, :], lnv[:, 1, :], lnv[:, 2, :]
                step(dve.tensor_scalar(v, mv[:, t0:t0 + TH, 1], EPS, None, ALU.add))
                step(dve.tensor_scalar(y.bitcast(I32), v.bitcast(I32), 1, None, ALU.logical_shift_right))
                step(dve.tensor_scalar(y.bitcast(I32), y.bitcast(I32), -1.0, float(0x5F3759DF), ALU.mult, ALU.add))
                for _ in range(3):
                    step(dve.scalar_tensor_tensor(w, y, -0.5, y, ALU.mult, ALU.mult))
                    step(dve.tensor_tensor(w, w, v, ALU.mult))
                    step(dve.scalar_tensor_tensor(y, w, 1.5, y, ALU.add, ALU.mult))
                for t in range(t0, t0 + TH):
                    dve.tensor_scalar(X[:, t, :], X[:, t, :], mv[:, t, 0:1], lnv[:, 1, t - t0:t - t0 + 1],
                                      ALU.subtract, ALU.mult).then_inc(xn_ready, 1)
                dve.wait_ge(xn_ready, NT * s + t0 + TH)

            def prepare_weights(n):
                if n == 0:
                    dve.wait_ge(ld_bin, 32)
                    dve.scalar_tensor_tensor(rest[:, :, 0:D], WB[:, :, :], -1.0, WB[:, :, :], ALU.mult, ALU.max)\
                        .then_inc(abs_ready, 1)
                    dve.wait_ge(abs_ready, 1)
                    step(dve.tensor_scalar(WB[:, :, :], WB[:, :, :], 0.0, 2.0, ALU.is_ge, ALU.mult))
                    step(dve.tensor_scalar(WB[:, :, :], WB[:, :, :], 1.0, None, ALU.subtract))
                if n == 1:
                    ps = r_slot()
                    r_done(dve.tensor_scalar(carry[:, :], ps[:, 0:D], 1.0 / D, None, ALU.mult))
                    r_wait()
                    dve.tensor_tensor(WB[:, :, :], WB[:, :, :], carry[:, :].unsqueeze(1).to_broadcast([P, ND, D]),
                                      ALU.mult).then_inc(bin_ready, 1)
                if n in (2, 3):
                    dve.wait_ge(ld_tern, 16)
                    step(dve.tensor_reduce(tern[:, n - 2:n - 1], gu[:, :, n - 2, :], AX.XY, ALU.add,
                                           apply_absolute_value=True))
                if n == 4:
                    dve.tensor_reduce(tern[:, 2:3], wd[:, :, :], AX.XY, ALU.add,
                                      apply_absolute_value=True).then_inc(abs_ready, 1)
                if n == 5:
                    ps = r_slot()
                    r_done(dve.tensor_scalar(tern[:, 3:6], ps[:, 0:3], 1.0 / (D * F), 1e-8, ALU.mult, ALU.add))
                    r_wait()
                    step(dve.tensor_scalar(tern[:, 6:9], tern[:, 3:6], 0.5, None, ALU.mult))
                    step(dve.tensor_scalar(tern[:, 9:12], tern[:, 3:6], -0.5, None, ALU.mult))
                    step(dve.tensor_scalar(tern[:, 12:13], tern[:, 3:4], -1.0, None, ALU.mult))
                    dve.tensor_tensor(tern[:, 13:14], tern[:, 4:5], tern[:, 5:6], ALU.mult).then_inc(tern_scale, 1)

            def copy_values(s):
                if s == 0:
                    dve.wait_ge(ld_glu, 16 * 3)
                    dve.tensor_copy(WF_r[:, 2 * ND * F:2 * ND * F + NF * D], raw[:, 2 * ND * F:2 * ND * F + NF * D])\
                        .then_inc(glu_ready, 1)
                if s != 6:
                    dve.wait_ge(v_blank, {0: 2, 4: 3}[s])
                for t in range(NT):
                    ps = r_slot()
                    r_done(dve.tensor_copy(v_all[:, t, :, 0:HD], ps[:, 0:D].rearrange("p (h d) -> p h d", d=HD)))

            def attention(s):
                a = a_of(s)
                for i, (tile, half) in enumerate(TILE_HALVES):
                    if i == TH:
                        copy_values(s)
                    n = PARTS0[s] + tile
                    dve.wait_ge(rows_copied, 8 * a + i + 1)
                    dve.wait_ge(e_free, e_chunk(s, i))
                    hi, mid, lo = (parts[:, n % 2, k, half * HALF:(half + 1) * HALF] for k in range(3))
                    tmp = rest[:, i % 2, :]
                    step(dve.tensor_tensor(tmp, tmp, hi, ALU.subtract))
                    step(dve.tensor_copy(mid, tmp))
                    dve.tensor_tensor(lo, tmp, mid, ALU.subtract).then_inc(rows_split, 1)
                    if half:
                        dve.wait_ge(rows_split, 8 * a + i + 1)
                        dve.nop().then_inc(parts_ready, 1)
                if s == LAST_ATT:
                    for b in range(2):
                        step(dve.tensor_copy(pmx[:, b, 2, :, :],
                                             cst[:, C_FLOOR:C_FLOOR + NT].unsqueeze(2).to_broadcast([P, NT, HG])))
                for item in PLAN:
                    if item[0] == "weights" and s == 4:
                        prepare_weights(item[1])
                    if item[0] == "suffix" and s == LAST_ATT:
                        t = item[1]
                        ps = r_slot()
                        if t == NT - 1:
                            dve.wait_ge(scr_written, 16 * (PARTS0[s] + 4))
                            step(dve.tensor_copy(wsuf[:, t, :], ps[:, 0:D]))
                            r_done(dve.tensor_copy(carry[:, :], ps[:, D:2 * D]))
                        else:
                            step(dve.tensor_tensor(wsuf[:, t, :], ps[:, 0:D], carry[:, :], ALU.add))
                            r_done(dve.tensor_tensor(carry[:, :], ps[:, D:2 * D], carry[:, :], ALU.add))
                        r_wait()
                    if item[0] == "max":
                        _, g, t, c, j = item
                        n = min((t + 1) * P - c * HALF, HALF)
                        ps = r_slot()
                        r_done(dve.tensor_reduce(pmx[:, g % 2, c, t, j:j + 1], ps[:, 0:n], AX.X, ALU.max))
                    if item[0] == "m":
                        _, g, qh = item
                        b = g % 2
                        ts = slice(qh * TH, (qh + 1) * TH)
                        r_wait()
                        step(dve.tensor_reduce(nm[:, b, ts, :], pmx[:, b, :, ts, :].rearrange("p c t j -> p t j c"),
                                               AX.X, ALU.max, negate=True))
                        split(nm[:, b, ts, :], mp[:, b, ts, 0, :], mp[:, b, ts, 1, :], mp[:, b, ts, 2, :],
                              nmr[:, ts, :]).then_inc(mp_ready, 1)
                    if item[0] == "mT":
                        _, g, qh = item
                        n = 2 * (NG * a + g) + qh
                        ps = r_slot()
                        if n >= 2:
                            dve.wait_ge(m_in[n % 2], 16 * (n // 2))
                        dve.tensor_copy(mrow[:, n % 4, :], ps[0:3 * HG, 0:HALF // 2].bitcast(BF16)).then_inc(mrow_ready, 1)
                        dve.wait_ge(mrow_ready, n + 1)
                        dve.nop().then_inc(r_free, 1)
                    if item[0] == "accT":
                        _, g, qh = item
                        t0 = qh * TH
                        if s == LAST_ATT:
                            dve.wait_ge(em_ready, 2 * g + qh + 1)
                        r_wait()
                        ps = r_slot()[:, :].rearrange("p (t h c) -> p t h c", t=TH, h=HG)
                        o = A[:, t0:t0 + TH, g * HG * HD:(g + 1) * HG * HD].rearrange("p t (h d) -> p t h d", d=HD)
                        den = rc[:, 0, :].rearrange("p (t h) -> p t h", h=HG)
                        inv = rc[:, 1, :].rearrange("p (t h) -> p t h", h=HG)
                        wide = inv.unsqueeze(3).to_broadcast([P, TH, HG, HD])
                        if s != LAST_ATT:
                            step(dve.reciprocal(inv, ps[:, :, :, HD]))
                            r_done(dve.tensor_tensor(o, ps[:, :, :, 0:HD], wide, ALU.mult))
                        else:
                            e = em[:, g % 2, t0:t0 + TH, :]
                            cnt = cst[:, C_CNT + t0:C_CNT + t0 + TH].unsqueeze(2).to_broadcast([P, TH, HG])
                            num = big[:, :].rearrange("p (t h d) -> p t h d", t=TH, h=HG)
                            w = wsuf[:, t0:t0 + TH, g * HG * HD:(g + 1) * HG * HD]\
                                .rearrange("p t (h d) -> p t h d", d=HD)
                            step(dve.tensor_tensor(den, e, cnt, ALU.mult))
                            step(dve.tensor_tensor(den, ps[:, :, :, HD], den, ALU.add))
                            step(dve.reciprocal(inv, den))
                            step(dve.tensor_tensor(num, w, e.unsqueeze(3).to_broadcast([P, TH, HG, HD]), ALU.mult))
                            step(dve.tensor_tensor(num, ps[:, :, :, 0:HD], num, ALU.add))
                            r_done(dve.tensor_tensor(o, num, wide, ALU.mult))
                    if item[0] == "proj":
                        residual(s, item[1])
                    if item[0] == "norm":
                        normalise(s, 0)
                if SUBLAYERS[s + 1] in (GLU, TERN):
                    split_x(s + 1, 0)
                post(s, 1)

            def windowed(s):
                dve.wait_ge(ld_rope, 16)
                def middle(i):
                    tile, half = W_HALVES[i]
                    n = PARTS0[s] + i // 2
                    rows = P if tile < 2 else KV * HD
                    cols = slice(half * HALF, (half + 1) * HALF)
                    dve.wait_ge(w_hi, i + 1)
                    x, left = (w_buf[i % 3][0:rows, k, :] for k in range(2))
                    step(dve.tensor_tensor(left, x, parts[0:rows, n % 2, 0, cols], ALU.subtract))
                    dve.tensor_copy(parts[0:rows, n % 2, 1, cols], left).then_inc(w_mid, 1)

                for i, (tile, half) in enumerate(W_HALVES):
                    rows, sc = (P, (HD / 2) ** -0.5) if tile < 2 else (KV * HD, 1.0)
                    cols = slice(half * HALF, (half + 1) * HALF)
                    x = w_buf[i % 3]
                    if i >= 3:
                        dve.wait_ge(w_lo, i - 2)
                    for k in range(2):
                        ps = r_slot()
                        r_done(dve.scalar_tensor_tensor(x[0:rows, k, :], ps[0:rows, :], sc, rope[0:rows, k, cols],
                                                        ALU.mult, ALU.mult))
                    r_wait()
                    dve.tensor_tensor(x[0:rows, 0, :], x[0:rows, 0, :], x[0:rows, 1, :], ALU.add).then_inc(w_rows, 1)
                    if i:
                        middle(i - 1)
                    dve.wait_ge(w_rows, i + 1)
                middle(len(W_HALVES) - 1)
                dve.wait_ge(w_blank, 1)
                ps = r_slot()
                vs = ps[:, :].rearrange("p (t h d) -> p t h d", t=NT, h=KV)
                step(dve.tensor_copy(v_prev[1][WIN:P, 1:NT, :, 0:HD], vs[WIN:P, 0:NT - 1]))
                r_done(dve.tensor_copy(v_own[:, :, :, 0:HD], vs))
                ps = r_slot()
                r_done(dve.tensor_copy(v_prev[0][0:WIN, 1:NT, :, 0:HD],
                                       ps[0:WIN, KV * HD:].rearrange("p (t h d) -> p t h d", t=NT - 1, h=KV)))

                def difference(gi):
                    t, g = divmod(gi, NG)
                    b = gi % 2
                    heads = slice(g * HG, (g + 1) * HG)
                    dve.wait_ge(w_free, HG * (gi + 1))
                    if gi >= 2:
                        dve.wait_ge(u_ready, gi - 1)
                        dve.wait_ge(r_full, uses_of_r(gi - 2))
                    step(dve.reciprocal(cc[:, b, 0, :], r12[:, t, heads, 1]))
                    step(dve.tensor_tensor(cc[:, b, 1, :], cc[:, b, 0, :], r12[:, t, heads, 0], ALU.mult))
                    dve.tensor_tensor(cc[:, b, 2, :], cc[:, b, 1, :], cst[:, C_LAM + g * HG:C_LAM + (g + 1) * HG], ALU.mult)\
                        .then_inc(ratio_ready, 1)
                    dve.wait_ge(ratio_ready, gi + 1)
                    for dst, cut in u_of(gi, 0):
                        last = dve.scalar_tensor_tensor(dst, e_head(gi, 0)[:, 1, cut], cc[:, b, 2, 0:1],
                                                        e_head(gi, 0)[:, 0, cut], ALU.mult, ALU.subtract)
                    last.then_inc(u0_ready, 1)

                for item in W_PLAN:
                    if item[0] == "S":
                        u = item[1]
                        for i in range(2):
                            dve.wait_ge(w_full, 2 * u + i + 1)
                            dve.tensor_reduce(nm2[:, u % 2, 2 * i:2 * i + 2],
                                              pair[u % 2][:, i, 0:2 * WK].rearrange("p (z n) -> p z n", z=2),
                                              AX.X, ALU.max, negate=True).then_inc(wmax_ready, 1)
                        if u % 2 == 0 and u >= 2:
                            difference(u // 2 - 1)
                    if item[0] == "flush":
                        difference(NT * NG - 1)
                    if item[0] == "uT":
                        gi = item[1]
                        for k in range(1 + (gi >= NG)):
                            n = (HALF, HALF // 2)[k]
                            ps = r_slot()
                            r_done(dve.tensor_scalar(uT[:, gi % NG, k, 0:n], ps[:, 0:n], -1.0, 0.0,
                                                     ALU.mult, ALU.max))
                    if item[0] == "accT":
                        t = item[1]
                        r_wait()
                        ps = r_slot()[:, :].rearrange("p (h g c) -> p h g c", h=HG, g=KV)
                        den = rc[:, 0, :].rearrange("p (h g) -> p h g", g=KV)
                        inv = rc[:, 1, :].rearrange("p (h g) -> p h g", g=KV)
                        r1 = r12[:, t, :, 0].rearrange("p (g h) -> p h g", g=KV)
                        o = A[:, t, :].rearrange("p (g h d) -> p h g d", g=KV, h=HG)
                        step(dve.scalar_tensor_tensor(den, r1, 1e-6, ps[:, :, :, HD], ALU.mult, ALU.add))
                        step(dve.reciprocal(inv, den))
                        r_done(dve.tensor_tensor(o, ps[:, :, :, 0:HD],
                                                 inv.unsqueeze(3).to_broadcast([P, HG, KV, HD]), ALU.mult))
                    if item[0] == "outT":
                        for c in range(ND):
                            r_done(dve.tensor_copy(xT[:, c, 0:HALF], r_slot()[:, :]))
                    if item[0] == "proj":
                        residual(s, item[1])
                    if item[0] == "norm":
                        normalise(s, 0)
                if SUBLAYERS[s + 1] in (GLU, TERN):
                    split_x(s + 1, 0)
                post(s, 1)

            def ranked(x, n, low, k):
                ge = rank[:, 0, 0:NT * n * n].rearrange("p (t i j) -> p t i j", t=NT, i=n)
                eq = rank[:, 1, 0:NT * n * n].rearrange("p (t i j) -> p t i j", t=NT, i=n)
                rival = x.unsqueeze(2).to_broadcast([P, NT, n, n])
                own = x.unsqueeze(3).to_broadcast([P, NT, n, n])
                lower = cst[:, low:low + n * n].rearrange("p (i j) -> p i j", i=n).unsqueeze(1)\
                    .to_broadcast([P, NT, n, n])
                step(dve.tensor_tensor(ge, rival, own, ALU.is_gt))
                step(dve.tensor_tensor(eq, rival, own, ALU.is_equal))
                step(dve.tensor_tensor(eq, eq, lower, ALU.mult))
                step(dve.tensor_tensor(ge, ge, eq, ALU.add))
                r = wm[:, k, :, 0:n]
                step(dve.tensor_reduce(r, ge, AX.X, ALU.add))
                step(dve.tensor_scalar(r, r, 2.0, None, ALU.is_lt))
                return r

            def route():
                ps = r_slot()[:, 0:NT * EXPERTS].rearrange("p (t e) -> p t e", t=NT)
                top = wm[:, 5, :, 0]
                step(dve.tensor_reduce(top, ps, AX.X, ALU.max))
                r_done(dve.tensor_tensor(wm[:, 0, :, :], ps, top.unsqueeze(2).to_broadcast([P, NT, EXPERTS]),
                                         ALU.subtract))
                r_wait()
                dve.nop().then_inc(logit_max, 1)
                dve.wait_ge(logit_exp, 1)
                step(dve.tensor_reduce(top, wm[:, 1, :, :], AX.X, ALU.add))
                step(dve.reciprocal(wm[:, 5, :, 1], top))
                step(dve.tensor_tensor(wm[:, 2, :, :], wm[:, 1, :, :],
                                       wm[:, 5, :, 1].unsqueeze(2).to_broadcast([P, NT, EXPERTS]), ALU.mult))
                step(dve.tensor_reduce(wm[:, 3, :, 0:4], wm[:, 2, :, :].rearrange("p t (g k) -> p t g k", g=4),
                                       AX.X, ALU.max))
                in_group = ranked(wm[:, 3, :, 0:4], 4, C_LOW4, 4)
                step(dve.tensor_tensor(wm[:, 1, :, :].rearrange("p t (g k) -> p t g k", g=4),
                                       wm[:, 2, :, :].rearrange("p t (g k) -> p t g k", g=4),
                                       in_group.unsqueeze(3).to_broadcast([P, NT, 4, 2]), ALU.mult))
                chosen = ranked(wm[:, 1, :, :], 8, C_LOW8, 4)
                step(dve.memset(wmx[:, :, EXPERTS:NEXP1], 1.0))
                step(dve.tensor_tensor(wmx[:, :, 0:EXPERTS], wm[:, 1, :, :], chosen, ALU.mult))
                tmp = rank[:, 0, 0:NT * NEXP1].rearrange("p (t e) -> p t e", t=NT)
                split(wmx[:, :, :], wp[:, :, 0, :], wp[:, :, 1, :], wp[:, :, 2, :], tmp).then_inc(wm_ready, 1)
                dve.wait_ge(wm_ready, 1)

            def copy_weights():
                ps = r_slot()
                r_done(dve.tensor_copy(wT[0:3 * NEXP1, :], ps[0:3 * NEXP1, :].bitcast(BF16)))

            def split_x(s, half):
                which = int(s > 1)
                dve.wait_ge(e_free, e_chunk(s, LEAD) - 1 if half else e_before(s) - ND)
                n = 2 * which + half
                f, fr = x_k[half]
                x = xT[:, :, half * HALF:(half + 1) * HALF]
                step(dve.tensor_scalar(f[:, 0].bitcast(I32), x.bitcast(I32), TOP, None, ALU.bitwise_and))
                dve.tensor_tensor(fr[:, 1], x, f[:, 0], ALU.subtract).then_inc(x_rest, 1)
                dve.wait_ge(x_rest, n + 1)
                dve.tensor_copy(fr[:, 0], f[:, 0]).then_inc(x_first, 1)
                dve.wait_ge(x_first, n + 1)

            def short_ffn(s, up_scale):
                which = int(s > 1)

                for half in range(2):
                    for fc in range(NF):
                        i = half * NF + fc
                        n = 2 * NF * which + i
                        ps = r_slot()
                        dve.wait_ge(e_free, e_chunk(s, i))
                        if i >= 2:
                            dve.wait_ge(h_last, n - 1)
                        r_done(dve.scalar_tensor_tensor(rest[:, i % 2, :], ps[:, :], up_scale(fc), sg[:, i % 4, :],
                                                        ALU.mult, ALU.mult))
                        r_wait()
                        if i >= 2:
                            dve.wait_ge(h_typed, n - 1)
                        dve.tensor_scalar(acc[:, i % 2, :].bitcast(I32), rest[:, i % 2, :].bitcast(I32),
                                          TOP, None, ALU.bitwise_and).then_inc(h_first, 1)
                        if i == 2:
                            split_x(s, 1)
                    post(s, half)

            def moe(s):
                nf = NF_MOE

                def rows(fc):
                    return P if fc < nf - 1 else F_MOE - P * (nf - 1)

                def gated(i):
                    n = rows(i % nf)
                    ps = r_slot()
                    dve.wait_ge(e_free, e_chunk(s, i))
                    r_done(dve.tensor_tensor(sgu[0:n, i % 3, :], ps[0:n, :], sg[0:n, i % 4, :], ALU.mult))

                def weighted(i):
                    n = rows(i % nf)
                    ps = r_slot()
                    r_done(dve.tensor_tensor(hid[i // nf][0:n, i % nf, :], ps[0:n, :], sgu[0:n, i % 3, :], ALU.mult))

                for half in range(2):
                    for i in range(half * nf, (half + 1) * nf):
                        gated(i)
                        if i == LEAD - 1:
                            route()
                        if i == LEAD:
                            copy_weights()
                            for k in range(LEAD):
                                weighted(k)
                        if i >= LEAD:
                            r_wait()
                            weighted(i)
                    post(s, half)

            step(dve.memset(pmx[:, :, :, :, :], LOWEST))
            for s in range(len(SUBLAYERS)):
                kind = SUBLAYERS[s]
                if kind == ATT:
                    attention(s)
                elif kind == WATT:
                    windowed(s)
                elif kind == GLU:
                    short_ffn(s, lambda fc: cst[:, C_SU + fc:C_SU + fc + 1])
                elif kind == MOE:
                    moe(s)
                elif kind == TERN:
                    short_ffn(s, lambda fc: tern[:, 13:14])
                else:
                    for half in range(2):
                        post(s, half)

        @block.tensor
        def _(pe):
            r_used = 0
            e_used = 0
            x_at = [0, 0]

            def r_slot():
                nonlocal r_used
                r_used += 1
                if r_used > 3:
                    pe.wait_ge(r_free, r_used - 3)
                return bank[(r_used - 1) % 3]

            def e_slot():
                nonlocal e_used
                e_used += 1
                if e_used > 2:
                    pe.wait_ge(e_free, e_used - 2)
                return pair[(e_used - 1) % 2]

            def x_ready(half):
                if x_at[half]:
                    pe.wait_ge(e_free, x_at[half])

            def over_width(ps, w, x):
                for c in range(ND):
                    last = pe.matmul(ps, w(c), x(c), start=(c == 0), stop=(c == ND - 1))
                return last

            def transpose_tiles(ps, src, half, c):
                for tt_ in range(TH):
                    last = pe.transpose(ps[:, tt_ * P:(tt_ + 1) * P], src[:, half * TH + tt_, c * P:(c + 1) * P], idf)
                return last

            def transpose_half(src, half):
                for c in range(ND):
                    transpose_tiles(e_slot()[:, 0, :], src, half, c).then_inc(e_full, 1)

            def new_x(s, half):
                pe.wait_ge(xn_ready, NT * s + TH * (half + 1))
                transpose_half(X, half)
                x_at[half] = e_used

            def project_tile(t, w):
                ps = r_slot()
                over_width(ps[:, 0:D], lambda c: xT[:, c, t * P:(t + 1) * P], lambda c: w[:, c, :]).then_inc(r_full, 1)

            def project_out(s, half, w):
                for t in range(half * TH, (half + 1) * TH):
                    project_tile(t, w)

            def last_half_out(s, w, new_first):
                pe.wait_ge(r_free, r_used)
                transpose_half(A, 1)
                if new_first:
                    new_x(s, 0)
                pe.wait_ge(e_free, e_used)
                project_out(s, 1, w)

            def attention(s):
                a = a_of(s)
                e_at = {}
                pe.wait_ge(*{0: (ld_x, 16 * 2), 4: (ld_att2, 16), 6: (ld_att3, 16)}[s])
                for i, (tile, half) in enumerate(TILE_HALVES):
                    if i == TH:
                        w = w_att(s, 2 * D, D)
                        for t in range(NT):
                            ps = r_slot()
                            over_width(ps[:, 0:D], lambda c: xT[:, c, t * P:(t + 1) * P], lambda c: w[:, c, :])\
                                .then_inc(r_full, 1)
                    side, hi = tile % 2, tile // 2
                    w = w_att(s, side * D + hi * P, P)
                    if i == LEAD:
                        if s:
                            new_x(s - 1, 1)
                        else:
                            pe.wait_ge(ld_x1, 16)
                    x_ready(half)
                    over_width(e_slot()[:, 0, :], lambda c: w[:, c, :],
                               lambda c: xT[:, c, half * HALF:(half + 1) * HALF]).then_inc(e_full, 1)
                v_at = r_used
                pe.wait_ge(cast_ready, 2)
                for item in PLAN:
                    if item == ("weights", 1) and s == 4:
                        pe.wait_ge(v_blank, 2)
                        pe.wait_ge(abs_ready, 1)
                        over_width(r_slot()[:, 0:D], lambda c: ones[:, :], lambda c: rest[:, c, 0:D]).then_inc(r_full, 1)
                    if item == ("weights", 5) and s == 4:
                        pe.wait_ge(abs_ready, 2)
                        pe.matmul(r_slot()[:, 0:3], ones[:, :], tern[:, 0:3], start=True, stop=True).then_inc(r_full, 1)
                    if item[0] == "suffix" and s == LAST_ATT:
                        t = item[1]
                        if t == NT - 1:
                            pe.wait_ge(r_free, v_at)
                            pe.wait_ge(v_blank, 2)
                        ps = r_slot()
                        v = v_all[:, t, :, 0:HD]
                        pe.matmul(ps[:, 0:D], cst[:, C_TRI:C_TRI + P], v, start=True, stop=True)
                        pe.matmul(ps[:, D:2 * D], ones[:, :], v, start=True, stop=True).then_inc(r_full, 1)
                    if item[0] == "max":
                        _, g, t, c, j = item
                        h = g * HG + j
                        if item == ("max", 0, 0, 0, 0):
                            pe.wait_ge(rep_a, 16 * REP[s][0])
                        if item == ("max", 2, 0, 0, 0):
                            pe.wait_ge(rep_b, 16 * REP[s][1])
                        n = min((t + 1) * P - c * HALF, HALF)
                        diag = (t + 1) * P - c * HALF <= HALF
                        ps = r_slot()
                        last = pe.matmul(ps[:, 0:n], q_op[0:KROWS, h, t * P:(t + 1) * P],
                                         k_op[0:KROWS, h, c * HALF:c * HALF + n], start=True, stop=not diag)
                        if diag:
                            last = pe.matmul(ps[:, n - P:n], idb[:, :], maskb[:, 0, :], start=False, stop=True)
                        last.then_inc(r_full, 1)
                    if item[0] == "mT":
                        _, g, qh = item
                        pe.wait_ge(mp_ready, 2 * (NG * a + g) + qh + 1)
                        ps = r_slot()[0:3 * HG, :].bitcast(BF16)
                        for t in range(qh * TH, (qh + 1) * TH):
                            last = pe.transpose(ps[:, t % TH * P:(t % TH + 1) * P],
                                                mp[:, g % 2, t, :, :].rearrange("p k j -> p (k j)"), idb[:, :])
                        last.then_inc(r_full, 1)
                    if item[0] == "exp":
                        _, g, qh, kb, i = item
                        if (g, qh, kb, i) == (0, 0, 0, 0):
                            pe.wait_ge(k_ones, 1 if s == 0 else 3)
                        if kb == i == 0:
                            n = 2 * (NG * a + g) + qh
                            pe.wait_ge(m_in[n % 2], 16 * (n // 2 + 1))
                        q0, n = span(qh, kb)
                        diag = kb * P >= qh * HALF
                        ps = e_slot()
                        for j in range(2):
                            h = g * HG + 2 * i + j
                            last = pe.matmul(ps[:, j, 0:n], k_op[0:KROWS + 3, h, kb * P:(kb + 1) * P],
                                             q_op[0:KROWS + 3, h, q0:q0 + n], start=True, stop=not diag)
                            if diag:
                                last = pe.matmul(ps[:, j, 0:P], idb[:, :], maskb[:, 1, :], start=False, stop=True)
                        last.then_inc(e_full, 1)
                        e_at[g, qh, kb] = e_used
                    if item[0] == "pv":
                        _, g, qh, kb = item
                        st = STEP[g, qh, kb]
                        q0, n = span(qh, kb)
                        if st == 0:
                            pe.wait_ge(r_free, v_at)
                        if kb == 0 and ACC0[s] + 2 * g + qh:
                            pe.wait_ge(acc_ready, ACC0[s] + 2 * g + qh)
                        pe.wait_ge(e_free, e_at[g, qh, kb])
                        for j in range(HG):
                            last = pe.matmul(pvb[j * STRIP:(j + 1) * STRIP, q0 - qh * HALF:HALF],
                                             v_all[:, kb, g * HG + j, :], pb[:, st % 2, j, 0:n],
                                             start=(kb == 0), stop=(kb == TH * (qh + 1) - 1))
                        last.then_inc(pv_done, 1)
                    if item[0] == "accT":
                        _, g, qh = item
                        n = ACC0[s] + 2 * g + qh
                        pe.wait_ge(acc_ready, n + 1)
                        ps = r_slot()
                        for tt_ in range(TH):
                            last = pe.transpose(ps[:, tt_ * P:(tt_ + 1) * P], acc[:, n % 2, tt_ * P:(tt_ + 1) * P], idf)
                        last.then_inc(r_full, 1)
                    if item[0] == "outT":
                        pe.wait_ge(r_free, r_used)
                        transpose_half(A, 0)
                    if item[0] == "proj":
                        pe.wait_ge(e_free, e_used)
                        project_tile(item[1], w_att(s, 3 * D, D))
                    if item[0] == "new":
                        new_x(s, 0)
                last_half_out(s, w_att(s, 3 * D, D), False)

            def windowed(s):
                assert e_used == e_before(s)
                pe.wait_ge(ld_watt, 16)
                for i, (tile, half) in enumerate(W_HALVES):
                    rows, at = ((P, (tile * P, D + tile * P)) if tile < 2 else (KV * HD, (2 * D, 2 * D + KV * HD)))
                    if i == 1:
                        new_x(s - 1, 1)
                    x_ready(half)
                    for k in range(2):
                        w = w_att(s, at[k], rows)
                        ps = r_slot()
                        over_width(ps[0:rows, :], lambda c: w[:, c, :],
                                   lambda c: xT[:, c, half * HALF:(half + 1) * HALF]).then_inc(r_full, 1)
                w = w_att(s, 2 * D + 2 * KV * HD, KV * HD)
                ps = r_slot()
                for t in range(NT):
                    last = over_width(ps[:, t * KV * HD:(t + 1) * KV * HD], lambda c: xT[:, c, t * P:(t + 1) * P],
                                      lambda c: w[:, c, :])
                last.then_inc(r_full, 1)
                ps = r_slot()
                for t in range(1, NT):
                    last = over_width(ps[0:WIN, t * KV * HD:(t + 1) * KV * HD],
                                      lambda c: xT[:, c, t * P - WIN:t * P], lambda c: w[:, c, :])
                last.then_inc(r_full, 1)
                v_at = r_used
                uT_at = {}
                pe.wait_ge(cast_ready, 3)
                pe.wait_ge(e_free, e_used)
                pe.wait_ge(rep_a, 16 * REP[s][0])
                for item in W_PLAN:
                    if item[0] == "S":
                        u = item[1]
                        t, p = divmod(u, NH // 2)
                        for i in range(2):
                            h = 2 * u + i
                            if h == NH // 2:
                                pe.wait_ge(rep_b, 16 * REP[s][1])
                            if h >= 4:
                                pe.wait_ge(w_free, h - 3)
                            for z in range(2):
                                o = pair[u % 2][:, i, z * WK:(z + 1) * WK]
                                pe.matmul(o, q_op[0:KROWS, 2 * p + i, t * P:(t + 1) * P],
                                          kw_op[0:KROWS, p // 2, z, t * P:t * P + WK], start=True, stop=False)
                                last = pe.matmul(o, idb[:, :], wmaskb[:, int(t == 0), 0:WK], start=False, stop=True)
                            last.then_inc(w_full, 1)
                    if item[0] == "uT":
                        gi = item[1]
                        pe.wait_ge(u_ready, gi + 1)
                        pe.wait_ge(u0_ready, gi + 1)
                        ps = r_slot()
                        for hh in range(HG):
                            last = pe.transpose(ps[:, hh * P:(hh + 1) * P], u_own[:, gi % 2, hh * P:(hh + 1) * P], idf)
                        last.then_inc(r_full, 1)
                        if gi >= NG:
                            ps = r_slot()
                            for k in range(2):
                                last = pe.transpose(ps[:, k * P:(k + 1) * P], u_prev[:, gi % 2, k * P:(k + 1) * P], idf)
                            last.then_inc(r_full, 1)
                        assert r_used == uses_of_r(gi)
                        uT_at[gi] = r_used
                    if item[0] == "pv":
                        t = item[1]
                        if t == 0:
                            pe.wait_ge(r_free, v_at)
                        pe.wait_ge(acc_ready, ACC0[s] + t)
                        pe.wait_ge(r_free, uT_at[NG * t + NG - 1])
                        for g in range(NG):
                            last = pe.matmul(pvb[g * STRIP:(g + 1) * STRIP, :], v_own[:, t, g, :], uT[:, g, 0, :],
                                             start=True, stop=(t == 0))
                        for k in range(2 if t else 0):
                            for g in range(NG):
                                o = pvb[g * STRIP:(g + 1) * STRIP, :].rearrange("p (j k q) -> p k j q", j=2, k=2)
                                last = pe.matmul(o[:, k], v_prev[k][:, t, g, :], uT[:, g, 1, 0:HALF // 2],
                                                 start=False, stop=(k == 1))
                        last.then_inc(pv_done, 1)
                    if item[0] == "accT":
                        t = item[1]
                        n = ACC0[s] + t
                        pe.wait_ge(acc_ready, n + 1)
                        ps = r_slot()
                        for hh in range(HG):
                            last = pe.transpose(ps[:, hh * P:(hh + 1) * P], acc[:, n % 2, hh * P:(hh + 1) * P], idf)
                        last.then_inc(r_full, 1)
                    if item[0] == "outT":
                        pe.wait_ge(r_free, r_used)
                        for c in range(ND):
                            transpose_tiles(r_slot(), A, 0, c).then_inc(r_full, 1)
                        outT_at = r_used
                    if item[0] == "proj":
                        pe.wait_ge(r_free, outT_at)
                        project_tile(item[1], w_att(s, 704, D))
                pe.wait_ge(w_free, NT * NH)
                last_half_out(s, w_att(s, 704, D), True)

            def short_ffn(s):
                which = int(s > 1)
                assert e_used == e_before(s)
                pe.wait_ge(*((glu_ready, 2) if s == 1 else (tern_ready, 1)))

                def gate_up(half):
                    pe.wait_ge(x_rest, 2 * which + half + 1)
                    pe.wait_ge(x_first, 2 * which + half + 1)
                    for fc in range(NF):
                        if (half, fc) == (0, LEAD):
                            new_x(s - 1, 1)
                        for side in range(2):
                            ps = e_slot()[:, 0, :] if side == 0 else r_slot()[:, :]
                            for c in range(ND):
                                for k in range(2):
                                    last = pe.matmul(ps, gu_r[:, c, side, fc * P:(fc + 1) * P], x_k[half][1][:, k, c, :],
                                                     start=(c + k == 0), stop=(c + k == 2))
                            last.then_inc((e_full, r_full)[side], 1)

                def down(half):
                    n = NF * (2 * which + half + 1)
                    pe.wait_ge(h_last, n)
                    pe.wait_ge(h_typed, n)
                    for t in range(half * TH, (half + 1) * TH):
                        ps = r_slot()
                        at = (t - half * TH) * P
                        for fc in range(NF):
                            for k in range(2):
                                last = pe.matmul(ps[:, 0:D], hid_k[half][:, k, fc, at:at + P], wd_r[:, fc, :],
                                                 start=(fc + k == 0), stop=(fc + k == NF))
                        last.then_inc(r_full, 1)

                gate_up(0)
                down(0)
                gate_up(1)
                if s < len(SUBLAYERS) - 1:
                    new_x(s, 0)
                down(1)

            def moe(s):
                assert e_used == e_before(s)
                nf = NF_MOE
                pe.wait_ge(ld_moe, 16)

                def rows(fc):
                    return P if fc < nf - 1 else F_MOE - P * (nf - 1)

                def project(ps, side, i):
                    half, fc = divmod(i, nf)
                    n = rows(fc)
                    return over_width(ps[0:n, :], lambda c: gu_moe[:, c, side, fc * P:fc * P + n],
                                      lambda c: xT[:, c, half * HALF:(half + 1) * HALF])

                def gate(i):
                    project(e_slot()[:, 0, :], 0, i).then_inc(e_full, 1)

                def up(i):
                    project(r_slot(), 1, i).then_inc(r_full, 1)

                def weights(i):
                    half, fc = divmod(i, nf)
                    n = rows(fc)
                    pe.matmul(r_slot()[0:n, :], selb[:, fc * P:fc * P + n],
                              wT[0:3 * NEXP1, half * HALF:(half + 1) * HALF], start=True, stop=True).then_inc(r_full, 1)

                def down(half):
                    pe.wait_ge(r_free, r_used)
                    for t in range(half * TH, (half + 1) * TH):
                        ps = r_slot()
                        at = (t - half * TH) * P
                        for fc in range(nf):
                            n = rows(fc)
                            last = pe.matmul(ps[:, 0:D], hid[half][0:n, fc, at:at + P], wd_moe[0:n, fc, :],
                                             start=(fc == 0), stop=(fc == nf - 1))
                        last.then_inc(r_full, 1)

                x_ready(0)
                for i in range(LEAD):
                    gate(i)
                    up(i)
                new_x(s - 1, 1)
                ps = r_slot()
                for t in range(NT):
                    x_ready(t // TH)
                    last = over_width(ps[:, t * EXPERTS:(t + 1) * EXPERTS], lambda c: xT[:, c, t * P:(t + 1) * P],
                                      lambda c: cst[:, C_GW + c * EXPERTS:C_GW + (c + 1) * EXPERTS])
                last.then_inc(r_full, 1)
                gate(LEAD)
                up(LEAD)
                gate(LEAD + 1)
                pe.wait_ge(wm_ready, 1)
                ps = r_slot()[0:3 * NEXP1, :].bitcast(BF16)
                for t in range(NT):
                    last = pe.transpose(ps[:, t * P:(t + 1) * P], wp[:, t, :, :].rearrange("p k e -> p (k e)"), idb[:, :])
                last.then_inc(r_full, 1)
                pe.wait_ge(r_free, r_used)
                pe.wait_ge(cast_ready, 4)
                for i in range(LEAD + 1):
                    weights(i)
                for half in range(2):
                    x_ready(half)
                    for i in range(max(half * nf, LEAD + 1), (half + 1) * nf):
                        if i > LEAD + 1:
                            gate(i)
                        up(i)
                        weights(i)
                    if half:
                        new_x(s, 0)
                    else:
                        pe.wait_ge(ld_moed, 16)
                    down(half)

            for s in range(len(SUBLAYERS)):
                kind = SUBLAYERS[s]
                if kind == ATT:
                    attention(s)
                elif kind == WATT:
                    windowed(s)
                elif kind == GLU:
                    short_ffn(s)
                elif kind == MOE:
                    moe(s)
                elif kind == TERN:
                    short_ffn(s)
                else:
                    pe.wait_ge(bin_ready, 1)
                    x_ready(0)
                    project_out(s, 0, WB)
                    new_x(s - 1, 1)
                    x_ready(1)
                    project_out(s, 1, WB)
                    new_x(s, 0)


def arrange(i):
    g = {k: np.asarray(v) for k, v in i.items()}

    def chunks(a):
        return np.ascontiguousarray(a.reshape(-1, P, a.shape[1]).transpose(1, 0, 2))

    x = g["L0_attn_x"].reshape(S, D)
    swap = (np.arange(HD) + HD // 2) % HD
    wq, wk = g["L1_attn_Wq"], g["L1_attn_Wk"]
    wqs = wq.reshape(D, NH, HD)[:, :, swap].reshape(D, NH * HD)
    wks = wk.reshape(D, KV, HD)[:, :, swap].reshape(D, KV * HD)
    cst = constants()
    cst[:, C_LAM:C_LAM + NH] = g["L1_attn_lam"][None, :]
    cst[:, C_SG:C_SG + NF] = g["L0_ffn_s_gate"].reshape(NF, P).T
    cst[:, C_SU:C_SU + NF] = g["L0_ffn_s_up"].reshape(NF, P).T
    cst[:, C_GW:C_GW + ND * EXPERTS] = chunks(g["L1_ffn_gate_weight"].T).reshape(P, -1)
    gate = np.concatenate([g["L1_ffn_gate_w"].reshape(-1, D), g["L1_ffn_sh_gate_w"]], 0).T
    up = np.concatenate([g["L1_ffn_up_w"].reshape(-1, D), g["L1_ffn_sh_up_w"]], 0).T
    down = np.concatenate([g["L1_ffn_down_w"].transpose(0, 2, 1).reshape(-1, D), g["L1_ffn_sh_down_w"].T,
                           np.zeros((NF_MOE * P - F_MOE, D), np.float32)], 0)
    flat = lambda a: np.ascontiguousarray(a).reshape(P, -1)
    return {
        "x": chunks(x),
        "xT": chunks(x.T),
        "cst": cst,
        "sel": expert_selector(),
        "rope": rope_tables(),
        "w_att0": flat(chunks(np.concatenate([g["L0_attn_w_project"].T, g["L0_attn_w_out"].T], 1))),
        "w_watt": flat(chunks(np.concatenate([wq, wqs, wk, wks, g["L1_attn_Wv"], g["L1_attn_Wo"]], 1))),
        "w_att2": flat(chunks(np.concatenate([g["L2_attn_w_qkv"], g["L2_attn_w_out"]], 1))),
        "w_att3": flat(chunks(np.concatenate([g[f"L3_attn_{k}"] for k in ("Wq", "Wk", "Wv", "Wo")], 1))),
        "glu_gu": flat(chunks(np.concatenate([g["L0_ffn_w_gate"], g["L0_ffn_w_up"]], 1))).view(np.int32),
        "glu_d": flat(chunks(g["L0_ffn_w_down"])).view(np.int32),
        "glu_sd": np.ascontiguousarray(g["L0_ffn_s_down"]),
        "moe_gu": flat(chunks(np.concatenate([gate, up], 1))),
        "moe_d": chunks(down),
        "bin_w": chunks(g["L2_ffn_weight"].T),
        "bin_b": np.ascontiguousarray(g["L2_ffn_bias"]),
        "tern_w": np.concatenate([flat(chunks(np.concatenate([g["L3_ffn_W_up"].T, g["L3_ffn_W_gate"].T], 1))),
                                  flat(chunks(g["L3_ffn_W_down"].T))], 1),
    }


def kernel(**inputs):
    import concourse.bacc as bacc
    from concourse.bass_utils import run_bass_kernel_spmd

    nc = bacc.Bacc("TRN2", target_bir_lowering=False, num_devices=1)
    arrays = arrange(inputs)
    t_in = {k: nc.dram_tensor("in_" + k, a.shape, mybir.dt.from_np(a.dtype), kind="ExternalInput").ap()
            for k, a in arrays.items()}
    out = nc.dram_tensor("out", (1, S, D), F32, kind="ExternalOutput").ap()
    build(nc, t_in, out)
    return run_bass_kernel_spmd(nc, [{"in_" + k: a for k, a in arrays.items()}], core_ids=[0]).results[0]["out"]
```
